# Optimizing a Trainium2 kernel written in Bass

```python
import numpy as np
import jax
import jax.numpy as jnp

def _softmax(x, axis=-1):
    return jax.nn.softmax(x, axis=axis)

def _gelu(x):
    return jax.nn.gelu(x, approximate=True)

def _silu(x):
    return jax.nn.silu(x)

def _sigmoid(x):
    return jax.nn.sigmoid(x)

def _layernorm(x, axis=-1, eps=1e-05):
    m = jnp.mean(x, axis=axis, keepdims=True)
    v = jnp.var(x, axis=axis, keepdims=True)
    return (x - m) / jnp.sqrt(v + eps)

def _scatter_add(tgt, idx, src, axis=0):
    return tgt.at[idx].add(src)

def _segment_sum(src, seg, n):
    return jax.ops.segment_sum(src, seg, n)
kernel_name = 'mk_lm_tower_d2_tok_ids1024_r4_20b601'

def setup_inputs(seed: int=0):
    np.random.seed(seed)
    _w = jnp.asarray

    def _rec_inputs():
        import jax
        import jax.numpy as jnp
        _rk = jax.random.key(seed)
        x = jax.random.randint(jax.random.fold_in(_rk, 1), (16, 128), 0, 49991, jnp.int32)
        return x
    x = _rec_inputs()

    def _L0_tok_setup():
        import jax, jax.numpy as jnp
        import numpy as np
        HIDDEN = 256
        CUTOFFS = [5000, 20000, 50000]
        PROJECT_FACTOR = 4
        NUM_TAILS = len(CUTOFFS) - 1
        CUTOFF_ENDS = [0] + CUTOFFS
        BATCH, SEQ = (8, 256)

        def _glorot(key, shape):
            fan_in, fan_out = shape
            limit = np.sqrt(6.0 / (fan_in + fan_out)).astype(np.float32)
            return jax.random.uniform(key, shape, jnp.float32, -limit, limit)
        key = jax.random.key(seed)
        ks = jax.random.split(key, 7)
        return {'x': jax.random.randint(ks[0], (BATCH, SEQ), 0, CUTOFFS[-1], dtype=jnp.int64.dtype if jax.config.jax_enable_x64 else jnp.int32), 'head_weight_proj': _glorot(ks[1], (HIDDEN, HIDDEN)), 'head_weight': _glorot(ks[2], (HIDDEN, CUTOFFS[0] + NUM_TAILS)), 'tail_weight_proj_0': _glorot(ks[3], (HIDDEN, HIDDEN // PROJECT_FACTOR)), 'tail_weight_0': _glorot(ks[4], (HIDDEN // PROJECT_FACTOR, CUTOFFS[1] - CUTOFFS[0])), 'tail_weight_proj_1': _glorot(ks[5], (HIDDEN, HIDDEN // PROJECT_FACTOR ** 2)), 'tail_weight_1': _glorot(ks[6], (HIDDEN // PROJECT_FACTOR ** 2, CUTOFFS[2] - CUTOFFS[1]))}
    _L0_tok_all = _L0_tok_setup()
    _L0_tok_in = {k: v for k, v in _L0_tok_all.items() if k in ('head_weight_proj', 'head_weight', 'tail_weight_proj_0', 'tail_weight_0', 'tail_weight_proj_1', 'tail_weight_1')}
    del _L0_tok_all

    def _L0_attn_setup():
        import jax, jax.numpy as jnp
        import numpy as np
        D_MODEL = 256
        D_STATE = 16
        D_CONV = 4
        EXPAND = 2
        D_INNER = EXPAND * D_MODEL
        DT_RANK = -(-D_INNER // 16)
        B_SZ, SEQ = (2, 512)
        EPS = 1e-05
        key = jax.random.key(seed)
        ks = jax.random.split(key, 10)
        s = 0.02
        x = jax.random.normal(ks[0], (B_SZ, SEQ, D_MODEL), jnp.float32)
        ln_gamma = jnp.ones((D_MODEL,), jnp.float32)
        ln_beta = jnp.zeros((D_MODEL,), jnp.float32)
        W_in = jax.random.normal(ks[1], (2 * D_INNER, D_MODEL), jnp.float32) * s
        conv_w = jax.random.normal(ks[2], (D_INNER, 1, D_CONV), jnp.float32) * 0.2
        conv_b = jax.random.normal(ks[3], (D_INNER,), jnp.float32) * s
        W_xproj = jax.random.normal(ks[4], (DT_RANK + 2 * D_STATE, D_INNER), jnp.float32) * s
        W_dt = jax.random.uniform(ks[5], (D_INNER, DT_RANK), jnp.float32, -DT_RANK ** (-0.5), DT_RANK ** (-0.5))
        b_dt = jax.random.normal(ks[6], (D_INNER,), jnp.float32) * s
        A_log = jnp.tile(jnp.log(jnp.arange(1, D_STATE + 1, dtype=jnp.float32)), (D_INNER, 1))
        D_param = jnp.ones((D_INNER,), jnp.float32)
        W_out = jax.random.normal(ks[7], (D_MODEL, D_INNER), jnp.float32) * s
        return dict(x=x, ln_gamma=ln_gamma, ln_beta=ln_beta, W_in=W_in, conv_w=conv_w, conv_b=conv_b, W_xproj=W_xproj, W_dt=W_dt, b_dt=b_dt, A_log=A_log, D_param=D_param, W_out=W_out)
    _L0_attn_all = _L0_attn_setup()
    _L0_attn_in = {k: v for k, v in _L0_attn_all.items() if k in ('ln_gamma', 'ln_beta', 'W_in', 'conv_w', 'conv_b', 'W_xproj', 'W_dt', 'b_dt', 'A_log', 'D_param', 'W_out')}
    del _L0_attn_all

    def _L0_ffn_setup():
        import jax, jax.numpy as jnp
        import numpy as np
        E = 8
        K = 2
        LN_EPS = 1e-05

        def _expert_ffn(x, w1, b1, gate, w2, b2):
            h = jax.nn.gelu((x @ w1 + b1) * gate, approximate=False)
            return h @ w2 + b2
        key = jax.random.key(seed)
        B, S, D, F = (4, 512, 256, 1024)
        F2 = F // 2
        ks = jax.random.split(key, 8)
        s = 0.02
        return {'hidden_states': jax.random.normal(ks[0], (B, S, D), jnp.float32), 'router_w': jax.random.normal(ks[1], (D, E), jnp.float32) * s, 'router_b': jnp.zeros((E,), jnp.float32), 'w1': jax.random.normal(ks[2], (E, D, F), jnp.float32) * s, 'b1': jnp.zeros((E, F), jnp.float32), 'gate': jnp.ones((E, F), jnp.float32), 'w2': jax.random.normal(ks[3], (E, F, D), jnp.float32) * s, 'b2': jnp.zeros((E, D), jnp.float32), 'sw1': jax.random.normal(ks[4], (D, F2), jnp.float32) * s, 'sb1': jnp.zeros((F2,), jnp.float32), 'sgate': jnp.ones((F2,), jnp.float32), 'sw2': jax.random.normal(ks[5], (F2, D), jnp.float32) * s, 'sb2': jnp.zeros((D,), jnp.float32), 'shared_weight': jnp.float32(0.5), 'ln_g': jnp.ones((D,), jnp.float32), 'ln_b': jnp.zeros((D,), jnp.float32)}
    _L0_ffn_all = _L0_ffn_setup()
    _L0_ffn_in = {k: v for k, v in _L0_ffn_all.items() if k in ('router_w', 'router_b', 'w1', 'b1', 'gate', 'w2', 'b2', 'sw1', 'sb1', 'sgate', 'sw2', 'sb2', 'shared_weight', 'ln_g', 'ln_b')}
    del _L0_ffn_all

    def _L1_attn_setup():
        import jax, jax.numpy as jnp
        import numpy as np
        B, S, E = (4, 512, 256)
        H, KVH = (16, 4)
        D = E // H
        QL, KVL = (64, 32)
        ROPE_BASE = 10000.0

        def _rope(x):
            d = x.shape[-1]
            inv_freq = 1.0 / ROPE_BASE ** (jnp.arange(0, d, 2, dtype=jnp.float32) / d)
            t = jnp.arange(x.shape[1], dtype=jnp.float32)
            freqs = jnp.outer(t, inv_freq)
            cos = jnp.cos(freqs)[None, :, None, :].astype(x.dtype)
            sin = jnp.sin(freqs)[None, :, None, :].astype(x.dtype)
            x1, x2 = (x[..., ::2], x[..., 1::2])
            r1 = x1 * cos - x2 * sin
            r2 = x1 * sin + x2 * cos
            return jnp.stack([r1, r2], axis=-1).reshape(x.shape)
        key = jax.random.key(seed)
        ks = jax.random.split(key, 7)
        s = 0.02
        return {'x': jax.random.normal(ks[0], (B, S, E), dtype=jnp.float32), 'Wqa': jax.random.normal(ks[1], (E, QL), dtype=jnp.float32) * s, 'Wqb': jax.random.normal(ks[2], (QL, E), dtype=jnp.float32) * s, 'Wkva': jax.random.normal(ks[3], (E, KVL), dtype=jnp.float32) * s, 'Wkvb': jax.random.normal(ks[4], (KVL, KVH * D * 2), dtype=jnp.float32) * s, 'Wout': jax.random.normal(ks[5], (E, E), dtype=jnp.float32) * s, 'bout': jax.random.normal(ks[6], (E,), dtype=jnp.float32) * s}
    _L1_attn_all = _L1_attn_setup()
    _L1_attn_in = {k: v for k, v in _L1_attn_all.items() if k in ('Wqa', 'Wqb', 'Wkva', 'Wkvb', 'Wout', 'bout')}
    del _L1_attn_all

    def _L1_ffn_setup():
        import jax, jax.numpy as jnp
        import numpy as np
        D_MODEL = 256
        MLP_DIM = 1024
        N_EXPERTS = 8
        B, T = (4, 256)
        key = jax.random.key(seed)
        ks = jax.random.split(key, 7)
        scale_in = (1.0 / D_MODEL) ** 0.5
        scale_out = (1.0 / MLP_DIM) ** 0.5
        bound_g = (1.0 / D_MODEL) ** 0.5
        w_gate = jax.random.uniform(ks[0], (D_MODEL, N_EXPERTS), minval=-bound_g, maxval=bound_g, dtype=jnp.float32)
        b_gate = jax.random.uniform(ks[1], (N_EXPERTS,), minval=-bound_g, maxval=bound_g, dtype=jnp.float32)
        W1 = jax.random.uniform(ks[2], (N_EXPERTS, D_MODEL, MLP_DIM), minval=-scale_in, maxval=scale_in, dtype=jnp.float32)
        b1 = jnp.zeros((N_EXPERTS, MLP_DIM), dtype=jnp.float32)
        W2 = jax.random.uniform(ks[3], (N_EXPERTS, MLP_DIM, D_MODEL), minval=-scale_out, maxval=scale_out, dtype=jnp.float32)
        b2 = jnp.zeros((N_EXPERTS, D_MODEL), dtype=jnp.float32)
        x = jax.random.normal(ks[4], (B, T, D_MODEL), dtype=jnp.float32)
        return {'x': x, 'w_gate': w_gate, 'b_gate': b_gate, 'W1': W1, 'b1': b1, 'W2': W2, 'b2': b2}
    _L1_ffn_all = _L1_ffn_setup()
    _L1_ffn_in = {k: v for k, v in _L1_ffn_all.items() if k in ('w_gate', 'b_gate', 'W1', 'b1', 'W2', 'b2')}
    del _L1_ffn_all
    return {'x': x, 'L0_tok_head_weight_proj': _L0_tok_in['head_weight_proj'], 'L0_tok_head_weight': _L0_tok_in['head_weight'], 'L0_tok_tail_weight_proj_0': _L0_tok_in['tail_weight_proj_0'], 'L0_tok_tail_weight_0': _L0_tok_in['tail_weight_0'], 'L0_tok_tail_weight_proj_1': _L0_tok_in['tail_weight_proj_1'], 'L0_tok_tail_weight_1': _L0_tok_in['tail_weight_1'], 'L0_attn_ln_gamma': _L0_attn_in['ln_gamma'], 'L0_attn_ln_beta': _L0_attn_in['ln_beta'], 'L0_attn_W_in': _L0_attn_in['W_in'], 'L0_attn_conv_w': _L0_attn_in['conv_w'], 'L0_attn_conv_b': _L0_attn_in['conv_b'], 'L0_attn_W_xproj': _L0_attn_in['W_xproj'], 'L0_attn_W_dt': _L0_attn_in['W_dt'], 'L0_attn_b_dt': _L0_attn_in['b_dt'], 'L0_attn_A_log': _L0_attn_in['A_log'], 'L0_attn_D_param': _L0_attn_in['D_param'], 'L0_attn_W_out': _L0_attn_in['W_out'], 'L0_ffn_router_w': _L0_ffn_in['router_w'], 'L0_ffn_router_b': _L0_ffn_in['router_b'], 'L0_ffn_w1': _L0_ffn_in['w1'], 'L0_ffn_b1': _L0_ffn_in['b1'], 'L0_ffn_gate': _L0_ffn_in['gate'], 'L0_ffn_w2': _L0_ffn_in['w2'], 'L0_ffn_b2': _L0_ffn_in['b2'], 'L0_ffn_sw1': _L0_ffn_in['sw1'], 'L0_ffn_sb1': _L0_ffn_in['sb1'], 'L0_ffn_sgate': _L0_ffn_in['sgate'], 'L0_ffn_sw2': _L0_ffn_in['sw2'], 'L0_ffn_sb2': _L0_ffn_in['sb2'], 'L0_ffn_shared_weight': _L0_ffn_in['shared_weight'], 'L0_ffn_ln_g': _L0_ffn_in['ln_g'], 'L0_ffn_ln_b': _L0_ffn_in['ln_b'], 'L1_attn_Wqa': _L1_attn_in['Wqa'], 'L1_attn_Wqb': _L1_attn_in['Wqb'], 'L1_attn_Wkva': _L1_attn_in['Wkva'], 'L1_attn_Wkvb': _L1_attn_in['Wkvb'], 'L1_attn_Wout': _L1_attn_in['Wout'], 'L1_attn_bout': _L1_attn_in['bout'], 'L1_ffn_w_gate': _L1_ffn_in['w_gate'], 'L1_ffn_b_gate': _L1_ffn_in['b_gate'], 'L1_ffn_W1': _L1_ffn_in['W1'], 'L1_ffn_b1': _L1_ffn_in['b1'], 'L1_ffn_W2': _L1_ffn_in['W2'], 'L1_ffn_b2': _L1_ffn_in['b2']}

def reference(x, L0_tok_head_weight_proj, L0_tok_head_weight, L0_tok_tail_weight_proj_0, L0_tok_tail_weight_0, L0_tok_tail_weight_proj_1, L0_tok_tail_weight_1, L0_attn_ln_gamma, L0_attn_ln_beta, L0_attn_W_in, L0_attn_conv_w, L0_attn_conv_b, L0_attn_W_xproj, L0_attn_W_dt, L0_attn_b_dt, L0_attn_A_log, L0_attn_D_param, L0_attn_W_out, L0_ffn_router_w, L0_ffn_router_b, L0_ffn_w1, L0_ffn_b1, L0_ffn_gate, L0_ffn_w2, L0_ffn_b2, L0_ffn_sw1, L0_ffn_sb1, L0_ffn_sgate, L0_ffn_sw2, L0_ffn_sb2, L0_ffn_shared_weight, L0_ffn_ln_g, L0_ffn_ln_b, L1_attn_Wqa, L1_attn_Wqb, L1_attn_Wkva, L1_attn_Wkvb, L1_attn_Wout, L1_attn_bout, L1_ffn_w_gate, L1_ffn_b_gate, L1_ffn_W1, L1_ffn_b1, L1_ffn_W2, L1_ffn_b2):
    import jax
    import jax.numpy as jnp

    def _L0_tok_ref(x, head_weight_proj, head_weight, tail_weight_proj_0, tail_weight_0, tail_weight_proj_1, tail_weight_1):
        import jax, jax.numpy as jnp
        import numpy as np
        HIDDEN = 256
        CUTOFFS = [5000, 20000, 50000]
        PROJECT_FACTOR = 4
        NUM_TAILS = len(CUTOFFS) - 1
        CUTOFF_ENDS = [0] + CUTOFFS
        BATCH, SEQ = (8, 256)

        def _glorot(key, shape):
            fan_in, fan_out = shape
            limit = np.sqrt(6.0 / (fan_in + fan_out)).astype(np.float32)
            return jax.random.uniform(key, shape, jnp.float32, -limit, limit)
        tables = [head_weight.T[:CUTOFFS[0]], tail_weight_0.T, tail_weight_1.T]
        projs = [head_weight_proj.T, tail_weight_proj_0.T, tail_weight_proj_1.T]
        y = jnp.zeros(x.shape + (HIDDEN,), dtype=jnp.float32)
        for i in range(len(CUTOFF_ENDS) - 1):
            l_idx, r_idx = (CUTOFF_ENDS[i], CUTOFF_ENDS[i + 1])
            mask = (x >= l_idx) & (x < r_idx)
            idx = jnp.where(mask, x - l_idx, 0)
            emb = tables[i][idx]
            proj = jnp.einsum('bsd,dh->bsh', emb, projs[i])
            y = y + jnp.where(mask[..., None], proj, 0.0)
        emb_scale = jnp.asarray(HIDDEN ** 0.5, y.dtype)
        return y * emb_scale

    def _L0_attn_ref(x, ln_gamma, ln_beta, W_in, conv_w, conv_b, W_xproj, W_dt, b_dt, A_log, D_param, W_out):
        import jax, jax.numpy as jnp
        import numpy as np
        D_MODEL = 256
        D_STATE = 16
        D_CONV = 4
        EXPAND = 2
        D_INNER = EXPAND * D_MODEL
        DT_RANK = -(-D_INNER // 16)
        B_SZ, SEQ = (2, 512)
        EPS = 1e-05
        resid = x
        mu = jnp.mean(x, -1, keepdims=True)
        var = jnp.mean((x - mu) ** 2, -1, keepdims=True)
        xn = (x - mu) / jnp.sqrt(var + EPS) * ln_gamma + ln_beta
        xz = xn @ W_in.T
        xs, z = jnp.split(xz, 2, axis=-1)
        xc = jnp.swapaxes(xs, 1, 2)
        xc = jax.lax.conv_general_dilated(xc, conv_w, window_strides=(1,), padding=[(D_CONV - 1, 0)], feature_group_count=D_INNER, dimension_numbers=('NCH', 'OIH', 'NCH')) + conv_b[None, :, None]
        u = jax.nn.silu(jnp.swapaxes(xc, 1, 2))
        proj = u @ W_xproj.T
        dt_low, Bc, Cc = jnp.split(proj, [DT_RANK, DT_RANK + D_STATE], axis=-1)
        delta = jax.nn.softplus(dt_low @ W_dt.T + b_dt)
        A = -jnp.exp(A_log)

        def step(h, inp):
            dt, bt, ct, ut = inp
            dA = jnp.exp(dt[..., None] * A)
            h = dA * h + (dt * ut)[..., None] * bt[:, None, :]
            y = jnp.einsum('bdn,bn->bd', h, ct)
            return (h, y)
        h0 = jnp.zeros((x.shape[0], D_INNER, D_STATE), u.dtype)
        seq = (jnp.moveaxis(delta, 1, 0), jnp.moveaxis(Bc, 1, 0), jnp.moveaxis(Cc, 1, 0), jnp.moveaxis(u, 1, 0))
        _, ys = jax.lax.scan(step, h0, seq)
        y = jnp.moveaxis(ys, 0, 1) + u * D_param
        y = y * jax.nn.silu(z)
        return resid + y @ W_out.T

    def _L0_ffn_ref(hidden_states, router_w, router_b, w1, b1, gate, w2, b2, sw1, sb1, sgate, sw2, sb2, shared_weight, ln_g, ln_b):
        import jax, jax.numpy as jnp
        import numpy as np
        E = 8
        K = 2
        LN_EPS = 1e-05

        def _expert_ffn(x, w1, b1, gate, w2, b2):
            h = jax.nn.gelu((x @ w1 + b1) * gate, approximate=False)
            return h @ w2 + b2
        x = hidden_states
        logits = jnp.einsum('bsd,de->bse', x, router_w) + router_b
        probs = jax.nn.softmax(logits, axis=-1)
        topk_p, topk_i = jax.lax.top_k(probs, K)
        topk_p = topk_p / jnp.sum(topk_p, axis=-1, keepdims=True)
        combine = jnp.sum(jax.nn.one_hot(topk_i, E, dtype=x.dtype) * topk_p[..., None], axis=-2)
        moe = jnp.zeros_like(x)
        for e in range(E):
            moe = moe + combine[..., e:e + 1] * _expert_ffn(x, w1[e], b1[e], gate[e], w2[e], b2[e])
        shared = _expert_ffn(x, sw1, sb1, sgate, sw2, sb2) * jax.nn.sigmoid(shared_weight)
        y = moe + shared
        mu = jnp.mean(y, axis=-1, keepdims=True)
        var = jnp.var(y, axis=-1, keepdims=True)
        return (y - mu) * jax.lax.rsqrt(var + LN_EPS) * ln_g + ln_b

    def _L1_attn_ref(x, Wqa, Wqb, Wkva, Wkvb, Wout, bout):
        import jax, jax.numpy as jnp
        import numpy as np
        B, S, E = (4, 512, 256)
        H, KVH = (16, 4)
        D = E // H
        QL, KVL = (64, 32)
        ROPE_BASE = 10000.0

        def _rope(x):
            d = x.shape[-1]
            inv_freq = 1.0 / ROPE_BASE ** (jnp.arange(0, d, 2, dtype=jnp.float32) / d)
            t = jnp.arange(x.shape[1], dtype=jnp.float32)
            freqs = jnp.outer(t, inv_freq)
            cos = jnp.cos(freqs)[None, :, None, :].astype(x.dtype)
            sin = jnp.sin(freqs)[None, :, None, :].astype(x.dtype)
            x1, x2 = (x[..., ::2], x[..., 1::2])
            r1 = x1 * cos - x2 * sin
            r2 = x1 * sin + x2 * cos
            return jnp.stack([r1, r2], axis=-1).reshape(x.shape)
        b, s, _ = x.shape
        scale = D ** (-0.5)
        q = (x @ Wqa @ Wqb).reshape(b, s, H, D)
        kv = (x @ Wkva @ Wkvb).reshape(b, s, KVH, D, 2)
        k, v = (kv[..., 0], kv[..., 1])
        q = _rope(q)
        k = _rope(k)
        g = H // KVH
        k = jnp.repeat(k, g, axis=2)
        v = jnp.repeat(v, g, axis=2)
        scores = jnp.einsum('bqhd,bkhd->bhqk', q, k) * scale
        causal = jnp.triu(jnp.ones((s, s), dtype=bool), k=1)
        scores = jnp.where(causal[None, None], -jnp.inf, scores)
        w = jax.nn.softmax(scores, axis=-1)
        out = jnp.einsum('bhqk,bkhd->bqhd', w, v).reshape(b, s, E)
        return out @ Wout + bout

    def _L1_ffn_ref(x, w_gate, b_gate, W1, b1, W2, b2):
        import jax, jax.numpy as jnp
        import numpy as np
        D_MODEL = 256
        MLP_DIM = 1024
        N_EXPERTS = 8
        B, T = (4, 256)
        b, t, d = x.shape
        x_flat = x.reshape(b * t, d)
        logits = x_flat @ w_gate + b_gate
        probs = jax.nn.softmax(logits, axis=-1)
        route_p = jnp.max(probs, axis=-1)
        route_idx = jnp.argmax(probs, axis=-1)
        h = jnp.einsum('nd,edm->enm', x_flat, W1) + b1[:, None, :]
        h = jax.nn.relu(h)
        y = jnp.einsum('enm,emd->end', h, W2) + b2[:, None, :]
        n = b * t
        out = y[route_idx, jnp.arange(n)] * route_p[:, None]
        return out.reshape(b, t, d)
    h = _L0_tok_ref(x, L0_tok_head_weight_proj, L0_tok_head_weight, L0_tok_tail_weight_proj_0, L0_tok_tail_weight_0, L0_tok_tail_weight_proj_1, L0_tok_tail_weight_1)
    h = h + _L0_attn_ref(_layernorm(h, axis=-1), L0_attn_ln_gamma, L0_attn_ln_beta, L0_attn_W_in, L0_attn_conv_w, L0_attn_conv_b, L0_attn_W_xproj, L0_attn_W_dt, L0_attn_b_dt, L0_attn_A_log, L0_attn_D_param, L0_attn_W_out)
    h = h + _L0_ffn_ref(_layernorm(h, axis=-1), L0_ffn_router_w, L0_ffn_router_b, L0_ffn_w1, L0_ffn_b1, L0_ffn_gate, L0_ffn_w2, L0_ffn_b2, L0_ffn_sw1, L0_ffn_sb1, L0_ffn_sgate, L0_ffn_sw2, L0_ffn_sb2, L0_ffn_shared_weight, L0_ffn_ln_g, L0_ffn_ln_b)
    h = h + _L1_attn_ref(_layernorm(h, axis=-1), L1_attn_Wqa, L1_attn_Wqb, L1_attn_Wkva, L1_attn_Wkvb, L1_attn_Wout, L1_attn_bout)
    h = h + _L1_ffn_ref(_layernorm(h, axis=-1), L1_ffn_w_gate, L1_ffn_b_gate, L1_ffn_W1, L1_ffn_b1, L1_ffn_W2, L1_ffn_b2)
    return h

_drawn_inputs = setup_inputs


def setup_inputs(seed=0):
    import zlib

    import numpy as np

    out = dict(_drawn_inputs(seed))
    spreads = {'L0_attn_ln_gamma': (1.0, 0.6),
     'L0_attn_ln_beta': (0.0, 0.492),
     'L0_attn_D_param': (1.0, 0.6),
     'L0_ffn_router_b': (0.0, 0.1),
     'L0_ffn_b1': (0.0, 0.1),
     'L0_ffn_gate': (1.0, 0.2),
     'L0_ffn_b2': (0.0, 0.1),
     'L0_ffn_sb1': (0.0, 0.1),
     'L0_ffn_sgate': (1.0, 0.2),
     'L0_ffn_sb2': (0.0, 0.1),
     'L0_ffn_ln_g': (1.0, 0.2),
     'L0_ffn_ln_b': (0.0, 0.1),
     'L1_ffn_b1': (0.0, 2.0),
     'L1_ffn_b2': (0.0, 1.778)}
    factors = {'L0_attn_conv_b': 7.063,
     'L0_attn_W_xproj': 8.0,
     'L0_attn_W_dt': 8.0,
     'L0_attn_b_dt': 8.0,
     'L0_attn_A_log': 8.0,
     'L1_attn_Wqa': 8.0,
     'L1_attn_Wqb': 8.0,
     'L1_attn_Wkva': 8.0,
     'L1_attn_Wkvb': 8.0,
     'L1_attn_Wout': 8.0,
     'L1_attn_bout': 16.009,
     'L1_ffn_b_gate': 25.259,
     'L1_ffn_W1': 6.149,
     'L1_ffn_W2': 3.25}
    for name, (base, spread) in spreads.items():
        noise = np.random.default_rng([zlib.crc32(name.encode()), seed]).standard_normal(out[name].shape)
        drawn = base * np.exp(spread * noise) if base else spread * noise
        out[name] = jnp.asarray(drawn.astype(out[name].dtype))
    for name, factor in factors.items():
        out[name] = (out[name] * factor).astype(out[name].dtype)
    return out
```

```python
from contextlib import ExitStack

import numpy as np

import concourse.bass as bass
from concourse import mybir

F32 = mybir.dt.float32
BF16 = mybir.dt.bfloat16
I32 = mybir.dt.int32
U32 = mybir.dt.uint32
ALU = mybir.AluOpType
ACT = mybir.ActivationFunctionType
AXX = mybir.AxisListType.X

P = 128
TILES = 16
TOKENS = TILES * P
DIM = 256
KC = DIM // P
SEQ_PER_GROUP = 4
GROUPS = TILES // SEQ_PER_GROUP
GT = SEQ_PER_GROUP * P
EPS = 1e-5

CUTOFFS = (0, 5000, 20000, 50000)
EMB_WIDTHS = (256, 64, 16)
EMB_STARTS = (0, 256, 320)
EMB_DIM = 336
EMB_CHUNKS = ((0, 128), (128, 128), (256, 80))

INNER = 512
DC = INNER // P
STATE = 16
TAPS = 4
DT_RANK = 32
SQ = 4
NQ = STATE // SQ

EXPERTS = 8
FF = 1024
FC = FF // P
SHARED_FF = 512
SC = SHARED_FF // P

HEADS = 16
KV_HEADS = 4
HEAD_DIM = 16


def nth(i, per, k=0):
    return i * per + k + 1


class Chain:

    def __init__(self, eng, sem, first=0):
        self.eng, self.sem, self.first, self.n = eng, sem, first, 0

    def __call__(self, ins):
        ins.then_inc(self.sem, 1)
        self.n += 1
        self.eng.wait_ge(self.sem, self.first + self.n)


class Memory:

    def __init__(self, nc, ctx, stage):
        self.nc, self.ctx, self.stage = nc, ctx, stage

    def sb(self, name, shape, dt=F32):
        return self.ctx.enter_context(self.nc.sbuf_tensor(f"{self.stage}_{name}", shape, dt))

    def ps(self, name, shape, dt=F32):
        return self.ctx.enter_context(self.nc.psum_tensor(f"{self.stage}_{name}", shape, dt))

    def sem(self, name):
        return self.ctx.enter_context(self.nc.semaphore(f"{self.stage}_{name}"))


RSQRT_LINKS = 12


def rsqrt_newton(dve, link, out, var, half):
    link(dve.tensor_scalar(var, var, EPS, None, ALU.add))
    link(dve.tensor_scalar(half.bitcast(I32), var.bitcast(I32), 1, None, ALU.logical_shift_right))
    link(dve.tensor_scalar(out.bitcast(I32), half.bitcast(I32), -1.0, float(0x5F3759DF), ALU.mult, ALU.add))
    for _ in range(3):
        link(dve.scalar_tensor_tensor(half, out, -0.5, out, ALU.mult, ALU.mult))
        link(dve.tensor_tensor(half, half, var, ALU.mult))
        link(dve.scalar_tensor_tensor(out, half, 1.5, out, ALU.add, ALU.mult))


def norm_links(n):
    return 2 * n + 6 + RSQRT_LINKS


def layer_norm(dve, link, outs, ins, stats, mean_var, rstd, half):
    n, width = len(ins), ins[0].shape[-1]
    mean, var, even_odd = mean_var[:, 0, 0:n], mean_var[:, 1, 0:n], mean_var[:, 2, 0:n]
    for i, x in enumerate(ins):
        link(dve.bn_stats(stats[:, i, :], x))
    link(dve.tensor_tensor(mean, stats[:, 0:n, 1], stats[:, 0:n, 4], ALU.add))
    link(dve.tensor_scalar(mean, mean, 0.5, None, ALU.mult))
    link(dve.tensor_tensor(even_odd, stats[:, 0:n, 1], stats[:, 0:n, 4], ALU.subtract))
    link(dve.scalar_tensor_tensor(even_odd, even_odd, 0.25, even_odd, ALU.mult, ALU.mult))
    link(dve.tensor_tensor(var, stats[:, 0:n, 2], stats[:, 0:n, 5], ALU.add))
    link(dve.scalar_tensor_tensor(var, var, 1.0 / width, even_odd, ALU.mult, ALU.add))
    rsqrt_newton(dve, link, rstd[:, 0:n], var, half[:, 0:n])
    for i, x in enumerate(ins):
        link(dve.tensor_scalar(outs[i], x, mean[:, i:i + 1], rstd[:, i:i + 1], ALU.subtract, ALU.mult))


def norm_scratch(mem, n):
    return (mem.sb("stats", [P, n, 6]), mem.sb("mean_var", [P, 3, n]), mem.sb("rstd", [P, n]), mem.sb("half", [P, n]))


def make_constants(nc, ctx):
    mem = Memory(nc, ctx, "const")
    ident = mem.sb("ident", [P, P])
    made = mem.sem("made")
    with nc.Block() as block:
        @block.gpsimd
        def _(pool):
            pool.memset(ident[:, :], 0.0).then_inc(made, 1)
            pool.wait_ge(made, 1)
            pool.affine_select(out=ident[:, :], in_=ident[:, :], compare_op=ALU.not_equal, fill=1.0,
                               base=0, pattern=[[-1, P]], channel_multiplier=1).then_inc(made, 1)
            pool.wait_ge(made, 2)
    return ident


def embed(nc, h, ident, token_ids, tables, projections):
    with ExitStack() as ctx:
        mem = Memory(nc, ctx, "emb")
        ids = mem.sb("ids", [P, TILES], I32)
        rows = mem.sb("rows", [P, 3, TILES], I32)
        emb = mem.sb("emb", [P, TILES, EMB_DIM])
        proj = mem.sb("proj", [P, 3, DIM])
        emb_t = mem.sb("emb_t", [P, 2, 3, P])
        t_ps = mem.ps("t_ps", [P, 2, 512])
        h_ps = mem.ps("h_ps", [P, 2, 512])
        ids_in, proj_in = mem.sem("ids_in"), mem.sem("proj_in")
        cleared, rows_ready = mem.sem("cleared"), mem.sem("rows_ready")
        gathered = [mem.sem(f"gathered{g}") for g in range(GROUPS)]
        transposed, copied, projected, stored = (mem.sem(n) for n in ("transposed", "copied", "projected", "stored"))

        with nc.Block() as block:
            @block.sync
            def _(sp):
                sp.dma_start(ids[:, :], token_ids).then_inc(ids_in, 16)
                for c, (a, n) in enumerate(EMB_CHUNKS):
                    sp.dma_start(proj[0:n, c, :], projections[a:a + n, :]).then_inc(proj_in, 16)

            @block.vector
            def _(dve):
                dve.memset(emb[:, :, :], 0.0).then_inc(cleared, 1)
                dve.wait_ge(ids_in, 16)
                for i in range(3):
                    dve.tensor_scalar(rows[:, i, :], ids[:, :], float(-CUTOFFS[i]), None, ALU.add).then_inc(rows_ready, 1)
                for s in range(TILES):
                    dve.wait_ge(projected, s + 1)
                    dve.tensor_scalar(h[:, s, :], h_ps[:, s % 2, 0:DIM], 16.0, None, ALU.mult).then_inc(stored, 1)

            @block.gpsimd
            def _(pool):
                pool.wait_ge(cleared, 1)
                pool.wait_ge(rows_ready, 3)
                for s in range(TILES):
                    for i in range(3):
                        a, n = EMB_STARTS[i], EMB_WIDTHS[i]
                        pool.indirect_dma_start(
                            emb[:, s, a:a + n], None, tables[i],
                            bass.IndirectOffsetOnAxis(rows[:, i, s:s + 1].bitcast(U32), 0),
                            bounds_check=CUTOFFS[i + 1] - CUTOFFS[i] - 1, oob_is_err=False,
                        ).then_inc(gathered[s // SEQ_PER_GROUP], 16)

            @block.tensor
            def _(pe):
                for s in range(TILES + 1):
                    if s < TILES:
                        if s % SEQ_PER_GROUP == 0:
                            pe.wait_ge(gathered[s // SEQ_PER_GROUP], 16 * 3 * SEQ_PER_GROUP)
                        if s >= 2:
                            pe.wait_ge(copied, 2 * (s - 1))
                        for c, (a, n) in enumerate(EMB_CHUNKS):
                            ins = pe.transpose(t_ps[0:n, s % 2, c * P:(c + 1) * P], emb[:, s, a:a + n], ident[:, :])
                        ins.then_inc(transposed, 1)
                    if s >= 1:
                        v = s - 1
                        if v == 0:
                            pe.wait_ge(proj_in, 48)
                        if v >= 2:
                            pe.wait_ge(stored, v - 1)
                        pe.wait_ge(copied, 2 * v + 2)
                        for c, (a, n) in enumerate(EMB_CHUNKS):
                            ins = pe.matmul(h_ps[:, v % 2, 0:DIM], emb_t[0:n, v % 2, c, :], proj[0:n, c, :],
                                            start=(c == 0), stop=(c == 2))
                        ins.then_inc(projected, 1)

            @block.scalar
            def _(act):
                for s in range(TILES):
                    act.wait_ge(transposed, s + 1)
                    if s >= 2:
                        act.wait_ge(projected, s - 1)
                    act.activation(emb_t[:, s % 2, 0:2, :], t_ps[:, s % 2, 0:2 * P], ACT.Copy).then_inc(copied, 1)
                    act.activation(emb_t[0:80, s % 2, 2, :], t_ps[0:80, s % 2, 2 * P:3 * P], ACT.Copy).then_inc(copied, 1)


def mamba(nc, h, ident, w, bc_dram):
    with ExitStack() as ctx:
        mem = Memory(nc, ctx, "mam")
        w_in = mem.sb("w_in", [P, KC, 2 * INNER])
        w_x = mem.sb("w_x", [P, DC, DT_RANK + 2 * STATE])
        w_dt = mem.sb("w_dt", [DT_RANK, INNER])
        w_out = mem.sb("w_out", [P, DC, DIM])
        gamma, beta = mem.sb("gamma", [P, KC]), mem.sb("beta", [P, KC])
        conv_w, conv_b = mem.sb("conv_w", [P, DC, TAPS]), mem.sb("conv_b", [P, DC])
        b_dt, skip = mem.sb("b_dt", [P, DC]), mem.sb("skip", [P, DC])
        a_log, decay = mem.sb("a_log", [P, DC, STATE]), mem.sb("decay", [P, DC, STATE])

        xa = mem.sb("xa", [P, SEQ_PER_GROUP, DIM])
        xn = mem.sb("xn", [P, SEQ_PER_GROUP, DIM])
        xn_t = mem.sb("xn_t", [P, KC, GT])
        conv = mem.sb("conv", [P, 2, GT])
        u = mem.sb("u", [P, DC, GT])
        silu_z = mem.sb("silu_z", [P, DC, GT])
        x_proj = mem.sb("x_proj", [DT_RANK + 2 * STATE, GT])
        soft = mem.sb("soft", [P, 2, GT])
        delta = mem.sb("delta", [P, DC, GT])
        delta_u = mem.sb("delta_u", [P, DC, GT])
        bc = mem.sb("bc", [P, 2, 2, SQ, GT])
        da = mem.sb("da", [P, 2, SQ, GT])
        hs = mem.sb("hs", [P, 2, SQ, GT])
        y = mem.sb("y", [P, DC, GT])
        scratch = norm_scratch(mem, SEQ_PER_GROUP)

        bank = mem.ps("bank", [P, 2, 512])
        wide = mem.ps("wide", [P, 2, 512])
        y_ps = mem.ps("y_ps", [P, DC, 512])

        weights_in = mem.sem("weights_in")
        decay_ready = mem.sem("decay_ready")
        chain = mem.sem("chain")
        xn_ready, xn_transposed, xn_t_ready = mem.sem("xn_ready"), mem.sem("xn_transposed"), mem.sem("xn_t_ready")
        xz_ready = mem.sem("xz_ready")
        bank_free = [mem.sem(f"bank_free{b}") for b in range(2)]
        wide_free = mem.sem("wide_free")
        conv_ready, u_ready = mem.sem("conv_ready"), mem.sem("u_ready")
        proj_ready, proj_copied = mem.sem("proj_ready"), mem.sem("proj_copied")
        bc_written, bc_in, bc_free = mem.sem("bc_written"), [mem.sem("bc_in0"), mem.sem("bc_in1")], mem.sem("bc_free")
        pre_delta, abs_ready, log_ready = mem.sem("pre_delta"), mem.sem("abs_ready"), mem.sem("log_ready")
        act_chain = mem.sem("act_chain")
        soft_free = mem.sem("soft_free")
        delta_ready = mem.sem("delta_ready")
        da_ready, scanned, hc_ready, summed = (mem.sem(n) for n in ("da_ready", "scanned", "hc_ready", "summed"))
        y_free, y_ready, out_ready = mem.sem("y_free"), mem.sem("y_ready"), mem.sem("out_ready")
        da_cleared = mem.sem("da_cleared")

        UNITS = NQ * DC
        BANK_USES = (7, 6)
        DVE_LINKS = 2 * norm_links(SEQ_PER_GROUP) + DC * (TAPS + 2) + UNITS + 2 * SEQ_PER_GROUP
        ACT_LINKS = 2 * DC

        with nc.Block() as block:
            @block.sync
            def _(sp):
                for dst, src in ((w_in[:, :, :], w["W_in"]), (w_x[:, :, :], w["W_xproj"]), (w_dt[:, :], w["W_dt"]),
                                 (w_out[:, :, :], w["W_out"]), (gamma[:, :], w["ln_gamma"]), (beta[:, :], w["ln_beta"]),
                                 (conv_w[:, :, :], w["conv_w"]), (conv_b[:, :], w["conv_b"]), (b_dt[:, :], w["b_dt"]),
                                 (skip[:, :], w["D_param"]), (a_log[:, :, :], w["A_log"])):
                    sp.dma_start(dst, src).then_inc(weights_in, 16)
                sp.sem_inc(bc_free, 2)
                with sp.Fori(0, GROUPS) as g:
                    sp.wait_ge(proj_copied, nth(g, 1))
                    sp.dma_start(bc_dram[bass.ds(g, 1), :, :].rearrange("g r t -> (g r) t"),
                                 x_proj[DT_RANK:, :]).then_inc(bc_written, 16)
                    sp.wait_ge(bc_written, 16 * g + 16)
                    for q in range(NQ):
                        sp.wait_ge(bc_free, nth(g, NQ, q))
                        for k in range(2):
                            row = k * STATE + q * SQ
                            src = bc_dram[bass.ds(g, 1), row:row + SQ, :].rearrange("g r t -> (g r t)")
                            sp.dma_start(bc[:, q % 2, k, :, :].rearrange("p r t -> p (r t)"),
                                         src.partition_broadcast(P)).then_inc(bc_in[q % 2], 16)

            @block.tensor
            def _(pe):
                pe.wait_ge(weights_in, 16 * 11)
                with pe.Fori(0, GROUPS) as g:
                    used = [0, 0]

                    def take(b):
                        pe.wait_ge(bank_free[b], nth(g, BANK_USES[b], used[b]))
                        used[b] += 1

                    pe.wait_ge(xn_ready, nth(g, 1))
                    pe.wait_ge(wide_free, nth(g, 1))
                    for k in range(KC):
                        for s in range(SEQ_PER_GROUP):
                            ins = pe.transpose(wide[:, k, s * P:(s + 1) * P], xn[:, s, k * P:(k + 1) * P], ident[:, :])
                    ins.then_inc(xn_transposed, 1)
                    pe.wait_ge(xn_t_ready, nth(g, KC, KC - 1))
                    for c in range(2 * DC):
                        take(c % 2)
                        for k in range(KC):
                            ins = pe.matmul(bank[:, c % 2, :], w_in[:, k, c * P:(c + 1) * P], xn_t[:, k, :],
                                            start=(k == 0), stop=(k == KC - 1))
                        ins.then_inc(xz_ready, 1)
                    pe.wait_ge(u_ready, nth(g, DC, DC - 1))
                    take(0)
                    for c in range(DC):
                        ins = pe.matmul(bank[0:DT_RANK + 2 * STATE, 0, :], w_x[:, c, :], u[:, c, :],
                                        start=(c == 0), stop=(c == DC - 1))
                    ins.then_inc(proj_ready, 1)
                    pe.wait_ge(proj_copied, nth(g, 1))
                    for c in range(DC):
                        take(c % 2)
                        pe.matmul(bank[:, c % 2, :], w_dt[:, c * P:(c + 1) * P], x_proj[0:DT_RANK, :],
                                  start=True, stop=True).then_inc(pre_delta, 1)
                    pe.wait_ge(y_free, nth(g, 1))
                    for q in range(NQ):
                        for c in range(DC):
                            n = q * DC + c
                            pe.wait_ge(hc_ready, nth(g, UNITS, n))
                            for i in range(SQ):
                                ins = pe.matmul(y_ps[:, c, :], ident[:, :], hs[:, n % 2, i, :],
                                                start=(q == 0 and i == 0), stop=(q == NQ - 1 and i == SQ - 1))
                            ins.then_inc(summed, 1)
                    pe.wait_ge(y_ready, nth(g, DC, DC - 1))
                    for s in range(SEQ_PER_GROUP):
                        for c in range(DC):
                            ins = pe.matmul(wide[:, s // 2, (s % 2) * DIM:(s % 2 + 1) * DIM],
                                            y[:, c, s * P:(s + 1) * P], w_out[:, c, :],
                                            start=(c == 0), stop=(c == DC - 1))
                    ins.then_inc(out_ready, 1)

            @block.scalar
            def _(act):
                act.wait_ge(weights_in, 16 * 11)
                act.activation(decay[:, :, :], a_log[:, :, :], ACT.Exp).then_inc(decay_ready, 1)
                with act.Fori(0, GROUPS) as g:
                    link = Chain(act, act_chain, g * ACT_LINKS)
                    act.wait_ge(xn_transposed, nth(g, 1))
                    for k in range(KC):
                        act.activation(xn_t[:, k, :], wide[:, k, :], ACT.Identity, bias=beta[:, k:k + 1],
                                       scale=gamma[:, k:k + 1]).then_inc(xn_t_ready, 1)
                    for c in range(DC):
                        act.wait_ge(conv_ready, nth(g, DC, c))
                        act.activation(u[:, c, :], conv[:, c % 2, :], ACT.Silu).then_inc(u_ready, 1)
                    for c in range(DC):
                        act.wait_ge(xz_ready, nth(g, 2 * DC, DC + c))
                        act.activation(silu_z[:, c, :], bank[:, c % 2, :], ACT.Silu).then_inc(bank_free[c % 2], 1)
                    act.wait_ge(proj_ready, nth(g, 1))
                    act.activation(x_proj[:, :], bank[0:DT_RANK + 2 * STATE, 0, :], ACT.Copy)\
                       .then_inc(proj_copied, 1)
                    act.wait_ge(proj_copied, nth(g, 1))
                    act.sem_inc(bank_free[0], 1)
                    act.preload_act_table_set("natural_log_exp_and_others")
                    for c in range(DC):
                        act.wait_ge(pre_delta, nth(g, DC, c))
                        act.wait_ge(soft_free, nth(g, DC, c))
                        act.activation(soft[:, c % 2, :], bank[:, c % 2, :], ACT.Abs, bias=b_dt[:, c:c + 1])\
                           .then_inc(abs_ready, 1)
                        act.wait_ge(abs_ready, nth(g, DC, c))
                        link(act.activation(soft[:, c % 2, :], soft[:, c % 2, :], ACT.Exp, scale=-1.0))
                        link(act.activation(soft[:, c % 2, :], soft[:, c % 2, :], ACT.Ln, bias=1.0))
                        act.sem_inc(log_ready, 1)
                    assert link.n == ACT_LINKS
                    for q in range(NQ):
                        for c in range(DC):
                            n = q * DC + c
                            if q == 0:
                                act.wait_ge(delta_ready, nth(g, DC, c))
                            act.wait_ge(scanned, nth(g, UNITS, n))
                            for i in range(SQ):
                                ins = act.activation(
                                    da[:, n % 2, i, :].rearrange("p (s t) -> p s t", t=P)[:, :, 1:],
                                    delta[:, c, :].rearrange("p (s t) -> p s t", t=P)[:, :, 1:],
                                    ACT.Exp, scale=decay[:, c, q * SQ + i:q * SQ + i + 1])
                            ins.then_inc(da_ready, 1)

            @block.vector
            def _(dve):
                dve.memset(da[:, :, :, :], 0.0).then_inc(da_cleared, 1)
                dve.wait_ge(decay_ready, 1)
                dve.tensor_scalar(decay[:, :, :], decay[:, :, :], -1.0, None, ALU.mult).then_inc(decay_ready, 1)
                dve.wait_ge(decay_ready, 2)
                dve.wait_ge(da_cleared, 1)
                for b in range(2):
                    dve.sem_inc(bank_free[b], 1)
                dve.sem_inc(wide_free, 1)
                dve.sem_inc(y_free, 1)
                dve.sem_inc(soft_free, 2)
                dve.sem_inc(scanned, 2)
                with dve.Fori(0, GROUPS) as g:
                    link = Chain(dve, chain, g * DVE_LINKS)
                    h_tiles = [h[:, bass.ds(g * SEQ_PER_GROUP + s, 1), :].rearrange("p a d -> p (a d)")
                               for s in range(SEQ_PER_GROUP)]
                    layer_norm(dve, link, [xa[:, s, :] for s in range(SEQ_PER_GROUP)], h_tiles, *scratch)
                    layer_norm(dve, link, [xn[:, s, :] for s in range(SEQ_PER_GROUP)],
                               [xa[:, s, :] for s in range(SEQ_PER_GROUP)], *scratch)
                    dve.sem_inc(xn_ready, 1)
                    for c in range(DC):
                        dve.wait_ge(xz_ready, nth(g, 2 * DC, c))
                        if c >= 2:
                            dve.wait_ge(u_ready, nth(g, DC, c - 2))
                        x_c = bank[:, c % 2, :].rearrange("p (s t) -> p s t", t=P)
                        o_c = conv[:, c % 2, :].rearrange("p (s t) -> p s t", t=P)
                        link(dve.tensor_scalar(conv[:, c % 2, :], bank[:, c % 2, :], conv_w[:, c, TAPS - 1:TAPS],
                                               conv_b[:, c:c + 1], ALU.mult, ALU.add))
                        for k in range(1, TAPS):
                            ins = dve.scalar_tensor_tensor(o_c[:, :, k:], x_c[:, :, :P - k],
                                                           conv_w[:, c, TAPS - 1 - k:TAPS - k],
                                                           o_c[:, :, k:], ALU.mult, ALU.add)
                            if k < TAPS - 1:
                                link(ins)
                        ins.then_inc(conv_ready, 1)
                        dve.wait_ge(conv_ready, nth(g, DC, c))
                        dve.sem_inc(bank_free[c % 2], 1)
                    for c in range(DC):
                        dve.wait_ge(abs_ready, nth(g, DC, c))
                        link(dve.tensor_scalar(delta[:, c, :], bank[:, c % 2, :], b_dt[:, c:c + 1], 0.0,
                                               ALU.add, ALU.max))
                        dve.sem_inc(bank_free[c % 2], 1)
                        dve.wait_ge(log_ready, nth(g, DC, c))
                        dve.tensor_tensor(delta[:, c, :], delta[:, c, :], soft[:, c % 2, :], ALU.add)\
                           .then_inc(delta_ready, 1)
                        dve.wait_ge(delta_ready, nth(g, DC, c))
                        dve.sem_inc(soft_free, 1)
                        link(dve.tensor_tensor(delta_u[:, c, :], delta[:, c, :], u[:, c, :], ALU.mult))
                    for q in range(NQ):
                        for c in range(DC):
                            n = q * DC + c
                            if c == 0:
                                dve.wait_ge(bc_in[q % 2], 32 * (g * (NQ // 2) + q // 2 + 1))
                            if n >= 2:
                                dve.wait_ge(summed, nth(g, UNITS, n - 2))
                            x_n = hs[:, n % 2, :, :]
                            link(dve.tensor_tensor(x_n, delta_u[:, c, :].unsqueeze(1).to_broadcast([P, SQ, GT]),
                                                   bc[:, q % 2, 0, :, :], ALU.mult))
                            dve.wait_ge(da_ready, nth(g, UNITS, n))
                            flat = x_n.rearrange("p i t -> p (i t)")
                            dve.tensor_tensor_scan(flat, da[:, n % 2, :, :].rearrange("p i t -> p (i t)"), flat,
                                                   0.0, ALU.mult, ALU.add).then_inc(scanned, 1)
                            dve.wait_ge(scanned, nth(g, UNITS, n) + 2)
                            dve.tensor_tensor(x_n, x_n, bc[:, q % 2, 1, :, :], ALU.mult).then_inc(hc_ready, 1)
                        dve.wait_ge(hc_ready, nth(g, UNITS, n))
                        dve.sem_inc(bc_free, 1)
                    for c in range(DC):
                        dve.wait_ge(summed, nth(g, UNITS, UNITS - DC + c))
                        link(dve.scalar_tensor_tensor(y[:, c, :], u[:, c, :], skip[:, c:c + 1], y_ps[:, c, :],
                                                      ALU.mult, ALU.add))
                        dve.tensor_tensor(y[:, c, :], y[:, c, :], silu_z[:, c, :], ALU.mult).then_inc(y_ready, 1)
                    dve.wait_ge(y_ready, nth(g, DC, DC - 1))
                    dve.sem_inc(y_free, 1)
                    for s in range(SEQ_PER_GROUP):
                        link(dve.tensor_tensor(h_tiles[s], h_tiles[s], xa[:, s, :], ALU.add))
                    dve.wait_ge(out_ready, nth(g, 1))
                    for s in range(SEQ_PER_GROUP):
                        link(dve.tensor_tensor(h_tiles[s], h_tiles[s],
                                               wide[:, s // 2, (s % 2) * DIM:(s % 2 + 1) * DIM], ALU.add))
                    dve.sem_inc(wide_free, 1)
                    assert link.n == DVE_LINKS


def attention(nc, h, ident, w):
    q_rank, kv_rank, kv_width = 64, 32, KV_HEADS * HEAD_DIM
    reps = HEADS // KV_HEADS
    with ExitStack() as ctx:
        mem = Memory(nc, ctx, "att")
        wqa, wkva = mem.sb("wqa", [P, KC, q_rank]), mem.sb("wkva", [P, KC, kv_rank])
        wqb = mem.sb("wqb", [q_rank, 2, DIM])
        wk = mem.sb("wk", [kv_rank, 2, kv_width])
        wv = mem.sb("wv", [kv_rank, kv_width])
        wout = mem.sb("wout", [P, KC, DIM])
        bout = mem.sb("bout", [P, DIM])
        rope_q, rope_k = mem.sb("rope_q", [P, 2, P]), mem.sb("rope_k", [kv_width, 2, P])
        pad_q, pad_k = mem.sb("pad_q", [P, 2, P]), mem.sb("pad_k", [kv_width, KV_HEADS, P])
        ident_b = mem.sb("ident_b", [P, P], BF16)
        causal = mem.sb("causal", [P, KV_HEADS, P], BF16)

        x = mem.sb("x", [P, SEQ_PER_GROUP, DIM])
        x_t = mem.sb("x_t", [P, KC, GT])
        qa, kva = mem.sb("qa", [q_rank, GT]), mem.sb("kva", [kv_rank, GT])
        turned = mem.sb("turned", [P, 3, GT])
        part = mem.sb("part", [P, GT])
        qp, kp = mem.sb("qp", [P, KV_HEADS, GT]), mem.sb("kp", [P, KV_HEADS, GT])
        v = mem.sb("v", [P, SEQ_PER_GROUP, KV_HEADS, HEAD_DIM + 1])
        top = mem.sb("top", [P, HEADS])
        prob = mem.sb("prob", [P, 2, HEADS, P])
        prob_t = mem.sb("prob_t", [P, 2, 8, P])
        inverse = mem.sb("inverse", [P, HEADS])
        o = mem.sb("o", [P, DIM])
        o_t = mem.sb("o_t", [P, KC, P])
        scratch = norm_scratch(mem, SEQ_PER_GROUP)

        s_ps = mem.ps("s_ps", [P, reps, KV_HEADS, P])
        pt_ps = mem.ps("pt_ps", [P, 2, 512])
        misc = mem.ps("misc", [P, 2, 512])

        weights_in, constants, chain = mem.sem("weights_in"), mem.sem("constants"), mem.sem("chain")
        free = [mem.sem("free0"), mem.sem("free1")]
        x_ready, x_turned, x_t_ready = mem.sem("x_ready"), mem.sem("x_turned"), mem.sem("x_t_ready")
        low_done, low_ready = mem.sem("low_done"), mem.sem("low_ready")
        qk_done, roped = mem.sem("qk_done"), mem.sem("roped")
        padded, pad_ready = mem.sem("padded"), mem.sem("pad_ready")
        v_done, v_ready = mem.sem("v_done"), mem.sem("v_ready")
        scores_done, scores_free, prob_ready, prob_free = (
            mem.sem(n) for n in ("scores_done", "scores_free", "prob_ready", "prob_free"))
        shifted = mem.sem("shifted")
        prob_turned, prob_t_ready, prob_used = mem.sem("prob_turned"), mem.sem("prob_t_ready"), mem.sem("prob_used")
        o_done, o_ready, o_turned, o_t_ready = (mem.sem(n) for n in ("o_done", "o_ready", "o_turned", "o_t_ready"))
        out_done, out_added = mem.sem("out_done"), mem.sem("out_added")

        S = SEQ_PER_GROUP
        USES = (10 + 2 * S, 9 + S)
        DVE_LINKS = norm_links(S) + 6 + S * (1 + 1 + 1)
        loads = ((wqa[:, :, :], w["Wqa"]), (wkva[:, :, :], w["Wkva"]), (wqb[:, :, :], w["Wqb"]), (wk[:, :, :], w["Wk"]),
                 (wv[:, :], w["Wv"]), (wout[:, :, :], w["Wout"]), (bout[:, :], w["bout"].partition_broadcast(P)),
                 (rope_q[:, :, :], w["rope_q"]), (rope_k[:, :, :], w["rope_k"]),
                 (pad_q[:, :, :], w["pad_q"]), (pad_k[:, :, :], w["pad_k"]))

        with nc.Block() as block:
            @block.sync
            def _(sp):
                for dst, src in loads:
                    sp.dma_start(dst, src).then_inc(weights_in, 16)

            @block.gpsimd
            def _(pool):
                pool.tensor_copy(ident_b[:, :], ident[:, :]).then_inc(constants, 1)
                pool.memset(v[:, :, :, :], 1.0).then_inc(constants, 1)
                pool.memset(causal[:, :, :], 0.0).then_inc(constants, 1)
                pool.wait_ge(constants, 3)
                pool.affine_select(out=causal[:, :, :], in_=causal[:, :, :], compare_op=ALU.is_ge, fill=-1e30, base=0,
                                   pattern=[[0, KV_HEADS], [-1, P]], channel_multiplier=1).then_inc(constants, 1)

            @block.tensor
            def _(pe):
                pe.wait_ge(weights_in, 16 * len(loads))
                pe.wait_ge(constants, 4)
                with pe.Fori(0, GROUPS) as g:
                    used = [0, 0]

                    def take(b):
                        pe.wait_ge(free[b], nth(g, USES[b], used[b]))
                        used[b] += 1

                    pe.wait_ge(x_ready, nth(g, 1))
                    for k in range(KC):
                        take(k)
                        for s in range(S):
                            ins = pe.transpose(misc[:, k, s * P:(s + 1) * P], x[:, s, k * P:(k + 1) * P], ident[:, :])
                        ins.then_inc(x_turned, 1)
                    pe.wait_ge(x_t_ready, nth(g, KC, KC - 1))
                    for b, (wgt, rank) in enumerate(((wqa, q_rank), (wkva, kv_rank))):
                        take(b)
                        for k in range(KC):
                            ins = pe.matmul(misc[0:rank, b, :], wgt[:, k, :], x_t[:, k, :], start=(k == 0), stop=(k == KC - 1))
                        ins.then_inc(low_done, 1)
                    pe.wait_ge(low_ready, nth(g, 2, 1))
                    for c in range(3):
                        for b in range(2):
                            take(b)
                            if c < 2:
                                ins = pe.matmul(misc[:, b, :], wqb[:, b, c * P:(c + 1) * P], qa[:, :], start=True, stop=True)
                            else:
                                ins = pe.matmul(misc[0:kv_width, b, :], wk[:, b, :], kva[:, :], start=True, stop=True)
                        ins.then_inc(qk_done, 1)
                    pe.wait_ge(roped, nth(g, 3, 2))
                    for c in range(KV_HEADS):
                        take(c % 2)
                        pe.matmul(misc[:, c % 2, :], pad_q[:, c % 2, :], turned[:, c // 2, :], start=True, stop=True)\
                          .then_inc(padded, 1)
                    for c in range(KV_HEADS):
                        take(c % 2)
                        pe.matmul(misc[:, c % 2, :], pad_k[:, c, :], turned[0:kv_width, 2, :], start=True, stop=True)\
                          .then_inc(padded, 1)
                    take(0)
                    for s in range(S):
                        ins = pe.matmul(misc[:, 0, s * kv_width:(s + 1) * kv_width], kva[:, s * P:(s + 1) * P], wv[:, :],
                                        start=True, stop=True)
                    ins.then_inc(v_done, 1)

                    def scores(s):
                        pe.wait_ge(scores_free, nth(g, S, s))
                        for r in range(reps):
                            pe.matmul(s_ps[:, r, :, :].rearrange("p c k -> p (c k)"), ident_b[:, :],
                                      causal[:, :, :].rearrange("p c k -> p (c k)"), start=True, stop=False,
                                      skip_group_check=True)
                        for c in range(KV_HEADS):
                            for r in range(reps):
                                rows, cols = slice(32 * r, 32 * r + 32), slice(s * P, (s + 1) * P)
                                ins = pe.matmul(s_ps[:, r, c, :], qp[rows, c, cols], kp[rows, c, cols], start=False,
                                                stop=(c == KV_HEADS - 1), skip_group_check=True)
                        ins.then_inc(scores_done, 1)

                    def values(s):
                        pe.wait_ge(prob_ready, nth(g, S, s))
                        take(1)
                        for half in range(2):
                            if half == 0 and s == 0:
                                pe.wait_ge(prob_t_ready, nth(g, 2 * S) + 1)
                            else:
                                pe.wait_ge(prob_t_ready, nth(g, 2 * S, 2 * s + half) + 1)
                            for i in range(8):
                                ins = pe.transpose(pt_ps[:, i // 4, (i % 4) * P:(i % 4 + 1) * P],
                                                   prob[:, s % 2, half * 8 + i, :], ident[:, :])
                            ins.then_inc(prob_turned, 1)
                            pe.wait_ge(prob_t_ready, nth(g, 2 * S, 2 * s + half) + 2)
                            for i in range(8):
                                r, c = (half * 8 + i) // KV_HEADS, (half * 8 + i) % KV_HEADS
                                head = c * reps + r
                                ins = pe.matmul(misc[:, 1, head * 17:(head + 1) * 17], prob_t[:, half, i, :], v[:, s, c, :],
                                                start=True, stop=True)
                            ins.then_inc(prob_used, 1)

                    def project(s):
                        pe.wait_ge(o_ready, nth(g, S, s))
                        take(0)
                        for k in range(KC):
                            ins = pe.transpose(misc[:, 0, k * P:(k + 1) * P], o[:, k * P:(k + 1) * P], ident[:, :])
                        ins.then_inc(o_turned, 1)
                        pe.wait_ge(o_t_ready, nth(g, S, s))
                        take(0)
                        for k in range(KC):
                            ins = pe.matmul(misc[:, 0, 0:DIM], o_t[:, k, :], wout[:, k, :], start=(k == 0), stop=(k == KC - 1))
                        ins.then_inc(out_done, 1)

                    pe.wait_ge(pad_ready, nth(g, 2 * KV_HEADS, 2 * KV_HEADS - 1))
                    scores(0)
                    pe.wait_ge(v_ready, nth(g, 1))
                    for s in range(S):
                        if s + 1 < S:
                            scores(s + 1)
                        values(s)
                        project(s)

            @block.scalar
            def _(act):
                act.wait_ge(constants, 4)
                act.sem_inc(prob_t_ready, 2)
                with act.Fori(0, GROUPS) as g:
                    for k in range(KC):
                        act.wait_ge(x_turned, nth(g, KC, k))
                        act.activation(x_t[:, k, :], misc[:, k, :], ACT.Copy).then_inc(x_t_ready, 1)
                        act.wait_ge(x_t_ready, nth(g, KC, k))
                        act.sem_inc(free[k], 1)
                    for b, (dst, rank) in enumerate(((qa, q_rank), (kva, kv_rank))):
                        act.wait_ge(low_done, nth(g, 2, b))
                        act.activation(dst[:, :], misc[0:rank, b, :], ACT.Copy).then_inc(low_ready, 1)
                        act.wait_ge(low_ready, nth(g, 2, b))
                        act.sem_inc(free[b], 1)
                    for n in range(2 * KV_HEADS):
                        dst = qp if n < KV_HEADS else kp
                        act.wait_ge(padded, nth(g, 2 * KV_HEADS, n))
                        act.activation(dst[:, n % KV_HEADS, :], misc[:, n % 2, :], ACT.Copy).then_inc(pad_ready, 1)
                        act.wait_ge(pad_ready, nth(g, 2 * KV_HEADS, n))
                        act.sem_inc(free[n % 2], 1)
                    act.wait_ge(v_done, nth(g, 1))
                    act.activation(v[:, :, :, 0:HEAD_DIM].rearrange("p s c d -> p (s c) d"),
                                   misc[:, 0, 0:S * kv_width].rearrange("p (n d) -> p n d", d=HEAD_DIM), ACT.Copy)\
                       .then_inc(v_ready, 1)
                    act.wait_ge(v_ready, nth(g, 1))
                    act.sem_inc(free[0], 1)
                    for s in range(S):
                        act.wait_ge(shifted, nth(g, S, s))
                        flat = prob[:, s % 2, :, :].rearrange("p n k -> p (n k)")
                        act.activation(flat, flat, ACT.Exp).then_inc(prob_ready, 1)
                        for half in range(2):
                            act.wait_ge(prob_turned, nth(g, 2 * S, 2 * s + half))
                            act.wait_ge(prob_used, nth(g, 2 * S, 2 * s + half))
                            act.activation(prob_t[:, half, :, :].rearrange("p n q -> p (n q)"),
                                           pt_ps[:, :, :].rearrange("p a n -> p (a n)"), ACT.Copy).then_inc(prob_t_ready, 1)
                        act.wait_ge(o_turned, nth(g, S, s))
                        act.activation(o_t[:, :, :].rearrange("p k n -> p (k n)"), misc[:, 0, 0:DIM], ACT.Copy)\
                           .then_inc(o_t_ready, 1)
                        act.wait_ge(o_t_ready, nth(g, S, s))
                        act.sem_inc(free[0], 1)

            @block.vector
            def _(dve):
                for b in range(2):
                    dve.sem_inc(free[b], 1)
                dve.sem_inc(scores_free, 1)
                dve.sem_inc(prob_used, 2)
                dve.wait_ge(weights_in, 16 * len(loads))
                with dve.Fori(0, GROUPS) as g:
                    link = Chain(dve, chain, g * DVE_LINKS)
                    h_tiles = [h[:, bass.ds(g * S + s, 1), :].rearrange("p a d -> p (a d)") for s in range(S)]
                    layer_norm(dve, link, [x[:, s, :] for s in range(S)], h_tiles, *scratch)
                    dve.sem_inc(x_ready, 1)
                    for c in range(3):
                        rows, table = (P, rope_q) if c < 2 else (kv_width, rope_k)

                        def over_seqs(k):
                            return table[:, k, :].unsqueeze(1).to_broadcast([rows, S, P])

                        def by_seq(v_):
                            return v_.rearrange("p (s t) -> p s t", t=P)

                        dve.wait_ge(qk_done, nth(g, 3, c))
                        link(dve.tensor_tensor(by_seq(turned[0:rows, c, :]), by_seq(misc[0:rows, 0, :]), over_seqs(0), ALU.mult))
                        dve.sem_inc(free[0], 1)
                        link(dve.tensor_tensor(by_seq(part[0:rows, :]), by_seq(misc[0:rows, 1, :]), over_seqs(1), ALU.mult))
                        dve.sem_inc(free[1], 1)
                        dve.tensor_tensor(turned[0:rows, c, :], turned[0:rows, c, :], part[0:rows, :], ALU.add)\
                           .then_inc(roped, 1)
                        dve.wait_ge(roped, nth(g, 3, c))

                    def shift(s):
                        dve.wait_ge(scores_done, nth(g, S, s))
                        scores = s_ps[:, :, :, :].rearrange("p r c k -> p (r c) k")
                        link(dve.tensor_reduce(top[:, :], scores, AXX, ALU.max))
                        if s >= 2:
                            dve.wait_ge(prob_used, nth(g, 2 * S, 2 * (s - 2) + 1) + 2)
                        dve.tensor_tensor(prob[:, s % 2, :, :], scores, top[:, :].unsqueeze(2).to_broadcast([P, HEADS, P]),
                                          ALU.subtract).then_inc(shifted, 1)
                        dve.wait_ge(shifted, nth(g, S, s))
                        dve.sem_inc(scores_free, 1)

                    shift(0)
                    for s in range(S):
                        if s + 1 < S:
                            shift(s + 1)
                        dve.wait_ge(prob_used, nth(g, 2 * S, 2 * s + 1) + 2)
                        o_all = misc[:, 1, 0:HEADS * 17].rearrange("p (n d) -> p n d", d=17)
                        link(dve.reciprocal(inverse[:, :], o_all[:, :, HEAD_DIM]))
                        if s:
                            dve.wait_ge(o_turned, nth(g, S, s - 1))
                        dve.tensor_tensor(o[:, :].rearrange("p (n d) -> p n d", d=HEAD_DIM), o_all[:, :, 0:HEAD_DIM],
                                          inverse[:, :].unsqueeze(2).to_broadcast([P, HEADS, HEAD_DIM]), ALU.mult)\
                           .then_inc(o_ready, 1)
                        dve.wait_ge(o_ready, nth(g, S, s))
                        dve.sem_inc(free[1], 1)
                        link(dve.tensor_tensor(h_tiles[s], h_tiles[s], bout[:, :], ALU.add))
                        dve.wait_ge(out_done, nth(g, S, s))
                        dve.tensor_tensor(h_tiles[s], h_tiles[s], misc[:, 0, 0:DIM], ALU.add).then_inc(out_added, 1)
                        dve.wait_ge(out_added, nth(g, S, s))
                        dve.sem_inc(free[0], 1)
                    assert link.n == DVE_LINKS, link.n


def most_tiles(choices):
    return (TOKENS * choices + EXPERTS * (P - 1)) // P


def over_tiles(eng, n, body):
    body(0, 0, True, False)
    with eng.Fori(0, (n - 3) // 2) as pair:
        body(pair * 2 + 1, 1, False, False)
        body(pair * 2 + 2, 0, False, False)
    body(n - 2, 1, False, False)
    body(n - 1, 0, False, True)


def moe(nc, h, ident, w, choices, slots, results, parked, stage):
    shared = choices == 2
    n_tiles = most_tiles(choices)
    pairs = choices * TILES
    with ExitStack() as ctx:
        mem = Memory(nc, ctx, stage)
        x = mem.sb("x", [P, TILES, DIM])
        x_t = h[:, :, :].rearrange("p t d -> p (t d)").rearrange("p (k n) -> p k n", k=KC)
        w1 = mem.sb("w1", [P, KC, EXPERTS, FF])
        w2 = mem.sb("w2", [P, FC, EXPERTS, DIM])
        b1 = mem.sb("b1", [P, FC, EXPERTS])
        b2 = mem.sb("b2", [P, EXPERTS, DIM])
        router_w, router_b = mem.sb("router_w", [P, KC, EXPERTS]), mem.sb("router_b", [P, EXPERTS])
        ff = mem.sb("ff", [P, 2, FF])
        hidden = ff[:, 0, :]
        active = ff[:, 1, :].rearrange("p (f n) -> p f n", f=FC)
        shared_act = ff[:, :, :].rearrange("p a n -> p (a n)").rearrange("p (f n) -> p f n", f=SC)
        x_in, x_in_t, y_out = (mem.sb(n, [P, 2, DIM]) for n in ("x_in", "x_in_t", "y_out"))
        if shared:
            gate = mem.sb("gate", [P, FC, EXPERTS])
            sw1, sw2 = mem.sb("sw1", [P, KC, SHARED_FF]), mem.sb("sw2", [P, SC, DIM])
            sb1, sgate = mem.sb("sb1", [P, SC]), mem.sb("sgate", [P, SC])
            sb2, ln_g, ln_b = mem.sb("sb2", [P, DIM]), mem.sb("ln_g", [P, DIM]), mem.sb("ln_b", [P, DIM])
            mix = mem.sb("mix", [P, 1])
        zeros = mem.sb("zeros", [P, DIM])
        lower, ones = mem.sb("lower", [P, P]), mem.sb("ones", [P, P])
        expert_no = mem.sb("expert_no", [P, EXPERTS])
        tile_no = mem.sb("tile_no", [1, n_tiles, EXPERTS])
        logits, top, top_i = mem.sb("logits", [P, TILES, EXPERTS]), mem.sb("top", [P, TILES, 8]), mem.sb("top_i", [P, TILES, 8], U32)
        top_f = mem.sb("top_f", [P, TILES, choices])
        total, weight = mem.sb("total", [P, TILES]), mem.sb("weight", [P, TILES, choices])
        onehot = mem.sb("onehot", [P, choices, TILES, EXPERTS])
        before = mem.sb("before", [P, choices, TILES, EXPERTS])
        counts = mem.sb("counts", [P, pairs, EXPERTS])
        running = mem.sb("running", [P, pairs, EXPERTS])
        tiles_i = mem.sb("tiles_i", [P, EXPERTS], I32)
        tiles_of, last_tile, base = (mem.sb(n, [P, EXPERTS]) for n in ("tiles_of", "last_tile", "base"))
        slot_f, slot = mem.sb("slot_f", [P, pairs]), mem.sb("slot", [P, pairs], I32)
        passed = mem.sb("passed", [1, n_tiles, EXPERTS])
        expert_f, expert = mem.sb("expert_f", [1, n_tiles]), mem.sb("expert", [1, n_tiles], I32)
        scratch = norm_scratch(mem, SEQ_PER_GROUP)

        h_ps = mem.ps("h_ps", [P, 2, 512])
        ht_ps = mem.ps("ht_ps", [P, 2, 512])
        xt_ps = mem.ps("xt_ps", [P, 512])
        y_ps = mem.ps("y_ps", [P, 2, 512])
        route_ps = mem.ps("route_ps", [P, 512])

        small_in, w1_in, w2_in = mem.sem("small_in"), mem.sem("w1_in"), mem.sem("w2_in")
        constants, chain, mixed = mem.sem("constants"), mem.sem("chain"), mem.sem("mixed")
        x_ready, h_parked, h_back = mem.sem("x_ready"), mem.sem("h_parked"), mem.sem("h_back")
        xt_done, xt_copied = mem.sem("xt_done"), mem.sem("xt_copied")
        logits_done, exp_asked, exp_ready, onehot_ready, counted = (
            mem.sem(n) for n in ("logits_done", "exp_asked", "exp_ready", "onehot_ready", "counted"))
        routed, cleared, scattered = mem.sem("routed"), mem.sem("cleared"), mem.sem("scattered")
        sh_done, sh_active, sh_out, sh_kept = (mem.sem(n) for n in ("sh_done", "sh_active", "sh_out", "sh_kept"))
        in_loaded = [mem.sem(f"in_loaded{b}") for b in range(2)]
        in_turned, turn_copied = mem.sem("in_turned"), mem.sem("turn_copied")
        hidden_done, hidden_kept = mem.sem("hidden_done"), mem.sem("hidden_kept")
        hidden_turned, active_ready = mem.sem("hidden_turned"), mem.sem("active_ready")
        y_done, y_kept = mem.sem("y_done"), mem.sem("y_kept")
        y_stored = [mem.sem(f"y_stored{b}") for b in range(2)]
        gathered, combined = [mem.sem("gathered0"), mem.sem("gathered1")], mem.sem("combined")

        small = [(router_w[:, :, :], w["router_w"]), (router_b[:, :], w["router_b"].partition_broadcast(P)),
                 (b1[:, :, :], w["b1"]), (b2[:, :, :].rearrange("p e d -> p (e d)"), w["b2"].partition_broadcast(P))]
        if shared:
            small += [(gate[:, :, :], w["gate"]), (sw1[:, :, :], w["sw1"]), (sw2[:, :, :], w["sw2"]), (sb1[:, :], w["sb1"]),
                      (sgate[:, :], w["sgate"]), (sb2[:, :], w["sb2"].partition_broadcast(P)),
                      (ln_g[:, :], w["ln_g"].partition_broadcast(P)), (ln_b[:, :], w["ln_b"].partition_broadcast(P)),
                      (mix[:, :], w["shared_weight"].partition_broadcast(P))]
        small_all = 16 * len(small)
        sh_uses = GROUPS * SC if shared else 0

        tiles_back = TILES // choices
        rounds = TILES // tiles_back
        back = h[:, :, :]

        def tile_rows(dram, j):
            return dram[bass.ds(j * P, P), :]

        with nc.Block() as block:
            @block.sync
            def _(sp):
                for dst, src in small:
                    sp.dma_start(dst, src).then_inc(small_in, 16)
                sp.dma_start(parked.rearrange("(t p) d -> p t d", p=P), h[:, :, :]).then_inc(h_parked, 16)
                for e in range(EXPERTS):
                    sp.dma_start(w1[:, :, e, :], w["w1"][:, :, e, :]).then_inc(w1_in, 16)
                for e in range(EXPERTS):
                    sp.dma_start(w2[:, :, e, :], w["w2"][:, :, e, :]).then_inc(w2_in, 16)
                sp.wait_ge(scattered, 16 * pairs)

                def load(j, b, first, last):
                    if not first:
                        sp.wait_ge(in_turned, j - 1 + b)
                    sp.dma_start(x_in[:, b, :], tile_rows(slots, j)).then_inc(in_loaded[b], 16)

                over_tiles(sp, n_tiles, load)
                sp.wait_ge(combined, rounds)
                sp.dma_start(h[:, :, :], parked.rearrange("(t p) d -> p t d", p=P)).then_inc(h_back, 16)

            @block.gpsimd
            def _(pool):
                pool.memset(zeros[:, :], 0.0).then_inc(constants, 1)
                pool.memset(lower[:, :], 1.0).then_inc(constants, 1)
                pool.memset(ones[:, :], 1.0).then_inc(constants, 1)
                pool.wait_ge(constants, 3)
                pool.affine_select(out=lower[:, :], in_=lower[:, :], compare_op=ALU.is_gt, fill=0.0, base=0,
                                   pattern=[[1, P]], channel_multiplier=-1).then_inc(constants, 1)
                pool.iota(expert_no[:, :], pattern=[[1, EXPERTS]], base=0, channel_multiplier=0,
                          allow_small_or_imprecise_dtypes=True).then_inc(constants, 1)
                pool.iota(tile_no[:, :, :], pattern=[[1, n_tiles], [0, EXPERTS]], base=0, channel_multiplier=0,
                          allow_small_or_imprecise_dtypes=True).then_inc(constants, 1)
                pool.dma_start(slots.rearrange("(a p) d -> p a d", p=P),
                               zeros[:, :].unsqueeze(1).to_broadcast([P, n_tiles, DIM])).then_inc(cleared, 16)
                pool.wait_ge(cleared, 16)
                pool.wait_ge(routed, 1)
                for t in range(TILES):
                    for k in range(choices):
                        pool.indirect_dma_start(
                            slots, bass.IndirectOffsetOnAxis(slot[:, k * TILES + t:k * TILES + t + 1].bitcast(U32), 0),
                            x[:, t, :], None, bounds_check=n_tiles * P - 1, oob_is_err=False).then_inc(scattered, 16)

                def store(j, b, first, last):
                    pool.wait_ge(y_kept, j + 1)
                    pool.dma_start(tile_rows(results, j), y_out[:, b, :]).then_inc(y_stored[b], 16)

                over_tiles(pool, n_tiles, store)
                pool.wait_ge(y_stored[0], 16 * ((n_tiles + 1) // 2))
                pool.wait_ge(y_stored[1], 16 * (n_tiles // 2))
                for r in range(rounds):
                    if r:
                        pool.wait_ge(combined, r)
                    for i in range(tiles_back):
                        for k in range(choices):
                            n = k * TILES + r * tiles_back + i
                            pool.indirect_dma_start(
                                back[:, i * choices + k, :], None, results,
                                bass.IndirectOffsetOnAxis(slot[:, n:n + 1].bitcast(U32), 0),
                                bounds_check=n_tiles * P - 1, oob_is_err=False).then_inc(gathered[r], 16)

            @block.tensor
            def _(pe):
                pe.wait_ge(small_in, small_all)
                for t in range(TILES + 1):
                    if t < TILES:
                        pe.wait_ge(x_ready, t // SEQ_PER_GROUP + 1)
                        if t >= 2:
                            pe.wait_ge(xt_copied, t - 1)
                        for k in range(KC):
                            ins = pe.transpose(y_ps[:, t % 2, k * P:(k + 1) * P], x[:, t, k * P:(k + 1) * P], ident[:, :])
                        ins.then_inc(xt_done, 1)
                    if t >= 1:
                        v = t - 1
                        pe.wait_ge(xt_copied, v + 1)
                        for k in range(KC):
                            ins = pe.matmul(route_ps[:, v * EXPERTS:(v + 1) * EXPERTS], x_t[:, k, v * P:(v + 1) * P],
                                            router_w[:, k, :], start=(k == 0), stop=(k == KC - 1))
                ins.then_inc(logits_done, 1)
                pe.wait_ge(onehot_ready, choices)
                pe.wait_ge(constants, 6)
                picks = onehot[:, :, :, :].rearrange("p c t e -> p (c t e)")
                width = pairs * EXPERTS
                pe.matmul(h_ps[:, 0, 0:width], lower[:, :], picks, start=True, stop=True)
                pe.matmul(h_ps[:, 1, 0:width], ones[:, :], picks, start=True, stop=True).then_inc(counted, 1)
                pe.wait_ge(routed, 1)
                if shared:
                    for g in range(GROUPS):
                        for f in range(SC):
                            n = g * SC + f
                            if n >= 2:
                                pe.wait_ge(sh_active, n - 1)
                            for k in range(KC):
                                ins = pe.matmul(h_ps[:, n % 2, :], sw1[:, k, f * P:(f + 1) * P],
                                                x_t[:, k, g * GT:(g + 1) * GT], start=(k == 0), stop=(k == KC - 1))
                            ins.then_inc(sh_done, 1)
                        pe.wait_ge(sh_active, (g + 1) * SC)
                        for s in range(SEQ_PER_GROUP):
                            n = g * SEQ_PER_GROUP + s
                            if n >= 2:
                                pe.wait_ge(sh_kept, n - 1)
                            for f in range(SC):
                                ins = pe.matmul(y_ps[:, n % 2, 0:DIM], shared_act[:, f, s * P:(s + 1) * P], sw2[:, f, :],
                                                start=(f == 0), stop=(f == SC - 1))
                            ins.then_inc(sh_out, 1)
                    pe.wait_ge(sh_kept, TILES)

                def turn_input(j, b):
                    pe.wait_ge(in_loaded[b], (j // 2 + 1) * 16 if isinstance(j, int) else j * 8 + (8 if b else 16))
                    pe.wait_ge(turn_copied, j) if not isinstance(j, int) or j > 0 else None
                    for k in range(KC):
                        ins = pe.transpose(xt_ps[:, k * P:(k + 1) * P], x_in[:, b, k * P:(k + 1) * P], ident[:, :])
                    ins.then_inc(in_turned, 1)

                def second(j, e):
                    pe.wait_ge(active_ready, j + 1)
                    for f in range(FC):
                        ins = pe.matmul(y_ps[:, 0, 0:DIM], active[:, f, :],
                                        w2[:, f, bass.ds(e, 1), :].rearrange("p a d -> p (a d)"),
                                        start=(f == 0), stop=(f == FC - 1))
                    ins.then_inc(y_done, 1)

                def expert_of(j):
                    return pe.value_load(expert[0:1, bass.ds(j, 1)], min_val=0, max_val=EXPERTS - 1)

                def tile(j, b, first, last):
                    e = expert_of(j)
                    e_before = None if first else expert_of(j - 1)
                    pe.wait_ge(turn_copied, j + 1)
                    if not first:
                        pe.wait_ge(hidden_kept, j)
                    for half in range(2):
                        for k in range(KC):
                            ins = pe.matmul(h_ps[:, half, :], x_in_t[:, b, k * P:(k + 1) * P],
                                            w1[:, k, bass.ds(e, 1), half * 512:(half + 1) * 512].rearrange("p a n -> p (a n)"),
                                            start=(k == 0), stop=(k == KC - 1))
                    ins.then_inc(hidden_done, 1)
                    if not last:
                        turn_input(j + 1, 1 - b)
                    if not first:
                        if not isinstance(j, int) or j > 1:
                            pe.wait_ge(y_kept, j - 1)
                        second(j - 1, e_before)
                    pe.wait_ge(hidden_kept, j + 1)
                    for f in range(FC):
                        ins = pe.transpose(ht_ps[:, f // 4, (f % 4) * P:(f % 4 + 1) * P], hidden[:, f * P:(f + 1) * P],
                                           ident[:, :])
                    ins.then_inc(hidden_turned, 1)

                pe.wait_ge(w1_in, 16 * EXPERTS)
                pe.wait_ge(w2_in, 16 * EXPERTS)
                turn_input(0, 0)
                over_tiles(pe, n_tiles, tile)
                e = expert_of(n_tiles - 1)
                pe.wait_ge(y_kept, n_tiles - 1)
                second(n_tiles - 1, e)

            @block.scalar
            def _(act):
                for t in range(TILES):
                    if t == 0:
                        act.wait_ge(h_parked, 16)
                        act.wait_ge(x_ready, GROUPS)
                    act.wait_ge(xt_done, t + 1)
                    act.activation(x_t[:, :, t * P:(t + 1) * P],
                                   y_ps[:, t % 2, 0:DIM].rearrange("p (k n) -> p k n", k=KC), ACT.Copy).then_inc(xt_copied, 1)
                if shared:
                    act.wait_ge(small_in, small_all)
                    act.activation(mix[:, :], mix[:, :], ACT.Exp, scale=-1.0).then_inc(mixed, 1)
                act.wait_ge(exp_asked, 1)
                act.activation(top[:, :, :], top[:, :, :], ACT.Exp).then_inc(exp_ready, 1)
                if shared:
                    act.wait_ge(mixed, 5)
                    for n in range(sh_uses):
                        f = n % SC
                        act.wait_ge(sh_done, n + 1)
                        if f == 0 and n:
                            act.wait_ge(sh_out, n)
                        act.activation(shared_act[:, f, :], h_ps[:, n % 2, :], ACT.Gelu, bias=sb1[:, f:f + 1],
                                       scale=sgate[:, f:f + 1]).then_inc(sh_active, 1)

                def turn_copy(j, b):
                    act.wait_ge(in_turned, j + 1)
                    act.activation(x_in_t[:, b, :], xt_ps[:, 0:DIM], ACT.Copy).then_inc(turn_copied, 1)

                def tile(j, b, first, last):
                    if not last:
                        turn_copy(j + 1, 1 - b)
                    e = act.value_load(expert[0:1, bass.ds(j, 1)], min_val=0, max_val=EXPERTS - 1)
                    act.wait_ge(hidden_turned, j + 1)
                    for f in range(FC):
                        act_args = dict(bias=b1[:, f, bass.ds(e, 1)])
                        if shared:
                            act_args["scale"] = gate[:, f, bass.ds(e, 1)]
                        ins = act.activation(active[:, f, :], ht_ps[:, f // 4, (f % 4) * P:(f % 4 + 1) * P],
                                             ACT.Gelu if shared else ACT.Relu, **act_args)
                    ins.then_inc(active_ready, 1)

                act.wait_ge(routed, 1)
                turn_copy(0, 0)
                over_tiles(act, n_tiles, tile)

            @block.vector
            def _(dve):
                link = Chain(dve, chain)
                for g in range(GROUPS):
                    tiles = range(g * SEQ_PER_GROUP, (g + 1) * SEQ_PER_GROUP)
                    layer_norm(dve, link, [x[:, t, :] for t in tiles], [h[:, t, :] for t in tiles], *scratch)
                    dve.sem_inc(x_ready, 1)
                dve.wait_ge(small_in, small_all)
                if shared:
                    dve.wait_ge(mixed, 1)
                    dve.tensor_scalar(mix[:, :], mix[:, :], 1.0, None, ALU.add).then_inc(mixed, 1)
                    dve.wait_ge(mixed, 2)
                    dve.reciprocal(mix[:, :], mix[:, :]).then_inc(mixed, 1)
                    dve.tensor_tensor(b1[:, :, :], b1[:, :, :], gate[:, :, :], ALU.mult).then_inc(mixed, 1)
                    dve.tensor_tensor(sb1[:, :], sb1[:, :], sgate[:, :], ALU.mult).then_inc(mixed, 1)
                    dve.wait_ge(mixed, 5)
                    link(dve.tensor_scalar(sb2[:, :], sb2[:, :], mix[:, 0:1], None, ALU.mult))
                dve.wait_ge(logits_done, 1)
                link(dve.tensor_tensor(logits[:, :, :], route_ps[:, 0:TILES * EXPERTS].rearrange("p (t e) -> p t e", e=EXPERTS),
                                       router_b[:, :].unsqueeze(1).to_broadcast([P, TILES, EXPERTS]), ALU.add))
                for t in range(TILES):
                    link(dve.max(top[:, t, :], logits[:, t, :]))
                for t in range(TILES):
                    link(dve.max_index(top_i[:, t, :], top[:, t, :], logits[:, t, :]))
                link(dve.tensor_copy(top_f[:, :, :], top_i[:, :, 0:choices]))
                link(dve.tensor_copy(total[:, :], top[:, :, 0]))
                dve.tensor_tensor(top[:, :, :], top[:, :, :], total[:, :].unsqueeze(2).to_broadcast([P, TILES, 8]),
                                  ALU.subtract).then_inc(exp_asked, 1)
                dve.wait_ge(constants, 6)
                for k in range(choices):
                    dve.tensor_tensor(onehot[:, k, :, :], top_f[:, :, k:k + 1].to_broadcast([P, TILES, EXPERTS]),
                                      expert_no[:, :].unsqueeze(1).to_broadcast([P, TILES, EXPERTS]),
                                      ALU.is_equal).then_inc(onehot_ready, 1)
                dve.wait_ge(exp_ready, 1)
                link(dve.tensor_reduce(total[:, :], top[:, :, 0:2] if shared else top[:, :, :], AXX, ALU.add))
                link(dve.reciprocal(total[:, :], total[:, :]))
                link(dve.tensor_tensor(weight[:, :, :], top[:, :, 0:choices],
                                       total[:, :].unsqueeze(2).to_broadcast([P, TILES, choices]), ALU.mult))
                width = pairs * EXPERTS
                dve.wait_ge(counted, 1)
                link(dve.tensor_copy(before[:, :, :, :].rearrange("p c t e -> p (c t e)"), h_ps[:, 0, 0:width]))
                link(dve.tensor_copy(counts[:, :, :].rearrange("p n e -> p (n e)"), h_ps[:, 1, 0:width]))
                for e in range(EXPERTS):
                    link(dve.tensor_tensor_scan(running[:, :, e], ones[:, 0:pairs], counts[:, :, e], 0.0, ALU.mult, ALU.add))
                link(dve.tensor_scalar(tiles_i[:, :], running[:, pairs - 1, :], float(P - 1), None, ALU.add))
                link(dve.tensor_scalar(tiles_i[:, :], tiles_i[:, :], 7, None, ALU.logical_shift_right))
                link(dve.tensor_copy(tiles_of[:, :], tiles_i[:, :]))
                link(dve.tensor_tensor_scan(last_tile[:, :], ones[:, 0:EXPERTS], tiles_of[:, :], 0.0, ALU.mult, ALU.add))
                link(dve.tensor_tensor(base[:, :], last_tile[:, :], tiles_of[:, :], ALU.subtract))
                link(dve.tensor_scalar(base[:, :], base[:, :], float(P), None, ALU.mult))
                at = before[:, :, :, :].rearrange("p c t e -> p (c t) e")
                link(dve.tensor_tensor(at, at, running[:, :, :], ALU.add))
                link(dve.tensor_tensor(at, at, counts[:, :, :], ALU.subtract))
                link(dve.tensor_tensor(at, at, base[:, :].unsqueeze(1).to_broadcast([P, pairs, EXPERTS]), ALU.add))
                link(dve.tensor_tensor(at, at, onehot[:, :, :, :].rearrange("p c t e -> p (c t) e"), ALU.mult))
                link(dve.tensor_reduce(slot_f[:, :], at, AXX, ALU.add))
                link(dve.tensor_copy(slot[:, :], slot_f[:, :]))
                link(dve.tensor_tensor(passed[:, :, :], last_tile[0:1, :].unsqueeze(1).to_broadcast([1, n_tiles, EXPERTS]),
                                       tile_no[:, :, :], ALU.is_le))
                link(dve.tensor_reduce(expert_f[:, :], passed[:, :, :], AXX, ALU.add))
                link(dve.tensor_scalar(expert[:, :], expert_f[:, :], float(EXPERTS - 1), None, ALU.min))
                dve.sem_inc(routed, 1)
                if shared:
                    dve.wait_ge(scattered, 16 * pairs)
                    for t in range(TILES):
                        dve.wait_ge(sh_out, t + 1)
                        dve.scalar_tensor_tensor(x[:, t, :], y_ps[:, t % 2, 0:DIM], mix[:, 0:1], sb2[:, :],
                                                 ALU.mult, ALU.add).then_inc(sh_kept, 1)

                def keep_y(j, b):
                    e = dve.value_load(expert[0:1, bass.ds(j, 1)], min_val=0, max_val=EXPERTS - 1)
                    dve.wait_ge(y_done, j + 1)
                    if not isinstance(j, int) or j >= 2:
                        dve.wait_ge(y_stored[b], (j // 2) * 16 if isinstance(j, int) else j * 8 - (8 if b else 0))
                    dve.tensor_tensor(y_out[:, b, :], y_ps[:, 0, 0:DIM],
                                      b2[:, bass.ds(e, 1), :].rearrange("p a d -> p (a d)"), ALU.add).then_inc(y_kept, 1)

                def tile(j, b, first, last):
                    dve.wait_ge(hidden_done, j + 1)
                    if not first:
                        dve.wait_ge(hidden_turned, j)
                    dve.tensor_copy(hidden, h_ps[:, :, :].rearrange("p a n -> p (a n)")).then_inc(hidden_kept, 1)
                    if not first:
                        keep_y(j - 1, 1 - b)

                over_tiles(dve, n_tiles, tile)
                keep_y(n_tiles - 1, (n_tiles - 1) % 2)

                for r in range(rounds):
                    dve.wait_ge(gathered[r], 16 * tiles_back * choices)
                    for i in range(tiles_back):
                        t = r * tiles_back + i
                        if shared:
                            for k in range(choices):
                                link(dve.scalar_tensor_tensor(x[:, t, :], back[:, i * choices + k, :], weight[:, t, k:k + 1],
                                                              x[:, t, :], ALU.mult, ALU.add))
                        else:
                            link(dve.tensor_scalar(x[:, t, :], back[:, i, :], weight[:, t, 0:1], None, ALU.mult))
                    dve.sem_inc(combined, 1)
                if shared:
                    for g in range(GROUPS):
                        tiles = [x[:, t, :] for t in range(g * SEQ_PER_GROUP, (g + 1) * SEQ_PER_GROUP)]
                        layer_norm(dve, link, tiles, tiles, *scratch)
                        for v in tiles:
                            link(dve.tensor_tensor(v, v, ln_g[:, :], ALU.mult))
                            link(dve.tensor_tensor(v, v, ln_b[:, :], ALU.add))
                dve.wait_ge(h_back, 16)
                link(dve.tensor_tensor(h[:, :, :], h[:, :, :], x[:, :, :], ALU.add))


def build(nc, x, out, stages=9):
    with ExitStack() as ctx:
        h = ctx.enter_context(nc.sbuf_tensor("h", [P, TILES, DIM], F32))
        ident = make_constants(nc, ctx)
        bc_dram = nc.dram_tensor("bc_rows", (GROUPS, 2 * STATE, GT), F32, kind="Internal").ap()
        embed(nc, h, ident, x["x"], [x["emb_head"], x["emb_tail_0"], x["emb_tail_1"]], x["emb_proj"])
        if stages >= 2:
            mamba(nc, h, ident, {k[len("mamba_"):]: v for k, v in x.items() if k.startswith("mamba_")}, bc_dram)
        parked = nc.dram_tensor("h_parked", (TOKENS, DIM), F32, kind="Internal").ap()

        def expert_rows(name, choices):
            return nc.dram_tensor(name, (most_tiles(choices) * P, DIM), F32, kind="Internal").ap()

        def part(prefix):
            return {k[len(prefix):]: v for k, v in x.items() if k.startswith(prefix)}

        if stages >= 3:
            moe(nc, h, ident, part("moe0_"), 2, expert_rows("slots0", 2), expert_rows("results0", 2), parked, "moe0")
        if stages >= 4:
            attention(nc, h, ident, part("att_"))
        if stages >= 5:
            moe(nc, h, ident, part("moe1_"), 1, expert_rows("slots1", 1), expert_rows("results1", 1), parked, "moe1")
        stored = ctx.enter_context(nc.semaphore("h_stored"))
        with nc.Block() as block:
            @block.sync
            def _(sp):
                sp.dma_start(out.rearrange("s p d -> p s d"), h[:, :, :]).then_inc(stored, 16)
                sp.wait_ge(stored, 16)


def rope_tables(rows, scale):
    d = np.arange(rows) % HEAD_DIM
    inv_freq = (np.float32(1) / np.float32(10000) ** ((d // 2 * 2).astype(np.float32) / np.float32(HEAD_DIM))).astype(np.float32)
    angle = inv_freq[:, None] * np.arange(P, dtype=np.float32)
    sign = np.where(d % 2 == 0, np.float32(-1), np.float32(1))[:, None]
    return (np.stack([np.cos(angle), sign * np.sin(angle)], 1) * np.float32(scale)).astype(np.float32)


def head_spread():
    pad_q, pad_k = np.zeros((P, 2, P), np.float32), np.zeros((KV_HEADS * HEAD_DIM, KV_HEADS, P), np.float32)
    for r in range(HEADS // KV_HEADS):
        for d in range(HEAD_DIM):
            for half in range(2):
                pad_q[(half * 4 + r) * HEAD_DIM + d, half, 32 * r + d] = 1
            for c in range(KV_HEADS):
                pad_k[c * HEAD_DIM + d, c, 32 * r + d] = 1
    return pad_q, pad_k


def host_layout(inputs):
    a = {k: np.asarray(v) for k, v in inputs.items()}

    def rows(m):
        return m.reshape(m.shape[0] // P, P, *m.shape[1:]).swapaxes(0, 1)

    t0, m0, f0, t1, f1 = "L0_tok_", "L0_attn_", "L0_ffn_", "L1_attn_", "L1_ffn_"
    swapped = np.arange(DIM) ^ 1
    kv = a[t1 + "Wkvb"].reshape(-1, KV_HEADS * HEAD_DIM, 2)
    pad_q, pad_k = head_spread()
    return {
        "x": a["x"].T,
        "emb_head": a[t0 + "head_weight"].T,
        "emb_tail_0": a[t0 + "tail_weight_0"].T,
        "emb_tail_1": a[t0 + "tail_weight_1"].T,
        "emb_proj": np.concatenate([a[t0 + "head_weight_proj"].T, a[t0 + "tail_weight_proj_0"].T,
                                    a[t0 + "tail_weight_proj_1"].T]),
        "mamba_ln_gamma": rows(a[m0 + "ln_gamma"]),
        "mamba_ln_beta": rows(a[m0 + "ln_beta"]),
        "mamba_W_in": rows(a[m0 + "W_in"].T),
        "mamba_conv_w": rows(a[m0 + "conv_w"][:, 0, :]),
        "mamba_conv_b": rows(a[m0 + "conv_b"]),
        "mamba_W_xproj": rows(a[m0 + "W_xproj"].T),
        "mamba_W_dt": a[m0 + "W_dt"].T,
        "mamba_b_dt": rows(a[m0 + "b_dt"]),
        "mamba_A_log": rows(a[m0 + "A_log"]),
        "mamba_D_param": rows(a[m0 + "D_param"]),
        "mamba_W_out": rows(a[m0 + "W_out"].T),
        "moe0_router_w": rows(a[f0 + "router_w"]),
        "moe0_router_b": a[f0 + "router_b"],
        "moe0_w1": rows(a[f0 + "w1"].swapaxes(0, 1)),
        "moe0_b1": rows(a[f0 + "b1"].T),
        "moe0_gate": rows(a[f0 + "gate"].T),
        "moe0_w2": rows(a[f0 + "w2"].swapaxes(0, 1)),
        "moe0_b2": a[f0 + "b2"].reshape(-1),
        "moe0_sw1": rows(a[f0 + "sw1"]),
        "moe0_sb1": rows(a[f0 + "sb1"]),
        "moe0_sgate": rows(a[f0 + "sgate"]),
        "moe0_sw2": rows(a[f0 + "sw2"]),
        "moe0_sb2": a[f0 + "sb2"],
        "moe0_shared_weight": a[f0 + "shared_weight"].reshape(1),
        "moe0_ln_g": a[f0 + "ln_g"],
        "moe0_ln_b": a[f0 + "ln_b"],
        "att_Wqa": rows(a[t1 + "Wqa"]),
        "att_Wkva": rows(a[t1 + "Wkva"]),
        "att_Wqb": np.stack([a[t1 + "Wqb"], a[t1 + "Wqb"][:, swapped]], 1),
        "att_Wk": np.stack([kv[:, :, 0], kv[:, swapped[:KV_HEADS * HEAD_DIM], 0]], 1),
        "att_Wv": kv[:, :, 1],
        "att_Wout": rows(a[t1 + "Wout"]),
        "att_bout": a[t1 + "bout"],
        "att_rope_q": rope_tables(P, float(HEAD_DIM) ** -0.5),
        "att_rope_k": rope_tables(KV_HEADS * HEAD_DIM, 1.0),
        "att_pad_q": pad_q,
        "att_pad_k": pad_k,
        "moe1_router_w": rows(a[f1 + "w_gate"]),
        "moe1_router_b": a[f1 + "b_gate"],
        "moe1_w1": rows(a[f1 + "W1"].swapaxes(0, 1)),
        "moe1_b1": rows(a[f1 + "b1"].T),
        "moe1_w2": rows(a[f1 + "W2"].swapaxes(0, 1)),
        "moe1_b2": a[f1 + "b2"].reshape(-1),
    }


def program(nc, arrays, stages=9):
    args = {}
    for name, a in arrays.items():
        args[name[3:]] = nc.dram_tensor(name, a.shape, mybir.dt.from_np(a.dtype), kind="ExternalInput").ap()
    out = nc.dram_tensor("out", (TILES, P, DIM), F32, kind="ExternalOutput").ap()
    build(nc, args, out, stages)


def kernel(**inputs):
    import concourse.bacc as bacc
    from concourse.bass_utils import run_bass_kernel_spmd

    arrays = {"in_" + k: np.ascontiguousarray(v) for k, v in host_layout(inputs).items()}
    nc = bacc.Bacc("TRN2", target_bir_lowering=False, num_devices=1)
    program(nc, arrays)
    result = run_bass_kernel_spmd(nc, [arrays], core_ids=[0])
    return result.results[0]["out"]
```

```python
from contextlib import ExitStack

import numpy as np

import concourse.bass as bass
from concourse import mybir

F32 = mybir.dt.float32
BF16 = mybir.dt.bfloat16
I32 = mybir.dt.int32
U32 = mybir.dt.uint32
ALU = mybir.AluOpType
ACT = mybir.ActivationFunctionType
AXX = mybir.AxisListType.X

P = 128
TILES = 16
TOKENS = TILES * P
DIM = 256
KC = DIM // P
SEQ_PER_GROUP = 4
GROUPS = TILES // SEQ_PER_GROUP
GT = SEQ_PER_GROUP * P
EPS = 1e-5

CUTOFFS = (0, 5000, 20000, 50000)
EMB_WIDTHS = (256, 64, 16)
EMB_STARTS = (0, 256, 320)
EMB_DIM = 336
EMB_CHUNKS = ((0, 128), (128, 128), (256, 80))

INNER = 512
DC = INNER // P
STATE = 16
TAPS = 4
DT_RANK = 32
SQ = 4
NQ = STATE // SQ

EXPERTS = 8
FF = 1024
FC = FF // P
SHARED_FF = 512
SC = SHARED_FF // P

HEADS = 16
KV_HEADS = 4
HEAD_DIM = 16


def nth(i, per, k=0):
    return i * per + k + 1


class Chain:

    def __init__(self, eng, sem, first=0):
        self.eng, self.sem, self.first, self.n = eng, sem, first, 0

    def __call__(self, ins):
        ins.then_inc(self.sem, 1)
        self.n += 1
        self.eng.wait_ge(self.sem, self.first + self.n)


class Memory:

    def __init__(self, nc, ctx, stage):
        self.nc, self.ctx, self.stage = nc, ctx, stage

    def sb(self, name, shape, dt=F32):
        return self.ctx.enter_context(self.nc.sbuf_tensor(f"{self.stage}_{name}", shape, dt))

    def ps(self, name, shape, dt=F32):
        return self.ctx.enter_context(self.nc.psum_tensor(f"{self.stage}_{name}", shape, dt))

    def sem(self, name):
        return self.ctx.enter_context(self.nc.semaphore(f"{self.stage}_{name}"))


RSQRT_LINKS = 12


def rsqrt_newton(dve, link, out, var, half):
    link(dve.tensor_scalar(var, var, EPS, None, ALU.add))
    link(dve.tensor_scalar(half.bitcast(I32), var.bitcast(I32), 1, None, ALU.logical_shift_right))
    link(dve.tensor_scalar(out.bitcast(I32), half.bitcast(I32), -1.0, float(0x5F3759DF), ALU.mult, ALU.add))
    for _ in range(3):
        link(dve.scalar_tensor_tensor(half, out, -0.5, out, ALU.mult, ALU.mult))
        link(dve.tensor_tensor(half, half, var, ALU.mult))
        link(dve.scalar_tensor_tensor(out, half, 1.5, out, ALU.add, ALU.mult))


def norm_links(n):
    return 2 * n + 6 + RSQRT_LINKS


def layer_norm(dve, link, outs, ins, stats, mean_var, rstd, half):
    n, width = len(ins), ins[0].shape[-1]
    mean, var, even_odd = mean_var[:, 0, 0:n], mean_var[:, 1, 0:n], mean_var[:, 2, 0:n]
    for i, x in enumerate(ins):
        link(dve.bn_stats(stats[:, i, :], x))
    link(dve.tensor_tensor(mean, stats[:, 0:n, 1], stats[:, 0:n, 4], ALU.add))
    link(dve.tensor_scalar(mean, mean, 0.5, None, ALU.mult))
    link(dve.tensor_tensor(even_odd, stats[:, 0:n, 1], stats[:, 0:n, 4], ALU.subtract))
    link(dve.scalar_tensor_tensor(even_odd, even_odd, 0.25, even_odd, ALU.mult, ALU.mult))
    link(dve.tensor_tensor(var, stats[:, 0:n, 2], stats[:, 0:n, 5], ALU.add))
    link(dve.scalar_tensor_tensor(var, var, 1.0 / width, even_odd, ALU.mult, ALU.add))
    rsqrt_newton(dve, link, rstd[:, 0:n], var, half[:, 0:n])
    for i, x in enumerate(ins):
        link(dve.tensor_scalar(outs[i], x, mean[:, i:i + 1], rstd[:, i:i + 1], ALU.subtract, ALU.mult))


def norm_scratch(mem, n):
    return (mem.sb("stats", [P, n, 6]), mem.sb("mean_var", [P, 3, n]), mem.sb("rstd", [P, n]), mem.sb("half", [P, n]))


def make_constants(nc, ctx):
    mem = Memory(nc, ctx, "const")
    ident = mem.sb("ident", [P, P])
    made = mem.sem("made")
    with nc.Block() as block:
        @block.gpsimd
        def _(pool):
            pool.memset(ident[:, :], 0.0).then_inc(made, 1)
            pool.wait_ge(made, 1)
            pool.affine_select(out=ident[:, :], in_=ident[:, :], compare_op=ALU.not_equal, fill=1.0,
                               base=0, pattern=[[-1, P]], channel_multiplier=1).then_inc(made, 1)
            pool.wait_ge(made, 2)
    return ident


def embed(nc, h, ident, token_ids, tables, projections):
    with ExitStack() as ctx:
        mem = Memory(nc, ctx, "emb")
        ids = mem.sb("ids", [P, TILES], I32)
        rows = mem.sb("rows", [P, 3, TILES], I32)
        emb = mem.sb("emb", [P, TILES, EMB_DIM])
        proj = mem.sb("proj", [P, 3, DIM])
        emb_t = mem.sb("emb_t", [P, 2, 3, P])
        t_ps = mem.ps("t_ps", [P, 2, 512])
        h_ps = mem.ps("h_ps", [P, 2, 512])
        ids_in, proj_in = mem.sem("ids_in"), mem.sem("proj_in")
        cleared, rows_ready = mem.sem("cleared"), mem.sem("rows_ready")
        gathered = [mem.sem(f"gathered{g}") for g in range(GROUPS)]
        transposed, copied, projected, stored = (mem.sem(n) for n in ("transposed", "copied", "projected", "stored"))

        with nc.Block() as block:
            @block.sync
            def _(sp):
                sp.dma_start(ids[:, :], token_ids).then_inc(ids_in, 16)
                for c, (a, n) in enumerate(EMB_CHUNKS):
                    sp.dma_start(proj[0:n, c, :], projections[a:a + n, :]).then_inc(proj_in, 16)

            @block.vector
            def _(dve):
                dve.memset(emb[:, :, :], 0.0).then_inc(cleared, 1)
                dve.wait_ge(ids_in, 16)
                for i in range(3):
                    dve.tensor_scalar(rows[:, i, :], ids[:, :], float(-CUTOFFS[i]), None, ALU.add).then_inc(rows_ready, 1)
                for s in range(TILES):
                    dve.wait_ge(projected, s + 1)
                    dve.tensor_scalar(h[:, s, :], h_ps[:, s % 2, 0:DIM], 16.0, None, ALU.mult).then_inc(stored, 1)

            @block.gpsimd
            def _(pool):
                pool.wait_ge(cleared, 1)
                pool.wait_ge(rows_ready, 3)
                for s in range(TILES):
                    for i in range(3):
                        a, n = EMB_STARTS[i], EMB_WIDTHS[i]
                        pool.indirect_dma_start(
                            emb[:, s, a:a + n], None, tables[i],
                            bass.IndirectOffsetOnAxis(rows[:, i, s:s + 1].bitcast(U32), 0),
                            bounds_check=CUTOFFS[i + 1] - CUTOFFS[i] - 1, oob_is_err=False,
                        ).then_inc(gathered[s // SEQ_PER_GROUP], 16)

            @block.tensor
            def _(pe):
                for s in range(TILES + 1):
                    if s < TILES:
                        if s % SEQ_PER_GROUP == 0:
                            pe.wait_ge(gathered[s // SEQ_PER_GROUP], 16 * 3 * SEQ_PER_GROUP)
                        if s >= 2:
                            pe.wait_ge(copied, 2 * (s - 1))
                        for c, (a, n) in enumerate(EMB_CHUNKS):
                            ins = pe.transpose(t_ps[0:n, s % 2, c * P:(c + 1) * P], emb[:, s, a:a + n], ident[:, :])
                        ins.then_inc(transposed, 1)
                    if s >= 1:
                        v = s - 1
                        if v == 0:
                            pe.wait_ge(proj_in, 48)
                        if v >= 2:
                            pe.wait_ge(stored, v - 1)
                        pe.wait_ge(copied, 2 * v + 2)
                        for c, (a, n) in enumerate(EMB_CHUNKS):
                            ins = pe.matmul(h_ps[:, v % 2, 0:DIM], emb_t[0:n, v % 2, c, :], proj[0:n, c, :],
                                            start=(c == 0), stop=(c == 2))
                        ins.then_inc(projected, 1)

            @block.scalar
            def _(act):
                for s in range(TILES):
                    act.wait_ge(transposed, s + 1)
                    if s >= 2:
                        act.wait_ge(projected, s - 1)
                    act.activation(emb_t[:, s % 2, 0:2, :], t_ps[:, s % 2, 0:2 * P], ACT.Copy).then_inc(copied, 1)
                    act.activation(emb_t[0:80, s % 2, 2, :], t_ps[0:80, s % 2, 2 * P:3 * P], ACT.Copy).then_inc(copied, 1)


def mamba(nc, h, ident, w, bc_dram):
    with ExitStack() as ctx:
        mem = Memory(nc, ctx, "mam")
        S = SEQ_PER_GROUP
        w_in = mem.sb("w_in", [P, KC, 2 * INNER])
        w_x = mem.sb("w_x", [P, DC, DT_RANK + 2 * STATE])
        w_dt = mem.sb("w_dt", [DT_RANK, INNER])
        w_out = mem.sb("w_out", [P, DC, DIM])
        gamma, beta = mem.sb("gamma", [P, KC]), mem.sb("beta", [P, KC])
        conv_w, conv_b = mem.sb("conv_w", [P, DC, TAPS]), mem.sb("conv_b", [P, DC])
        b_dt, skip = mem.sb("b_dt", [P, DC]), mem.sb("skip", [P, DC])
        skip_diag = mem.sb("skip_diag", [P, DC, P])
        a_log, decay = mem.sb("a_log", [P, DC, STATE]), mem.sb("decay", [P, DC, STATE])

        xa = mem.sb("xa", [P, S, DIM])
        xn = mem.sb("xn", [P, S, DIM])
        xn_t = mem.sb("xn_t", [P, KC, GT])
        conv = mem.sb("conv", [P, DC, GT])
        x_proj = mem.sb("x_proj", [DT_RANK + 2 * STATE, GT])
        soft = mem.sb("soft", [P, 2, GT])
        delta = mem.sb("delta", [P, DC, GT])
        delta_u = mem.sb("delta_u", [P, DC, GT])
        u = mem.sb("u", [P, DC, GT])
        silu_z = mem.sb("silu_z", [P, DC, GT])
        bc = mem.sb("bc", [P, 2, 2, SQ, GT])
        da = mem.sb("da", [P, 2, SQ, GT])
        hs = mem.sb("hs", [P, 2, SQ, GT])
        y = mem.sb("y", [P, DC, GT])
        scratch = norm_scratch(mem, S)

        bank = mem.ps("bank", [P, 2, 512])
        wide = mem.ps("wide", [P, 2, 512])
        y_ps = mem.ps("y_ps", [P, DC, 512])

        weights_in = mem.sem("weights_in")
        decay_ready = mem.sem("decay_ready")
        pre_chain, scan_chain, out_chain = (
            mem.sem(n) for n in ("pre_chain", "scan_chain", "out_chain"))
        xn_ready, xn_transposed, xn_t_ready = mem.sem("xn_ready"), mem.sem("xn_transposed"), mem.sem("xn_t_ready")
        xz_ready = mem.sem("xz_ready")
        bank_free = [mem.sem(f"bank_free{b}") for b in range(2)]
        wide_free = mem.sem("wide_free")
        tap_ready, conv_ready, u_ready, z_ready = (mem.sem(n) for n in ("tap_ready", "conv_ready", "u_ready", "z_ready"))
        proj_ready, proj_copied = mem.sem("proj_ready"), mem.sem("proj_copied")
        bc_written, bc_in, bc_free = mem.sem("bc_written"), [mem.sem("bc_in0"), mem.sem("bc_in1")], mem.sem("bc_free")
        pre_delta, log_ready = mem.sem("pre_delta"), mem.sem("log_ready")
        act_chain = mem.sem("act_chain")
        delta_ready = mem.sem("delta_ready")
        da_ready, scanned, hc_ready, summed = (mem.sem(n) for n in ("da_ready", "scanned", "hc_ready", "summed"))
        y_free, y_ready, out_ready = mem.sem("y_free"), mem.sem("y_ready"), mem.sem("out_ready")
        da_cleared, skip_ready = mem.sem("da_cleared"), mem.sem("skip_ready")

        UNITS = NQ * DC
        BANK_USES = (7, 6)
        PRE_LINKS = 2 * norm_links(S) + S + DC * (TAPS - 2) + DC
        ACT_LINKS = 3 * DC

        def by_seq(v):
            return v.rearrange("p (s t) -> p s t", t=P)

        def h_tiles(g):
            return [h[:, bass.ds(g * S + s, 1), :].rearrange("p a d -> p (a d)") for s in range(S)]

        def run_groups(eng, unit, prepare, beside, tail):
            def group(g, first, last):
                for n in range(UNITS):
                    unit(g, n)
                    if not first and n in tail:
                        tail[n](g - 1)
                    for step in beside.get(n, ()):
                        step(g)
                    if not last:
                        for step in prepare.get(n, ()):
                            step(g + 1)

            for n in sorted(prepare):
                for step in prepare[n]:
                    step(0)
            group(0, True, False)
            with eng.Fori(1, GROUPS - 1) as g:
                group(g, False, False)
            group(GROUPS - 1, False, True)
            for n in sorted(tail):
                tail[n](GROUPS - 1)

        with nc.Block() as block:
            @block.sync
            def _(sp):
                for dst, src in ((w_in[:, :, :], w["W_in"]), (w_x[:, :, :], w["W_xproj"]), (w_dt[:, :], w["W_dt"]),
                                 (w_out[:, :, :], w["W_out"]), (gamma[:, :], w["ln_gamma"]), (beta[:, :], w["ln_beta"]),
                                 (conv_w[:, :, :], w["conv_w"]), (conv_b[:, :], w["conv_b"]), (b_dt[:, :], w["b_dt"]),
                                 (skip[:, :], w["D_param"]), (a_log[:, :, :], w["A_log"])):
                    sp.dma_start(dst, src).then_inc(weights_in, 16)
                sp.sem_inc(bc_free, 2)
                with sp.Fori(0, GROUPS) as g:
                    sp.wait_ge(bc_written, 16 * g + 16)
                    for q in range(NQ):
                        sp.wait_ge(bc_free, nth(g, NQ, q))
                        for k in range(2):
                            row = k * STATE + q * SQ
                            src = bc_dram[bass.ds(g, 1), row:row + SQ, :].rearrange("g r t -> (g r t)")
                            sp.dma_start(bc[:, q % 2, k, :, :].rearrange("p r t -> p (r t)"),
                                         src.partition_broadcast(P)).then_inc(bc_in[q % 2], 16)

            @block.gpsimd
            def _(pool):
                with pool.Fori(0, GROUPS) as g:
                    pool.wait_ge(proj_copied, nth(g, 1))
                    pool.dma_start(bc_dram[bass.ds(g, 1), :, :].rearrange("g r t -> (g r) t"),
                                   x_proj[DT_RANK:, :]).then_inc(bc_written, 16)

            @block.tensor
            def _(pe):
                pe.wait_ge(weights_in, 16 * 11)

                def take(g, b, use):
                    pe.wait_ge(bank_free[b], nth(g, BANK_USES[b], use))

                def transpose_x(g):
                    pe.wait_ge(xn_ready, nth(g, 1))
                    pe.wait_ge(wide_free, 1 if isinstance(g, int) and g == 0 else 2 * g)
                    for k in range(KC):
                        for s in range(S):
                            ins = pe.transpose(wide[:, k, s * P:(s + 1) * P], xn[:, s, k * P:(k + 1) * P], ident[:, :])
                    ins.then_inc(xn_transposed, 1)

                def in_product(c):
                    def step(g):
                        if c == 0:
                            pe.wait_ge(xn_t_ready, nth(g, KC, KC - 1))
                        take(g, c % 2, c // 2 if c < DC else 5 - c % 2 + (c - DC) // 2)
                        for k in range(KC):
                            ins = pe.matmul(bank[:, c % 2, :], w_in[:, k, c * P:(c + 1) * P], xn_t[:, k, :],
                                            start=(k == 0), stop=(k == KC - 1))
                        ins.then_inc(xz_ready, 1)
                    return step

                def bc_dt_product(g):
                    pe.wait_ge(u_ready, nth(g, DC, DC - 1))
                    take(g, 0, 2)
                    for c in range(DC):
                        ins = pe.matmul(bank[0:DT_RANK + 2 * STATE, 0, :], w_x[:, c, :], u[:, c, :],
                                        start=(c == 0), stop=(c == DC - 1))
                    ins.then_inc(proj_ready, 1)

                def delta_product(c):
                    def step(g):
                        if c == 0:
                            pe.wait_ge(proj_copied, nth(g, 1))
                        take(g, c % 2, 3 - c % 2 + c // 2)
                        pe.matmul(bank[:, c % 2, :], w_dt[:, c * P:(c + 1) * P], x_proj[0:DT_RANK, :],
                                  start=True, stop=True).then_inc(pre_delta, 1)
                    return step

                def unit(g, n):
                    q, c = divmod(n, DC)
                    if q == 0:
                        pe.wait_ge(y_free, nth(g, DC, c))
                    pe.wait_ge(hc_ready, nth(g, UNITS, n))
                    if q == 0:
                        pe.matmul(y_ps[:, c, :], skip_diag[:, c, :], u[:, c, :], start=True, stop=False)
                    for i in range(SQ):
                        ins = pe.matmul(y_ps[:, c, :], ident[:, :], hs[:, n % 2, i, :],
                                        start=False, stop=(q == NQ - 1 and i == SQ - 1))
                    ins.then_inc(summed, 1)

                def out_product(g):
                    pe.wait_ge(y_ready, nth(g, DC, DC - 1))
                    pe.wait_ge(wide_free, 2 * g + 2 if isinstance(g, int) and g == GROUPS - 1 else 2 * g + 3)
                    for s in range(S):
                        for c in range(DC):
                            ins = pe.matmul(wide[:, s // 2, (s % 2) * DIM:(s % 2 + 1) * DIM],
                                            y[:, c, s * P:(s + 1) * P], w_out[:, c, :],
                                            start=(c == 0), stop=(c == DC - 1))
                    ins.then_inc(out_ready, 1)

                pe.wait_ge(skip_ready, DC)
                run_groups(pe, unit,
                           {2: [transpose_x], 4: [in_product(0), in_product(1)], 5: [in_product(2)], 6: [in_product(3)],
                            10: [bc_dt_product], 11: [delta_product(0), delta_product(1)],
                            12: [delta_product(2), delta_product(3)]},
                           {0: [in_product(4), in_product(5)], 2: [in_product(6), in_product(7)]},
                           {0: out_product})

            @block.scalar
            def _(act):
                act.wait_ge(weights_in, 16 * 11)
                act.activation(decay[:, :, :], a_log[:, :, :], ACT.Exp).then_inc(decay_ready, 1)

                def keep_x(g):
                    act.wait_ge(xn_transposed, nth(g, 1))
                    for k in range(KC):
                        act.activation(xn_t[:, k, :], wide[:, k, :], ACT.Identity, bias=beta[:, k:k + 1],
                                       scale=gamma[:, k:k + 1]).then_inc(xn_t_ready, 1)
                    act.wait_ge(xn_t_ready, nth(g, KC, KC - 1))
                    act.sem_inc(wide_free, 1)

                def last_tap(c):
                    def step(g):
                        act.wait_ge(xz_ready, nth(g, 2 * DC, c))
                        act.activation(conv[:, c, :], bank[:, c % 2, :], ACT.Identity, bias=conv_b[:, c:c + 1],
                                       scale=conv_w[:, c, TAPS - 1:TAPS]).then_inc(tap_ready, 1)
                    return step

                def silu_of_z(g):
                    for c in range(DC):
                        act.wait_ge(xz_ready, nth(g, 2 * DC, DC + c))
                        act.activation(silu_z[:, c, :], bank[:, c % 2, :], ACT.Silu).then_inc(z_ready, 1)
                        act.wait_ge(z_ready, nth(g, DC, c))
                        act.sem_inc(bank_free[c % 2], 1)
                    act.preload_act_table_set("natural_log_exp_and_others")

                def silu_of_x(g):
                    act.wait_ge(conv_ready, nth(g, DC, DC - 1))
                    for c in range(DC):
                        act.activation(u[:, c, :], conv[:, c, :], ACT.Silu).then_inc(u_ready, 1)
                    act.preload_act_table_set("natural_log_exp_and_others")

                def keep_proj(g):
                    act.wait_ge(proj_ready, nth(g, 1))
                    if not isinstance(g, int) or g:
                        act.wait_ge(bc_written, 16 * g)
                    act.activation(x_proj[:, :], bank[0:DT_RANK + 2 * STATE, 0, :], ACT.Copy)\
                       .then_inc(proj_copied, 1)
                    act.wait_ge(proj_copied, nth(g, 1))
                    act.sem_inc(bank_free[0], 1)

                def softplus_terms(chunks):
                    def step(g):
                        for c in chunks:
                            link = Chain(act, act_chain, g * ACT_LINKS + 3 * c)
                            if not isinstance(g, int) or g:
                                act.wait_ge(da_ready, g * UNITS - (DC - 1) + c)
                            act.wait_ge(pre_delta, nth(g, DC, c))
                            if c >= 2:
                                act.wait_ge(delta_ready, nth(g, DC, c - 2))
                            act.activation(delta[:, c, :], bank[:, c % 2, :], ACT.Relu, bias=b_dt[:, c:c + 1])
                            link(act.activation(soft[:, c % 2, :], bank[:, c % 2, :], ACT.Abs, bias=b_dt[:, c:c + 1]))
                            act.sem_inc(bank_free[c % 2], 1)
                            link(act.activation(soft[:, c % 2, :], soft[:, c % 2, :], ACT.Exp, scale=-1.0))
                            link(act.activation(soft[:, c % 2, :], soft[:, c % 2, :], ACT.Ln, bias=1.0))
                            act.sem_inc(log_ready, 1)
                    return step

                def unit(g, n):
                    q, c = divmod(n, DC)
                    if q == 0:
                        act.wait_ge(delta_ready, nth(g, DC, c))
                    act.wait_ge(scanned, nth(g, UNITS, n))
                    for i in range(SQ):
                        ins = act.activation(by_seq(da[:, n % 2, i, :])[:, :, 1:], by_seq(delta[:, c, :])[:, :, 1:],
                                             ACT.Exp, scale=decay[:, c, q * SQ + i:q * SQ + i + 1])
                    ins.then_inc(da_ready, 1)

                run_groups(act, unit,
                           {5: [keep_x], 6: [last_tap(0)], 7: [last_tap(1)], 8: [last_tap(2)], 9: [last_tap(3)],
                            10: [silu_of_x], 12: [keep_proj], 13: [softplus_terms((0, 1))],
                            15: [softplus_terms((2, 3))]},
                           {4: [silu_of_z]}, {})

            @block.vector
            def _(dve):
                dve.memset(da[:, :, :, :], 0.0).then_inc(da_cleared, 1)
                dve.wait_ge(decay_ready, 1)
                dve.tensor_scalar(decay[:, :, :], decay[:, :, :], -1.0, None, ALU.mult).then_inc(decay_ready, 1)
                dve.wait_ge(decay_ready, 2)
                dve.wait_ge(da_cleared, 1)
                for c in range(DC):
                    dve.tensor_scalar(skip_diag[:, c, :], ident[:, :], skip[:, c:c + 1], None, ALU.mult).then_inc(skip_ready, 1)
                for b in range(2):
                    dve.sem_inc(bank_free[b], 1)
                dve.sem_inc(wide_free, 1)
                dve.sem_inc(y_free, DC)
                dve.sem_inc(scanned, 2)

                def norm_h(g):
                    link = Chain(dve, pre_chain, g * PRE_LINKS)
                    layer_norm(dve, link, [xa[:, s, :] for s in range(S)], h_tiles(g), *scratch)

                def norm_x(g):
                    link = Chain(dve, pre_chain, g * PRE_LINKS + norm_links(S))
                    layer_norm(dve, link, [xn[:, s, :] for s in range(S)], [xa[:, s, :] for s in range(S)], *scratch)
                    dve.sem_inc(xn_ready, 1)
                    for s, h_s in enumerate(h_tiles(g)):
                        link(dve.tensor_tensor(h_s, h_s, xa[:, s, :], ALU.add))

                def convolve(c):
                    def step(g):
                        link = Chain(dve, pre_chain, g * PRE_LINKS + 2 * norm_links(S) + S + c * (TAPS - 2))
                        dve.wait_ge(tap_ready, nth(g, DC, c))
                        x_c, o_c = by_seq(bank[:, c % 2, :]), by_seq(conv[:, c, :])
                        for k in range(1, TAPS):
                            ins = dve.scalar_tensor_tensor(o_c[:, :, k:], x_c[:, :, :P - k],
                                                           conv_w[:, c, TAPS - 1 - k:TAPS - k],
                                                           o_c[:, :, k:], ALU.mult, ALU.add)
                            if k < TAPS - 1:
                                link(ins)
                        ins.then_inc(conv_ready, 1)
                        dve.wait_ge(conv_ready, nth(g, DC, c))
                        dve.sem_inc(bank_free[c % 2], 1)
                    return step

                def softplus(chunks):
                    def step(g):
                        for c in chunks:
                            link = Chain(dve, pre_chain, (g + 1) * PRE_LINKS - DC + c)
                            dve.wait_ge(log_ready, nth(g, DC, c))
                            dve.tensor_tensor(delta[:, c, :], delta[:, c, :], soft[:, c % 2, :], ALU.add)\
                               .then_inc(delta_ready, 1)
                            dve.wait_ge(delta_ready, nth(g, DC, c))
                            link(dve.tensor_tensor(delta_u[:, c, :], delta[:, c, :], u[:, c, :], ALU.mult))
                    return step

                def unit(g, n):
                    q, c = divmod(n, DC)
                    link = Chain(dve, scan_chain, g * UNITS + n)
                    if c == 0:
                        dve.wait_ge(bc_in[q % 2], 32 * (g * (NQ // 2) + q // 2 + 1))
                    if n >= 2:
                        dve.wait_ge(summed, nth(g, UNITS, n - 2))
                    elif not isinstance(g, int) or g:
                        dve.wait_ge(summed, g * UNITS + n - 1)
                    x_n = hs[:, n % 2, :, :]
                    link(dve.tensor_tensor(x_n, delta_u[:, c, :].unsqueeze(1).to_broadcast([P, SQ, GT]),
                                           bc[:, q % 2, 0, :, :], ALU.mult))
                    dve.wait_ge(da_ready, nth(g, UNITS, n))
                    flat = x_n.rearrange("p i t -> p (i t)")
                    dve.tensor_tensor_scan(flat, da[:, n % 2, :, :].rearrange("p i t -> p (i t)"), flat,
                                           0.0, ALU.mult, ALU.add).then_inc(scanned, 1)
                    dve.wait_ge(scanned, nth(g, UNITS, n) + 2)
                    dve.tensor_tensor(x_n, x_n, bc[:, q % 2, 1, :, :], ALU.mult).then_inc(hc_ready, 1)
                    if c == DC - 1:
                        dve.wait_ge(hc_ready, nth(g, UNITS, n))
                        dve.sem_inc(bc_free, 1)
                    if n == UNITS - 2:
                        gate(g, 0)
                    if n == UNITS - 1:
                        gate(g, 1)
                        gate(g, 2)

                def gate(g, c):
                    dve.wait_ge(summed, nth(g, UNITS, UNITS - DC + c))
                    if c == 0 or c == DC - 1:
                        dve.wait_ge(z_ready, nth(g, DC, c if c else DC - 2))
                    dve.tensor_tensor(y[:, c, :], y_ps[:, c, :], silu_z[:, c, :], ALU.mult).then_inc(y_ready, 1)
                    dve.wait_ge(y_ready, nth(g, DC, c))
                    dve.sem_inc(y_free, 1)

                def add_out(g):
                    link = Chain(dve, out_chain, g * S)
                    dve.wait_ge(out_ready, nth(g, 1))
                    for s, h_s in enumerate(h_tiles(g)):
                        link(dve.tensor_tensor(h_s, h_s, wide[:, s // 2, (s % 2) * DIM:(s % 2 + 1) * DIM], ALU.add))
                    dve.sem_inc(wide_free, 1)

                run_groups(dve, unit,
                           {0: [norm_h], 1: [norm_x], 5: [convolve(0)], 6: [convolve(1)], 7: [convolve(2)],
                            8: [convolve(3)], 13: [softplus((0, 1))], 15: [softplus((2, 3))]},
                           {}, {0: lambda g: gate(g, DC - 1), 1: add_out})


def attention(nc, h, ident, w):
    with ExitStack() as ctx:
        mem = Memory(nc, ctx, "att")
        q_cos, q_sin = mem.sb("q_cos", [P, KC, TOKENS]), mem.sb("q_sin", [P, KC, TOKENS])
        keys = mem.sb("keys", [P, TILES, KV_HEADS, P])
        v = mem.sb("v", [P, TILES, KV_HEADS, HEAD_DIM + 1])
        wout = mem.sb("wout", [P, KC, DIM])
        bout = mem.sb("bout", [P, DIM])
        ident_b = mem.sb("ident_b", [P, P], BF16)
        causal = mem.sb("causal", [P, KV_HEADS, P], BF16)
        attention_inputs(nc, h, ident, w, q_cos, q_sin, keys, v, wout, bout, ident_b, causal)
        attention_heads(nc, h, ident, q_cos, q_sin, keys, v, wout, bout, ident_b, causal)


def attention_inputs(nc, h, ident, w, q_cos, q_sin, keys, v, wout, bout, ident_b, causal):
    q_rank, kv_rank, kv_width = 64, 32, KV_HEADS * HEAD_DIM
    S = SEQ_PER_GROUP
    with ExitStack() as ctx:
        mem = Memory(nc, ctx, "qkv")
        wqa, wkva = mem.sb("wqa", [P, KC, q_rank]), mem.sb("wkva", [P, KC, kv_rank])
        wqb = mem.sb("wqb", [q_rank, 2, DIM])
        wk = mem.sb("wk", [kv_rank, 2, 2 * kv_width])
        wv = mem.sb("wv", [kv_rank, kv_width])
        rope_q, rope_k = mem.sb("rope_q", [P, 2, P]), mem.sb("rope_k", [P, 2, P])
        key_head = mem.sb("key_head", [P, KV_HEADS])

        x = mem.sb("x", [P, S, DIM])
        x_t = mem.sb("x_t", [P, KC, GT])
        qa, kva = mem.sb("qa", [q_rank, GT]), mem.sb("kva", [kv_rank, GT])
        k_cos, k_sin = mem.sb("k_cos", [P, GT]), mem.sb("k_sin", [P, GT])
        scratch = norm_scratch(mem, S)

        xt_ps = mem.ps("xt_ps", [P, KC, 512])
        low_ps = mem.ps("low_ps", [P, 2, 512])
        qk_ps = mem.ps("qk_ps", [P, 2, 512])
        v_ps = mem.ps("v_ps", [P, 512])

        weights_in, constants = mem.sem("weights_in"), mem.sem("constants")
        norm_chain, keys_chain = mem.sem("norm_chain"), mem.sem("keys_chain")
        x_ready, x_turned, x_t_ready = mem.sem("x_ready"), mem.sem("x_turned"), mem.sem("x_t_ready")
        low_done, low_ready = mem.sem("low_done"), mem.sem("low_ready")
        qk_done, qk_used = mem.sem("qk_done"), mem.sem("qk_used")
        v_done, v_ready = mem.sem("v_done"), mem.sem("v_ready")

        USES = 2 * (KC + 1)
        loads = ((wqa[:, :, :], w["Wqa"]), (wkva[:, :, :], w["Wkva"]), (wqb[:, :, :], w["Wqb"]), (wk[:, :, :], w["Wk"]),
                 (wv[:, :], w["Wv"]), (wout[:, :, :], w["Wout"]), (bout[:, :], w["bout"].partition_broadcast(P)),
                 (rope_q[:, :, :], w["rope_q"]),
                 (rope_k[:, :, :], w["rope_k"]), (key_head[:, :], w["key_head"]))

        def by_seq(a):
            return a.rearrange("p (s t) -> p s t", t=P)

        with nc.Block() as block:
            @block.sync
            def _(sp):
                for dst, src in loads:
                    sp.dma_start(dst, src).then_inc(weights_in, 16)

            @block.gpsimd
            def _(pool):
                pool.memset(v[:, :, :, :], 1.0).then_inc(constants, 1)
                pool.tensor_copy(ident_b[:, :], ident[:, :]).then_inc(constants, 1)
                pool.memset(causal[:, :, :], 0.0).then_inc(constants, 1)
                pool.wait_ge(constants, 3)
                pool.affine_select(out=causal[:, :, :], in_=causal[:, :, :], compare_op=ALU.is_ge, fill=-1e30, base=0,
                                   pattern=[[0, KV_HEADS], [-1, P]], channel_multiplier=1).then_inc(constants, 1)
                pool.wait_ge(constants, 4)

            @block.tensor
            def _(pe):
                pe.wait_ge(weights_in, 16 * len(loads))

                def turn(g):
                    pe.wait_ge(x_ready, nth(g, 1))
                    for k in range(KC):
                        for s in range(S):
                            ins = pe.transpose(xt_ps[:, k, s * P:(s + 1) * P], x[:, s, k * P:(k + 1) * P], ident[:, :])
                        ins.then_inc(x_turned, 1)

                def products(g):
                    pe.wait_ge(x_t_ready, nth(g, KC, KC - 1))
                    for b, (wgt, rank) in enumerate(((wqa, q_rank), (wkva, kv_rank))):
                        for k in range(KC):
                            ins = pe.matmul(low_ps[0:rank, b, :], wgt[:, k, :], x_t[:, k, :],
                                            start=(k == 0), stop=(k == KC - 1))
                        ins.then_inc(low_done, 1)
                    for c in range(KC + 1):
                        if c == 0 or c == KC:
                            pe.wait_ge(low_ready, nth(g, 2, min(c, 1)))
                        for b in range(2):
                            pe.wait_ge(qk_used, nth(g, USES, 2 * c + b))
                            if c < KC:
                                ins = pe.matmul(qk_ps[:, b, :], wqb[:, b, c * P:(c + 1) * P], qa[:, :], start=True, stop=True)
                            else:
                                ins = pe.matmul(qk_ps[:, b, :], wk[:, b, :], kva[:, :], start=True, stop=True)
                            ins.then_inc(qk_done, 1)
                    pe.wait_ge(v_ready, nth(g, 1))
                    for s in range(S):
                        ins = pe.matmul(v_ps[:, s * kv_width:(s + 1) * kv_width], kva[:, s * P:(s + 1) * P], wv[:, :],
                                        start=True, stop=True)
                    ins.then_inc(v_done, 1)

                turn(0)
                with pe.Fori(0, GROUPS - 1) as g:
                    products(g)
                    turn(g + 1)
                products(GROUPS - 1)

            @block.scalar
            def _(act):
                act.wait_ge(constants, 4)

                def keep_x(g):
                    for k in range(KC):
                        act.wait_ge(x_turned, nth(g, KC, k))
                        act.activation(x_t[:, k, :], xt_ps[:, k, :], ACT.Copy).then_inc(x_t_ready, 1)

                def keep_low(g):
                    for b, (dst, rank) in enumerate(((qa, q_rank), (kva, kv_rank))):
                        act.wait_ge(low_done, nth(g, 2, b))
                        act.activation(dst[:, :], low_ps[0:rank, b, :], ACT.Copy).then_inc(low_ready, 1)

                keep_x(0)
                with act.Fori(0, GROUPS - 1) as g:
                    keep_low(g)
                    keep_x(g + 1)
                keep_low(GROUPS - 1)

            @block.vector
            def _(dve):
                dve.sem_inc(qk_used, 2)
                dve.sem_inc(v_ready, 1)
                dve.wait_ge(weights_in, 16 * len(loads))
                dve.wait_ge(constants, 4)

                def normalise(g):
                    link = Chain(dve, norm_chain, g * norm_links(S))
                    h_tiles = [h[:, bass.ds(g * S + s, 1), :].rearrange("p a d -> p (a d)") for s in range(S)]
                    if not isinstance(g, int):
                        dve.wait_ge(x_turned, g * KC)
                    layer_norm(dve, link, [x[:, s, :] for s in range(S)], h_tiles, *scratch)
                    dve.sem_inc(x_ready, 1)

                def rotate(g):
                    for c in range(KC + 1):
                        for b, (q_part, k_part) in enumerate(((q_cos, k_cos), (q_sin, k_sin))):
                            to = q_part[:, c, bass.ds(g * GT, GT)] if c < KC else k_part[:, :]
                            dve.wait_ge(qk_done, nth(g, USES, 2 * c + b))
                            rope = rope_q if c < KC else rope_k
                            dve.tensor_tensor(by_seq(to), by_seq(qk_ps[:, b, :]),
                                              rope[:, b, :].unsqueeze(1).to_broadcast([P, S, P]), ALU.mult)\
                               .then_inc(qk_used, 1)

                def lay_keys(g):
                    link = Chain(dve, keys_chain, g * (1 + KV_HEADS))
                    dve.wait_ge(qk_used, nth(g, USES, USES - 1) + 2)
                    link(dve.tensor_tensor(k_cos[:, :], k_cos[:, :], k_sin[:, :], ALU.add))
                    for c in range(KV_HEADS):
                        link(dve.tensor_scalar(keys[:, bass.ds(g * S, S), c, :], by_seq(k_cos[:, :]),
                                               key_head[:, c:c + 1], None, ALU.mult))
                    dve.wait_ge(v_done, nth(g, 1))
                    dve.tensor_copy(v[:, bass.ds(g * S, S), :, 0:HEAD_DIM].rearrange("p s c d -> p (s c) d"),
                                    v_ps[:, 0:S * kv_width].rearrange("p (n d) -> p n d", d=HEAD_DIM)).then_inc(v_ready, 1)

                normalise(0)
                with dve.Fori(0, GROUPS - 1) as g:
                    normalise(g + 1)
                    rotate(g)
                    lay_keys(g)
                rotate(GROUPS - 1)
                lay_keys(GROUPS - 1)


def attention_heads(nc, h, ident, q_cos, q_sin, keys, v, wout, bout, ident_b, causal):
    reps = HEADS // KV_HEADS
    half = KV_HEADS * HEAD_DIM
    with ExitStack() as ctx:
        mem = Memory(nc, ctx, "heads")
        q = mem.sb("q", [P, 2, reps, P])
        top = mem.sb("top", [P, HEADS])
        prob = mem.sb("prob", [P, 2, HEADS, P])
        prob_t = mem.sb("prob_t", [P, reps, KV_HEADS, P])
        inverse = mem.sb("inverse", [P, HEADS])
        o = mem.sb("o", [P, DIM])
        o_t = mem.sb("o_t", [P, KC, P])

        s_ps = mem.ps("s_ps", [P, reps, KV_HEADS, P])
        pt_ps = mem.ps("pt_ps", [P, 2, 512])
        o_ps = mem.ps("o_ps", [P, 512])
        out_ps = mem.ps("out_ps", [P, 512])

        top_chain, o_chain, h_chain = mem.sem("top_chain"), mem.sem("o_chain"), mem.sem("h_chain")
        q_cleared = mem.sem("q_cleared")
        q_ready, scores_done, scores_free, shifted, prob_ready = (
            mem.sem(n) for n in ("q_ready", "scores_done", "scores_free", "shifted", "prob_ready"))
        prob_turned, prob_t_ready, prob_used = mem.sem("prob_turned"), mem.sem("prob_t_ready"), mem.sem("prob_used")
        o_ready, o_turned, o_t_ready = (mem.sem(n) for n in ("o_ready", "o_turned", "o_t_ready"))
        out_done, out_added = mem.sem("out_done"), mem.sem("out_added")

        def over_sequences(eng, body):
            body(0, 0, True, False)
            with eng.Fori(0, TILES // 2 - 2) as pair:
                body(pair * 2 + 1, 1, False, False)
                body(pair * 2 + 2, 0, False, False)
            for s in range(TILES - 3, TILES):
                body(s, s % 2, False, s == TILES - 1)

        with nc.Block() as block:
            @block.tensor
            def _(pe):
                def scores(s, b):
                    pe.wait_ge(q_ready, s * 2 + 2)
                    pe.wait_ge(scores_free, s + 1)
                    for r in range(reps):
                        pe.matmul(s_ps[:, r, :, :].rearrange("p c k -> p (c k)"), ident_b[:, :],
                                  causal[:, :, :].rearrange("p c k -> p (c k)"), start=True, stop=False)
                        ins = pe.matmul(s_ps[:, r, :, :].rearrange("p c k -> p (c k)"), q[:, b, r, :],
                                        keys[:, bass.ds(s, 1), :, :].rearrange("p a c k -> p (a c k)"),
                                        start=False, stop=True)
                    ins.then_inc(scores_done, 1)

                def turn_prob(s, b, r, first):
                    if r >= 2 or not first:
                        pe.wait_ge(prob_t_ready, s * reps + r - 1)
                    for c in range(KV_HEADS):
                        ins = pe.transpose(pt_ps[:, r % 2, c * P:(c + 1) * P], prob[:, b, r * KV_HEADS + c, :], ident[:, :])
                    ins.then_inc(prob_turned, 1)

                def values(s, r):
                    pe.wait_ge(prob_t_ready, s * reps + r + 1)
                    for c in range(KV_HEADS):
                        head = c * reps + r
                        ins = pe.matmul(o_ps[:, head * 17:(head + 1) * 17], prob_t[:, r, c, :],
                                        v[:, bass.ds(s, 1), c, :].rearrange("p a d -> p (a d)"), start=True, stop=True)
                    ins.then_inc(prob_used, 1)

                def turn_o(s):
                    pe.wait_ge(o_ready, s + 1)
                    pe.wait_ge(out_added, s + 1)
                    for k in range(KC):
                        ins = pe.transpose(out_ps[:, k * P:(k + 1) * P], o[:, k * P:(k + 1) * P], ident[:, :])
                    ins.then_inc(o_turned, 1)

                def project(s):
                    pe.wait_ge(o_t_ready, s + 1)
                    for k in range(KC):
                        ins = pe.matmul(out_ps[:, 0:DIM], o_t[:, k, :], wout[:, k, :], start=(k == 0), stop=(k == KC - 1))
                    ins.then_inc(out_done, 1)

                def sequence(s, b, first, last):
                    if not last:
                        scores(s + 1, 1 - b)
                    pe.wait_ge(prob_ready, s + 1)
                    turn_prob(s, b, 0, first)
                    turn_prob(s, b, 1, first)
                    if not first:
                        turn_o(s - 1)
                    values(s, 0)
                    turn_prob(s, b, 2, first)
                    values(s, 1)
                    turn_prob(s, b, 3, first)
                    if not first:
                        project(s - 1)
                    values(s, 2)
                    values(s, 3)

                scores(0, 0)
                over_sequences(pe, sequence)
                turn_o(TILES - 1)
                project(TILES - 1)

            @block.scalar
            def _(act):
                def exponent(s, b):
                    act.wait_ge(shifted, s + 1)
                    flat = prob[:, b, :, :].rearrange("p n k -> p (n k)")
                    act.activation(flat, flat, ACT.Exp).then_inc(prob_ready, 1)

                def keep_prob(s, r, first):
                    act.wait_ge(prob_turned, s * reps + r + 1)
                    if not first:
                        act.wait_ge(prob_used, s * reps - reps + r + 1)
                    act.activation(prob_t[:, r, :, :].rearrange("p c q -> p (c q)"), pt_ps[:, r % 2, :], ACT.Copy)\
                       .then_inc(prob_t_ready, 1)

                def keep_o(s):
                    act.wait_ge(o_turned, s + 1)
                    act.activation(o_t[:, :, :].rearrange("p k n -> p (k n)"), out_ps[:, 0:DIM], ACT.Copy)\
                       .then_inc(o_t_ready, 1)

                def sequence(s, b, first, last):
                    keep_prob(s, 0, first)
                    keep_prob(s, 1, first)
                    if not first:
                        keep_o(s - 1)
                    keep_prob(s, 2, first)
                    keep_prob(s, 3, first)
                    if not last:
                        exponent(s + 1, 1 - b)

                exponent(0, 0)
                over_sequences(act, sequence)
                keep_o(TILES - 1)

            @block.vector
            def _(dve):
                dve.memset(q[:, :, :, :], 0.0).then_inc(q_cleared, 1)
                dve.wait_ge(q_cleared, 1)
                dve.sem_inc(scores_free, 1)
                dve.sem_inc(out_added, 1)

                def h_tile(s):
                    return h[:, bass.ds(s, 1), :].rearrange("p a d -> p (a d)")

                def add_q(s, b):
                    if not isinstance(s, int) or s >= 2:
                        dve.wait_ge(scores_done, s - 1)
                    for n in range(2):
                        rows, cols = slice(n * half, (n + 1) * half), bass.ds(s * P, P)
                        dve.tensor_tensor(q[rows, b, n::2, :], q_cos[rows, :, cols], q_sin[rows, :, cols],
                                          ALU.add).then_inc(q_ready, 1)

                def shift(s, b):
                    link = Chain(dve, top_chain, s)
                    dve.wait_ge(scores_done, s + 1)
                    scores = s_ps[:, :, :, :].rearrange("p r c k -> p (r c) k")
                    link(dve.tensor_reduce(top[:, :], scores, AXX, ALU.max))
                    if not isinstance(s, int) or s >= 2:
                        dve.wait_ge(prob_turned, s * reps - reps)
                    dve.tensor_tensor(prob[:, b, :, :], scores, top[:, :].unsqueeze(2).to_broadcast([P, HEADS, P]),
                                      ALU.subtract).then_inc(shifted, 1)
                    dve.wait_ge(shifted, s + 1)
                    dve.sem_inc(scores_free, 1)

                def divide(s, first):
                    link = Chain(dve, o_chain, s)
                    dve.wait_ge(prob_used, s * reps + reps)
                    o_all = o_ps[:, 0:HEADS * 17].rearrange("p (n d) -> p n d", d=17)
                    link(dve.reciprocal(inverse[:, :], o_all[:, :, HEAD_DIM]))
                    if not first:
                        dve.wait_ge(o_turned, s)
                    dve.tensor_tensor(o[:, :].rearrange("p (n d) -> p n d", d=HEAD_DIM), o_all[:, :, 0:HEAD_DIM],
                                      inverse[:, :].unsqueeze(2).to_broadcast([P, HEADS, HEAD_DIM]), ALU.mult)\
                       .then_inc(o_ready, 1)

                def add_out(s):
                    link = Chain(dve, h_chain, s)
                    link(dve.tensor_tensor(h_tile(s), h_tile(s), bout[:, :], ALU.add))
                    dve.wait_ge(out_done, s + 1)
                    dve.tensor_tensor(h_tile(s), h_tile(s), out_ps[:, 0:DIM], ALU.add).then_inc(out_added, 1)

                def sequence(s, b, first, last):
                    if not last:
                        shift(s + 1, 1 - b)
                    if not first:
                        add_out(s - 1)
                    if not isinstance(s, int) or s + 2 < TILES:
                        add_q(s + 2, b)
                    divide(s, first)

                add_q(0, 0)
                add_q(1, 1)
                shift(0, 0)
                over_sequences(dve, sequence)
                add_out(TILES - 1)


def most_tiles(choices):
    return (TOKENS * choices + EXPERTS * (P - 1)) // P


def over_tiles(eng, n, body):
    body(0, 0, True, False)
    with eng.Fori(0, (n - 3) // 2) as pair:
        body(pair * 2 + 1, 1, False, False)
        body(pair * 2 + 2, 0, False, False)
    body(n - 2, 1, False, False)
    body(n - 1, 0, False, True)


def moe(nc, h, ident, w, choices, slots, results, parked, stage):
    shared = choices == 2
    n_tiles = most_tiles(choices)
    pairs = choices * TILES
    with ExitStack() as ctx:
        mem = Memory(nc, ctx, stage)
        x = mem.sb("x", [P, TILES, DIM])
        x_t = h[:, :, :].rearrange("p t d -> p (t d)").rearrange("p (k n) -> p k n", k=KC)
        w1 = mem.sb("w1", [P, KC, EXPERTS, FF])
        w2 = mem.sb("w2", [P, FC, EXPERTS, DIM])
        b1 = mem.sb("b1", [P, FC, EXPERTS])
        b2 = mem.sb("b2", [P, EXPERTS, DIM])
        router_w, router_b = mem.sb("router_w", [P, KC, EXPERTS]), mem.sb("router_b", [P, EXPERTS])
        ff = mem.sb("ff", [P, 2, FF])
        hidden = ff[:, 0, :]
        active = ff[:, 1, :].rearrange("p (f n) -> p f n", f=FC)
        shared_act = ff[:, :, :].rearrange("p a n -> p (a n)").rearrange("p (f n) -> p f n", f=SC)
        x_in, x_in_t, y_out = (mem.sb(n, [P, 2, DIM]) for n in ("x_in", "x_in_t", "y_out"))
        if shared:
            gate = mem.sb("gate", [P, FC, EXPERTS])
            sw1, sw2 = mem.sb("sw1", [P, KC, SHARED_FF]), mem.sb("sw2", [P, SC, DIM])
            sb1, sgate = mem.sb("sb1", [P, SC]), mem.sb("sgate", [P, SC])
            sb2, ln_g, ln_b = mem.sb("sb2", [P, DIM]), mem.sb("ln_g", [P, DIM]), mem.sb("ln_b", [P, DIM])
            mix = mem.sb("mix", [P, 1])
        zeros = mem.sb("zeros", [P, DIM])
        lower, ones = mem.sb("lower", [P, P]), mem.sb("ones", [P, P])
        expert_no = mem.sb("expert_no", [P, EXPERTS])
        tile_no = mem.sb("tile_no", [1, n_tiles, EXPERTS])
        logits, top, top_i = mem.sb("logits", [P, TILES, EXPERTS]), mem.sb("top", [P, TILES, 8]), mem.sb("top_i", [P, TILES, 8], U32)
        top_f = mem.sb("top_f", [P, TILES, choices])
        total, weight = mem.sb("total", [P, TILES]), mem.sb("weight", [P, TILES, choices])
        onehot = mem.sb("onehot", [P, choices, TILES, EXPERTS])
        before = mem.sb("before", [P, choices, TILES, EXPERTS])
        counts = mem.sb("counts", [P, pairs, EXPERTS])
        running = mem.sb("running", [P, pairs, EXPERTS])
        tiles_i = mem.sb("tiles_i", [P, EXPERTS], I32)
        tiles_of, last_tile, base = (mem.sb(n, [P, EXPERTS]) for n in ("tiles_of", "last_tile", "base"))
        slot_f, slot = mem.sb("slot_f", [P, pairs]), mem.sb("slot", [P, pairs], I32)
        passed = mem.sb("passed", [1, n_tiles, EXPERTS])
        expert_f, expert = mem.sb("expert_f", [1, n_tiles]), mem.sb("expert", [1, n_tiles], I32)
        scratch = norm_scratch(mem, SEQ_PER_GROUP)

        h_ps = mem.ps("h_ps", [P, 2, 512])
        ht_ps = mem.ps("ht_ps", [P, 2, 512])
        xt_ps = mem.ps("xt_ps", [P, 512])
        y_ps = mem.ps("y_ps", [P, 2, 512])
        route_ps = mem.ps("route_ps", [P, 512])

        small_in, w1_in, w2_in = mem.sem("small_in"), mem.sem("w1_in"), mem.sem("w2_in")
        constants, chain, mixed = mem.sem("constants"), mem.sem("chain"), mem.sem("mixed")
        x_ready, h_parked, h_back = mem.sem("x_ready"), mem.sem("h_parked"), mem.sem("h_back")
        xt_done, xt_copied = mem.sem("xt_done"), mem.sem("xt_copied")
        logits_done, exp_asked, exp_ready, onehot_ready, counted = (
            mem.sem(n) for n in ("logits_done", "exp_asked", "exp_ready", "onehot_ready", "counted"))
        routed, cleared, scattered = mem.sem("routed"), mem.sem("cleared"), mem.sem("scattered")
        sh_done, sh_active, sh_out, sh_kept = (mem.sem(n) for n in ("sh_done", "sh_active", "sh_out", "sh_kept"))
        in_loaded = [mem.sem(f"in_loaded{b}") for b in range(2)]
        in_turned, turn_copied = mem.sem("in_turned"), mem.sem("turn_copied")
        hidden_done, hidden_kept = mem.sem("hidden_done"), mem.sem("hidden_kept")
        hidden_turned, active_ready = mem.sem("hidden_turned"), mem.sem("active_ready")
        y_done, y_kept = mem.sem("y_done"), mem.sem("y_kept")
        y_stored, y_out_free = mem.sem("y_stored"), mem.sem("y_out_free")
        gathered, combined = [mem.sem("gathered0"), mem.sem("gathered1")], mem.sem("combined")

        small = [(router_w[:, :, :], w["router_w"]), (router_b[:, :], w["router_b"].partition_broadcast(P)),
                 (b1[:, :, :], w["b1"]), (b2[:, :, :].rearrange("p e d -> p (e d)"), w["b2"].partition_broadcast(P))]
        if shared:
            small += [(gate[:, :, :], w["gate"]), (sw1[:, :, :], w["sw1"]), (sw2[:, :, :], w["sw2"]), (sb1[:, :], w["sb1"]),
                      (sgate[:, :], w["sgate"]), (sb2[:, :], w["sb2"].partition_broadcast(P)),
                      (ln_g[:, :], w["ln_g"].partition_broadcast(P)), (ln_b[:, :], w["ln_b"].partition_broadcast(P)),
                      (mix[:, :], w["shared_weight"].partition_broadcast(P))]
        small_all = 16 * len(small)
        sh_uses = GROUPS * SC if shared else 0

        tiles_back = TILES // choices
        rounds = TILES // tiles_back
        back = h[:, :, :]

        def tile_rows(dram, j):
            return dram[bass.ds(j * P, P), :]

        with nc.Block() as block:
            @block.sync
            def _(sp):
                for dst, src in small:
                    sp.dma_start(dst, src).then_inc(small_in, 16)
                sp.dma_start(parked.rearrange("(t p) d -> p t d", p=P), h[:, :, :]).then_inc(h_parked, 16)
                for e in range(EXPERTS):
                    sp.dma_start(w1[:, :, e, :], w["w1"][:, :, e, :]).then_inc(w1_in, 16)
                for e in range(EXPERTS):
                    sp.dma_start(w2[:, :, e, :], w["w2"][:, :, e, :]).then_inc(w2_in, 16)
                sp.wait_ge(scattered, 16 * pairs)

                def load(j, b, first, last):
                    if not first:
                        sp.wait_ge(in_turned, j - 1 + b)
                    sp.dma_start(x_in[:, b, :], tile_rows(slots, j)).then_inc(in_loaded[b], 16)

                over_tiles(sp, n_tiles, load)
                sp.wait_ge(combined, rounds)
                sp.dma_start(h[:, :, :], parked.rearrange("(t p) d -> p t d", p=P)).then_inc(h_back, 16)

            @block.gpsimd
            def _(pool):
                pool.memset(zeros[:, :], 0.0).then_inc(constants, 1)
                pool.memset(lower[:, :], 1.0).then_inc(constants, 1)
                pool.memset(ones[:, :], 1.0).then_inc(constants, 1)
                pool.wait_ge(constants, 3)
                pool.affine_select(out=lower[:, :], in_=lower[:, :], compare_op=ALU.is_gt, fill=0.0, base=0,
                                   pattern=[[1, P]], channel_multiplier=-1).then_inc(constants, 1)
                pool.iota(expert_no[:, :], pattern=[[1, EXPERTS]], base=0, channel_multiplier=0,
                          allow_small_or_imprecise_dtypes=True).then_inc(constants, 1)
                pool.iota(tile_no[:, :, :], pattern=[[1, n_tiles], [0, EXPERTS]], base=0, channel_multiplier=0,
                          allow_small_or_imprecise_dtypes=True).then_inc(constants, 1)
                pool.dma_start(slots.rearrange("(a p) d -> p a d", p=P),
                               zeros[:, :].unsqueeze(1).to_broadcast([P, n_tiles, DIM])).then_inc(cleared, 16)
                pool.wait_ge(cleared, 16)
                pool.wait_ge(routed, 1)
                for t in range(TILES):
                    for k in range(choices):
                        pool.indirect_dma_start(
                            slots, bass.IndirectOffsetOnAxis(slot[:, k * TILES + t:k * TILES + t + 1].bitcast(U32), 0),
                            x[:, t, :], None, bounds_check=n_tiles * P - 1, oob_is_err=False).then_inc(scattered, 16)

                pool.sem_inc(y_out_free, 2)

                def store(j, b, first, last):
                    pool.wait_ge(y_kept, j + 2)
                    pool.dma_start(tile_rows(results, j), y_out[:, b, :]).then_inc(y_stored, 16)
                    pool.wait_ge(y_stored, j * 16 + 16)
                    pool.sem_inc(y_out_free, 1)

                over_tiles(pool, n_tiles, store)
                for r in range(rounds):
                    if r:
                        pool.wait_ge(combined, r)
                    for i in range(tiles_back):
                        for k in range(choices):
                            n = k * TILES + r * tiles_back + i
                            pool.indirect_dma_start(
                                back[:, i * choices + k, :], None, results,
                                bass.IndirectOffsetOnAxis(slot[:, n:n + 1].bitcast(U32), 0),
                                bounds_check=n_tiles * P - 1, oob_is_err=False).then_inc(gathered[r], 16)

            @block.tensor
            def _(pe):
                pe.wait_ge(small_in, small_all)
                for t in range(TILES + 1):
                    if t < TILES:
                        pe.wait_ge(x_ready, t // SEQ_PER_GROUP + 1)
                        if t >= 2:
                            pe.wait_ge(xt_copied, t - 1)
                        for k in range(KC):
                            ins = pe.transpose(y_ps[:, t % 2, k * P:(k + 1) * P], x[:, t, k * P:(k + 1) * P], ident[:, :])
                        ins.then_inc(xt_done, 1)
                    if t >= 1:
                        v = t - 1
                        pe.wait_ge(xt_copied, v + 1)
                        for k in range(KC):
                            ins = pe.matmul(route_ps[:, v * EXPERTS:(v + 1) * EXPERTS], x_t[:, k, v * P:(v + 1) * P],
                                            router_w[:, k, :], start=(k == 0), stop=(k == KC - 1))
                ins.then_inc(logits_done, 1)
                pe.wait_ge(onehot_ready, choices)
                pe.wait_ge(constants, 6)
                picks = onehot[:, :, :, :].rearrange("p c t e -> p (c t e)")
                width = pairs * EXPERTS
                pe.matmul(h_ps[:, 0, 0:width], lower[:, :], picks, start=True, stop=True)
                pe.matmul(h_ps[:, 1, 0:width], ones[:, :], picks, start=True, stop=True).then_inc(counted, 1)
                pe.wait_ge(routed, 1)
                if shared:
                    for g in range(GROUPS):
                        for f in range(SC):
                            n = g * SC + f
                            if n >= 2:
                                pe.wait_ge(sh_active, n - 1)
                            for k in range(KC):
                                ins = pe.matmul(h_ps[:, n % 2, :], sw1[:, k, f * P:(f + 1) * P],
                                                x_t[:, k, g * GT:(g + 1) * GT], start=(k == 0), stop=(k == KC - 1))
                            ins.then_inc(sh_done, 1)
                        pe.wait_ge(sh_active, (g + 1) * SC)
                        for s in range(SEQ_PER_GROUP):
                            n = g * SEQ_PER_GROUP + s
                            if n >= 2:
                                pe.wait_ge(sh_kept, n - 1)
                            for f in range(SC):
                                ins = pe.matmul(y_ps[:, n % 2, 0:DIM], shared_act[:, f, s * P:(s + 1) * P], sw2[:, f, :],
                                                start=(f == 0), stop=(f == SC - 1))
                            ins.then_inc(sh_out, 1)
                    pe.wait_ge(sh_kept, TILES)

                def turn_input(j, b):
                    pe.wait_ge(in_loaded[b], (j // 2 + 1) * 16 if isinstance(j, int) else j * 8 + (8 if b else 16))
                    pe.wait_ge(turn_copied, j) if not isinstance(j, int) or j > 0 else None
                    for k in range(KC):
                        ins = pe.transpose(xt_ps[:, k * P:(k + 1) * P], x_in[:, b, k * P:(k + 1) * P], ident[:, :])
                    ins.then_inc(in_turned, 1)

                def second(j, e):
                    pe.wait_ge(active_ready, j + 1)
                    for f in range(FC):
                        ins = pe.matmul(y_ps[:, 0, 0:DIM], active[:, f, :],
                                        w2[:, f, bass.ds(e, 1), :].rearrange("p a d -> p (a d)"),
                                        start=(f == 0), stop=(f == FC - 1))
                    ins.then_inc(y_done, 1)

                def expert_of(j):
                    return pe.value_load(expert[0:1, bass.ds(j, 1)], min_val=0, max_val=EXPERTS - 1)

                def tile(j, b, first, last):
                    e = expert_of(j)
                    e_before = None if first else expert_of(j - 1)
                    pe.wait_ge(turn_copied, j + 1)
                    if not first:
                        pe.wait_ge(hidden_kept, j)
                    for half in range(2):
                        for k in range(KC):
                            ins = pe.matmul(h_ps[:, half, :], x_in_t[:, b, k * P:(k + 1) * P],
                                            w1[:, k, bass.ds(e, 1), half * 512:(half + 1) * 512].rearrange("p a n -> p (a n)"),
                                            start=(k == 0), stop=(k == KC - 1))
                    ins.then_inc(hidden_done, 1)
                    if not last:
                        turn_input(j + 1, 1 - b)
                    if not first:
                        pe.wait_ge(y_kept, j)
                        second(j - 1, e_before)
                    pe.wait_ge(hidden_kept, j + 1)
                    for f in range(FC):
                        ins = pe.transpose(ht_ps[:, f // 4, (f % 4) * P:(f % 4 + 1) * P], hidden[:, f * P:(f + 1) * P],
                                           ident[:, :])
                    ins.then_inc(hidden_turned, 1)

                pe.wait_ge(w1_in, 16 * EXPERTS)
                pe.wait_ge(w2_in, 16 * EXPERTS)
                turn_input(0, 0)
                over_tiles(pe, n_tiles, tile)
                e = expert_of(n_tiles - 1)
                pe.wait_ge(y_kept, n_tiles)
                second(n_tiles - 1, e)

            @block.scalar
            def _(act):
                for t in range(TILES):
                    if t == 0:
                        act.wait_ge(h_parked, 16)
                        act.wait_ge(x_ready, GROUPS)
                    act.wait_ge(xt_done, t + 1)
                    act.activation(x_t[:, :, t * P:(t + 1) * P],
                                   y_ps[:, t % 2, 0:DIM].rearrange("p (k n) -> p k n", k=KC), ACT.Copy).then_inc(xt_copied, 1)
                if shared:
                    act.wait_ge(small_in, small_all)
                    act.activation(mix[:, :], mix[:, :], ACT.Exp, scale=-1.0).then_inc(mixed, 1)
                act.wait_ge(exp_asked, 1)
                act.activation(top[:, :, :], top[:, :, :], ACT.Exp).then_inc(exp_ready, 1)
                if shared:
                    act.wait_ge(mixed, 5)
                    for n in range(sh_uses):
                        f = n % SC
                        act.wait_ge(sh_done, n + 1)
                        if f == 0 and n:
                            act.wait_ge(sh_out, n)
                        act.activation(shared_act[:, f, :], h_ps[:, n % 2, :], ACT.Gelu, bias=sb1[:, f:f + 1],
                                       scale=sgate[:, f:f + 1]).then_inc(sh_active, 1)

                def turn_copy(j, b):
                    act.wait_ge(in_turned, j + 1)
                    act.activation(x_in_t[:, b, :], xt_ps[:, 0:DIM], ACT.Copy).then_inc(turn_copied, 1)

                def tile(j, b, first, last):
                    if not last:
                        turn_copy(j + 1, 1 - b)
                    e = act.value_load(expert[0:1, bass.ds(j, 1)], min_val=0, max_val=EXPERTS - 1)
                    act.wait_ge(hidden_turned, j + 1)
                    for f in range(FC):
                        act_args = dict(bias=b1[:, f, bass.ds(e, 1)])
                        if shared:
                            act_args["scale"] = gate[:, f, bass.ds(e, 1)]
                        ins = act.activation(active[:, f, :], ht_ps[:, f // 4, (f % 4) * P:(f % 4 + 1) * P],
                                             ACT.Gelu if shared else ACT.Relu, **act_args)
                    ins.then_inc(active_ready, 1)

                act.wait_ge(routed, 1)
                turn_copy(0, 0)
                over_tiles(act, n_tiles, tile)

            @block.vector
            def _(dve):
                link = Chain(dve, chain)
                for g in range(GROUPS):
                    tiles = range(g * SEQ_PER_GROUP, (g + 1) * SEQ_PER_GROUP)
                    layer_norm(dve, link, [x[:, t, :] for t in tiles], [h[:, t, :] for t in tiles], *scratch)
                    dve.sem_inc(x_ready, 1)
                dve.wait_ge(small_in, small_all)
                if shared:
                    dve.wait_ge(mixed, 1)
                    dve.tensor_scalar(mix[:, :], mix[:, :], 1.0, None, ALU.add).then_inc(mixed, 1)
                    dve.wait_ge(mixed, 2)
                    dve.reciprocal(mix[:, :], mix[:, :]).then_inc(mixed, 1)
                    dve.tensor_tensor(b1[:, :, :], b1[:, :, :], gate[:, :, :], ALU.mult).then_inc(mixed, 1)
                    dve.tensor_tensor(sb1[:, :], sb1[:, :], sgate[:, :], ALU.mult).then_inc(mixed, 1)
                    dve.wait_ge(mixed, 5)
                    link(dve.tensor_scalar(sb2[:, :], sb2[:, :], mix[:, 0:1], None, ALU.mult))
                dve.wait_ge(logits_done, 1)
                link(dve.tensor_tensor(logits[:, :, :], route_ps[:, 0:TILES * EXPERTS].rearrange("p (t e) -> p t e", e=EXPERTS),
                                       router_b[:, :].unsqueeze(1).to_broadcast([P, TILES, EXPERTS]), ALU.add))
                for t in range(TILES):
                    link(dve.max(top[:, t, :], logits[:, t, :]))
                for t in range(TILES):
                    link(dve.max_index(top_i[:, t, :], top[:, t, :], logits[:, t, :]))
                link(dve.tensor_copy(top_f[:, :, :], top_i[:, :, 0:choices]))
                link(dve.tensor_copy(total[:, :], top[:, :, 0]))
                dve.tensor_tensor(top[:, :, :], top[:, :, :], total[:, :].unsqueeze(2).to_broadcast([P, TILES, 8]),
                                  ALU.subtract).then_inc(exp_asked, 1)
                dve.wait_ge(constants, 6)
                for k in range(choices):
                    dve.tensor_tensor(onehot[:, k, :, :], top_f[:, :, k:k + 1].to_broadcast([P, TILES, EXPERTS]),
                                      expert_no[:, :].unsqueeze(1).to_broadcast([P, TILES, EXPERTS]),
                                      ALU.is_equal).then_inc(onehot_ready, 1)
                dve.wait_ge(exp_ready, 1)
                link(dve.tensor_reduce(total[:, :], top[:, :, 0:2] if shared else top[:, :, :], AXX, ALU.add))
                link(dve.reciprocal(total[:, :], total[:, :]))
                link(dve.tensor_tensor(weight[:, :, :], top[:, :, 0:choices],
                                       total[:, :].unsqueeze(2).to_broadcast([P, TILES, choices]), ALU.mult))
                width = pairs * EXPERTS
                dve.wait_ge(counted, 1)
                link(dve.tensor_copy(before[:, :, :, :].rearrange("p c t e -> p (c t e)"), h_ps[:, 0, 0:width]))
                link(dve.tensor_copy(counts[:, :, :].rearrange("p n e -> p (n e)"), h_ps[:, 1, 0:width]))
                for e in range(EXPERTS):
                    link(dve.tensor_tensor_scan(running[:, :, e], ones[:, 0:pairs], counts[:, :, e], 0.0, ALU.mult, ALU.add))
                link(dve.tensor_scalar(tiles_i[:, :], running[:, pairs - 1, :], float(P - 1), None, ALU.add))
                link(dve.tensor_scalar(tiles_i[:, :], tiles_i[:, :], 7, None, ALU.logical_shift_right))
                link(dve.tensor_copy(tiles_of[:, :], tiles_i[:, :]))
                link(dve.tensor_tensor_scan(last_tile[:, :], ones[:, 0:EXPERTS], tiles_of[:, :], 0.0, ALU.mult, ALU.add))
                link(dve.tensor_tensor(base[:, :], last_tile[:, :], tiles_of[:, :], ALU.subtract))
                link(dve.tensor_scalar(base[:, :], base[:, :], float(P), None, ALU.mult))
                at = before[:, :, :, :].rearrange("p c t e -> p (c t) e")
                link(dve.tensor_tensor(at, at, running[:, :, :], ALU.add))
                link(dve.tensor_tensor(at, at, counts[:, :, :], ALU.subtract))
                link(dve.tensor_tensor(at, at, base[:, :].unsqueeze(1).to_broadcast([P, pairs, EXPERTS]), ALU.add))
                link(dve.tensor_tensor(at, at, onehot[:, :, :, :].rearrange("p c t e -> p (c t) e"), ALU.mult))
                link(dve.tensor_reduce(slot_f[:, :], at, AXX, ALU.add))
                link(dve.tensor_copy(slot[:, :], slot_f[:, :]))
                link(dve.tensor_tensor(passed[:, :, :], last_tile[0:1, :].unsqueeze(1).to_broadcast([1, n_tiles, EXPERTS]),
                                       tile_no[:, :, :], ALU.is_le))
                link(dve.tensor_reduce(expert_f[:, :], passed[:, :, :], AXX, ALU.add))
                link(dve.tensor_scalar(expert[:, :], expert_f[:, :], float(EXPERTS - 1), None, ALU.min))
                dve.sem_inc(routed, 1)
                if shared:
                    dve.wait_ge(scattered, 16 * pairs)
                    for t in range(TILES):
                        dve.wait_ge(sh_out, t + 1)
                        dve.scalar_tensor_tensor(x[:, t, :], y_ps[:, t % 2, 0:DIM], mix[:, 0:1], sb2[:, :],
                                                 ALU.mult, ALU.add).then_inc(sh_kept, 1)

                dve.sem_inc(y_kept, 1)

                def keep_y(j, b):
                    e = dve.value_load(expert[0:1, bass.ds(j, 1)], min_val=0, max_val=EXPERTS - 1)
                    dve.wait_ge(y_done, j + 1)
                    dve.wait_ge(y_out_free, j + 1)
                    dve.tensor_tensor(y_out[:, b, :], y_ps[:, 0, 0:DIM],
                                      b2[:, bass.ds(e, 1), :].rearrange("p a d -> p (a d)"), ALU.add).then_inc(y_kept, 1)

                def tile(j, b, first, last):
                    dve.wait_ge(hidden_done, j + 1)
                    if not first:
                        dve.wait_ge(hidden_turned, j)
                    dve.tensor_copy(hidden, h_ps[:, :, :].rearrange("p a n -> p (a n)")).then_inc(hidden_kept, 1)
                    if not first:
                        keep_y(j - 1, 1 - b)

                over_tiles(dve, n_tiles, tile)
                keep_y(n_tiles - 1, (n_tiles - 1) % 2)

                for r in range(rounds):
                    dve.wait_ge(gathered[r], 16 * tiles_back * choices)
                    for i in range(tiles_back):
                        t = r * tiles_back + i
                        if shared:
                            for k in range(choices):
                                link(dve.scalar_tensor_tensor(x[:, t, :], back[:, i * choices + k, :], weight[:, t, k:k + 1],
                                                              x[:, t, :], ALU.mult, ALU.add))
                        else:
                            link(dve.tensor_scalar(x[:, t, :], back[:, i, :], weight[:, t, 0:1], None, ALU.mult))
                    dve.sem_inc(combined, 1)
                if shared:
                    for g in range(GROUPS):
                        tiles = [x[:, t, :] for t in range(g * SEQ_PER_GROUP, (g + 1) * SEQ_PER_GROUP)]
                        layer_norm(dve, link, tiles, tiles, *scratch)
                        for v in tiles:
                            link(dve.tensor_tensor(v, v, ln_g[:, :], ALU.mult))
                            link(dve.tensor_tensor(v, v, ln_b[:, :], ALU.add))
                dve.wait_ge(h_back, 16)
                link(dve.tensor_tensor(h[:, :, :], h[:, :, :], x[:, :, :], ALU.add))


def build(nc, x, out, stages=9):
    with ExitStack() as ctx:
        h = ctx.enter_context(nc.sbuf_tensor("h", [P, TILES, DIM], F32))
        ident = make_constants(nc, ctx)
        bc_dram = nc.dram_tensor("bc_rows", (GROUPS, 2 * STATE, GT), F32, kind="Internal").ap()
        embed(nc, h, ident, x["x"], [x["emb_head"], x["emb_tail_0"], x["emb_tail_1"]], x["emb_proj"])
        if stages >= 2:
            mamba(nc, h, ident, {k[len("mamba_"):]: v for k, v in x.items() if k.startswith("mamba_")}, bc_dram)
        parked = nc.dram_tensor("h_parked", (TOKENS, DIM), F32, kind="Internal").ap()

        def expert_rows(name, choices):
            return nc.dram_tensor(name, (most_tiles(choices) * P, DIM), F32, kind="Internal").ap()

        def part(prefix):
            return {k[len(prefix):]: v for k, v in x.items() if k.startswith(prefix)}

        if stages >= 3:
            moe(nc, h, ident, part("moe0_"), 2, expert_rows("slots0", 2), expert_rows("results0", 2), parked, "moe0")
        if stages >= 4:
            attention(nc, h, ident, part("att_"))
        if stages >= 5:
            moe(nc, h, ident, part("moe1_"), 1, expert_rows("slots1", 1), expert_rows("results1", 1), parked, "moe1")
        stored = ctx.enter_context(nc.semaphore("h_stored"))
        with nc.Block() as block:
            @block.sync
            def _(sp):
                sp.dma_start(out.rearrange("s p d -> p s d"), h[:, :, :]).then_inc(stored, 16)
                sp.wait_ge(stored, 16)


def rope_tables(rows, scale):
    d = np.arange(rows) % HEAD_DIM
    inv_freq = (np.float32(1) / np.float32(10000) ** ((d // 2 * 2).astype(np.float32) / np.float32(HEAD_DIM))).astype(np.float32)
    angle = inv_freq[:, None] * np.arange(P, dtype=np.float32)
    sign = np.where(d % 2 == 0, np.float32(-1), np.float32(1))[:, None]
    return (np.stack([np.cos(angle), sign * np.sin(angle)], 1) * np.float32(scale)).astype(np.float32)


def host_layout(inputs):
    a = {k: np.asarray(v) for k, v in inputs.items()}

    def rows(m):
        return m.reshape(m.shape[0] // P, P, *m.shape[1:]).swapaxes(0, 1)

    t0, m0, f0, t1, f1 = "L0_tok_", "L0_attn_", "L0_ffn_", "L1_attn_", "L1_ffn_"
    swapped = np.arange(DIM) ^ 1
    kv = a[t1 + "Wkvb"].reshape(-1, KV_HEADS * HEAD_DIM, 2)
    by_r = np.arange(DIM).reshape(KV_HEADS, HEADS // KV_HEADS, HEAD_DIM).swapaxes(0, 1).reshape(-1)
    kv_width = KV_HEADS * HEAD_DIM
    wk = np.stack([kv[:, :, 0], kv[:, swapped[:kv_width], 0]], 1)
    return {
        "x": a["x"].T,
        "emb_head": a[t0 + "head_weight"].T,
        "emb_tail_0": a[t0 + "tail_weight_0"].T,
        "emb_tail_1": a[t0 + "tail_weight_1"].T,
        "emb_proj": np.concatenate([a[t0 + "head_weight_proj"].T, a[t0 + "tail_weight_proj_0"].T,
                                    a[t0 + "tail_weight_proj_1"].T]),
        "mamba_ln_gamma": rows(a[m0 + "ln_gamma"]),
        "mamba_ln_beta": rows(a[m0 + "ln_beta"]),
        "mamba_W_in": rows(a[m0 + "W_in"].T),
        "mamba_conv_w": rows(a[m0 + "conv_w"][:, 0, :]),
        "mamba_conv_b": rows(a[m0 + "conv_b"]),
        "mamba_W_xproj": rows(a[m0 + "W_xproj"].T),
        "mamba_W_dt": a[m0 + "W_dt"].T,
        "mamba_b_dt": rows(a[m0 + "b_dt"]),
        "mamba_A_log": rows(a[m0 + "A_log"]),
        "mamba_D_param": rows(a[m0 + "D_param"]),
        "mamba_W_out": rows(a[m0 + "W_out"].T),
        "moe0_router_w": rows(a[f0 + "router_w"]),
        "moe0_router_b": a[f0 + "router_b"],
        "moe0_w1": rows(a[f0 + "w1"].swapaxes(0, 1)),
        "moe0_b1": rows(a[f0 + "b1"].T),
        "moe0_gate": rows(a[f0 + "gate"].T),
        "moe0_w2": rows(a[f0 + "w2"].swapaxes(0, 1)),
        "moe0_b2": a[f0 + "b2"].reshape(-1),
        "moe0_sw1": rows(a[f0 + "sw1"]),
        "moe0_sb1": rows(a[f0 + "sb1"]),
        "moe0_sgate": rows(a[f0 + "sgate"]),
        "moe0_sw2": rows(a[f0 + "sw2"]),
        "moe0_sb2": a[f0 + "sb2"],
        "moe0_shared_weight": a[f0 + "shared_weight"].reshape(1),
        "moe0_ln_g": a[f0 + "ln_g"],
        "moe0_ln_b": a[f0 + "ln_b"],
        "att_Wqa": rows(a[t1 + "Wqa"]),
        "att_Wkva": rows(a[t1 + "Wkva"]),
        "att_Wqb": np.stack([a[t1 + "Wqb"][:, by_r], a[t1 + "Wqb"][:, swapped[by_r]]], 1),
        "att_Wk": np.concatenate([wk, wk], 2),
        "att_Wv": kv[:, :, 1],
        "att_Wout": rows(a[t1 + "Wout"]),
        "att_bout": a[t1 + "bout"],
        "att_rope_q": rope_tables(P, float(HEAD_DIM) ** -0.5),
        "att_rope_k": rope_tables(P, 1.0),
        "att_key_head": (np.arange(P)[:, None] % kv_width // HEAD_DIM == np.arange(KV_HEADS)).astype(np.float32),
        "moe1_router_w": rows(a[f1 + "w_gate"]),
        "moe1_router_b": a[f1 + "b_gate"],
        "moe1_w1": rows(a[f1 + "W1"].swapaxes(0, 1)),
        "moe1_b1": rows(a[f1 + "b1"].T),
        "moe1_w2": rows(a[f1 + "W2"].swapaxes(0, 1)),
        "moe1_b2": a[f1 + "b2"].reshape(-1),
    }


def program(nc, arrays, stages=9):
    args = {}
    for name, a in arrays.items():
        args[name[3:]] = nc.dram_tensor(name, a.shape, mybir.dt.from_np(a.dtype), kind="ExternalInput").ap()
    out = nc.dram_tensor("out", (TILES, P, DIM), F32, kind="ExternalOutput").ap()
    build(nc, args, out, stages)


def kernel(**inputs):
    import concourse.bacc as bacc
    from concourse.bass_utils import run_bass_kernel_spmd

    arrays = {"in_" + k: np.ascontiguousarray(v) for k, v in host_layout(inputs).items()}
    nc = bacc.Bacc("TRN2", target_bir_lowering=False, num_devices=1)
    program(nc, arrays)
    result = run_bass_kernel_spmd(nc, [arrays], core_ids=[0])
    return result.results[0]["out"]
```

```python
from contextlib import ExitStack

import numpy as np

import concourse.bass as bass
from concourse import mybir

F32 = mybir.dt.float32
BF16 = mybir.dt.bfloat16
I32 = mybir.dt.int32
U32 = mybir.dt.uint32
ALU = mybir.AluOpType
ACT = mybir.ActivationFunctionType
AXX = mybir.AxisListType.X

P = 128
TILES = 16
TOKENS = TILES * P
DIM = 256
KC = DIM // P
SEQ_PER_GROUP = 4
GROUPS = TILES // SEQ_PER_GROUP
GT = SEQ_PER_GROUP * P
EPS = 1e-5

CUTOFFS = (0, 5000, 20000, 50000)
EMB_WIDTHS = (256, 64, 16)
EMB_STARTS = (0, 256, 320)
EMB_DIM = 336
EMB_CHUNKS = ((0, 128), (128, 128), (256, 80))

INNER = 512
DC = INNER // P
STATE = 16
TAPS = 4
DT_RANK = 32
SQ = 4
NQ = STATE // SQ

EXPERTS = 8
FF = 1024
FC = FF // P
SHARED_FF = 512
SC = SHARED_FF // P

HEADS = 16
KV_HEADS = 4
HEAD_DIM = 16


def nth(i, per, k=0):
    return i * per + k + 1


class Chain:

    def __init__(self, eng, sem, first=0):
        self.eng, self.sem, self.first, self.n = eng, sem, first, 0

    def __call__(self, ins, wait=True):
        ins.then_inc(self.sem, 1)
        self.n += 1
        if wait:
            self.eng.wait_ge(self.sem, self.first + self.n)


class Memory:

    def __init__(self, nc, ctx, stage):
        self.nc, self.ctx, self.stage = nc, ctx, stage

    def sb(self, name, shape, dt=F32):
        return self.ctx.enter_context(self.nc.sbuf_tensor(f"{self.stage}_{name}", shape, dt))

    def ps(self, name, shape, dt=F32):
        return self.ctx.enter_context(self.nc.psum_tensor(f"{self.stage}_{name}", shape, dt))

    def sem(self, name):
        return self.ctx.enter_context(self.nc.semaphore(f"{self.stage}_{name}"))


RSQRT_LINKS = 12


def rsqrt_newton(dve, link, out, var, half):
    link(dve.tensor_scalar(var, var, EPS, None, ALU.add))
    link(dve.tensor_scalar(half.bitcast(I32), var.bitcast(I32), 1, None, ALU.logical_shift_right))
    link(dve.tensor_scalar(out.bitcast(I32), half.bitcast(I32), -1.0, float(0x5F3759DF), ALU.mult, ALU.add))
    for _ in range(3):
        link(dve.scalar_tensor_tensor(half, out, -0.5, out, ALU.mult, ALU.mult))
        link(dve.tensor_tensor(half, half, var, ALU.mult))
        link(dve.scalar_tensor_tensor(out, half, 1.5, out, ALU.add, ALU.mult))


def norm_links(n):
    return 2 * n + 6 + RSQRT_LINKS


def norm_statistics(dve, link, ins, stats, mean_var, rstd, half):
    n, width = len(ins), ins[0].shape[-1]
    for i, x in enumerate(ins):
        link(dve.bn_stats(stats[:, i, :], x), wait=i == n - 1)
    mean, var, even_odd = mean_var[:, 0, 0:n], mean_var[:, 1, 0:n], mean_var[:, 2, 0:n]
    link(dve.tensor_tensor(mean, stats[:, 0:n, 1], stats[:, 0:n, 4], ALU.add))
    link(dve.tensor_scalar(mean, mean, 0.5, None, ALU.mult))
    link(dve.tensor_tensor(even_odd, stats[:, 0:n, 1], stats[:, 0:n, 4], ALU.subtract))
    link(dve.scalar_tensor_tensor(even_odd, even_odd, 0.25, even_odd, ALU.mult, ALU.mult))
    link(dve.tensor_tensor(var, stats[:, 0:n, 2], stats[:, 0:n, 5], ALU.add))
    link(dve.scalar_tensor_tensor(var, var, 1.0 / width, even_odd, ALU.mult, ALU.add))
    rsqrt_newton(dve, link, rstd[:, 0:n], var, half[:, 0:n])
    return mean, rstd


def layer_norm(dve, link, outs, ins, *scratch):
    mean, rstd = norm_statistics(dve, link, ins, *scratch)
    n = len(ins)
    for i, x in enumerate(ins):
        link(dve.tensor_scalar(outs[i], x, mean[:, i:i + 1], rstd[:, i:i + 1], ALU.subtract, ALU.mult), wait=i == n - 1)


def norm_scratch(mem, n):
    return (mem.sb("stats", [P, n, 6]), mem.sb("mean_var", [P, 3, n]), mem.sb("rstd", [P, n]), mem.sb("half", [P, n]))


def make_constants(nc, ctx):
    mem = Memory(nc, ctx, "const")
    ident = mem.sb("ident", [P, P])
    made = mem.sem("made")
    with nc.Block() as block:
        @block.gpsimd
        def _(pool):
            pool.memset(ident[:, :], 0.0).then_inc(made, 1)
            pool.wait_ge(made, 1)
            pool.affine_select(out=ident[:, :], in_=ident[:, :], compare_op=ALU.not_equal, fill=1.0,
                               base=0, pattern=[[-1, P]], channel_multiplier=1).then_inc(made, 1)
            pool.wait_ge(made, 2)
    return ident


class Embedding:
    RING = 4

    def __init__(self, nc, ctx, h, ident, token_ids, tables, projections, space):
        mem = Memory(nc, ctx, "emb")
        self.h, self.ident, self.token_ids, self.tables, self.projections = h, ident, token_ids, tables, projections
        self.turned, self.product = space[:, 0, :], space[:, 1, :]
        self.ids = mem.sb("ids", [P, TILES], I32)
        self.rows = mem.sb("rows", [P, 3, TILES], I32)
        self.emb = mem.sb("emb", [P, self.RING, EMB_DIM])
        self.proj = mem.sb("proj", [P, 3, DIM])
        self.emb_t = mem.sb("emb_t", [P, 3, P])
        self.ids_in, self.proj_in = mem.sem("ids_in"), mem.sem("proj_in")
        self.cleared, self.rows_ready = mem.sem("cleared"), mem.sem("rows_ready")
        self.gathered = [mem.sem(f"gathered{n}") for n in range(self.RING)]
        self.transposed, self.copied, self.projected, self.stored = (
            mem.sem(n) for n in ("transposed", "copied", "projected", "stored"))

    def load(self, sp):
        sp.dma_start(self.ids[:, :], self.token_ids).then_inc(self.ids_in, 16)
        for c, (a, n) in enumerate(EMB_CHUNKS):
            sp.dma_start(self.proj[0:n, c, :], self.projections[a:a + n, :]).then_inc(self.proj_in, 16)

    def number_rows(self, dve):
        dve.memset(self.emb[:, :, :], 0.0).then_inc(self.cleared, 1)
        dve.wait_ge(self.ids_in, 16)
        for i in range(3):
            dve.tensor_scalar(self.rows[:, i, :], self.ids[:, :], float(-CUTOFFS[i]), None, ALU.add).then_inc(self.rows_ready, 1)

    def gather(self, pool, tiles):
        pool.wait_ge(self.rows_ready, 3)
        for s in tiles:
            if s >= self.RING:
                pool.wait_ge(self.transposed, s - self.RING + 1)
                pool.memset(self.emb[:, s % self.RING, :], 0.0).then_inc(self.cleared, 1)
            pool.wait_ge(self.cleared, max(1, s - self.RING + 2))
            for i in range(3):
                a, n = EMB_STARTS[i], EMB_WIDTHS[i]
                pool.indirect_dma_start(
                    self.emb[:, s % self.RING, a:a + n], None, self.tables[i],
                    bass.IndirectOffsetOnAxis(self.rows[:, i, s:s + 1].bitcast(U32), 0),
                    bounds_check=CUTOFFS[i + 1] - CUTOFFS[i] - 1, oob_is_err=False,
                ).then_inc(self.gathered[s % self.RING], 16)

    def turn(self, pe, s):
        pe.wait_ge(self.gathered[s % self.RING], 16 * 3 * (s // self.RING + 1))
        if s >= 1:
            pe.wait_ge(self.copied, 2 * s)
        for c, (a, n) in enumerate(EMB_CHUNKS):
            ins = pe.transpose(self.turned[0:n, c * P:(c + 1) * P], self.emb[:, s % self.RING, a:a + n], self.ident[:, :])
        ins.then_inc(self.transposed, 1)

    def project(self, pe, s):
        if s == 0:
            pe.wait_ge(self.proj_in, 16 * len(EMB_CHUNKS))
        else:
            pe.wait_ge(self.stored, s)
        pe.wait_ge(self.copied, 2 * s + 2)
        for c, (a, n) in enumerate(EMB_CHUNKS):
            ins = pe.matmul(self.product[:, 0:DIM], self.emb_t[0:n, c, :], self.proj[0:n, c, :],
                            start=(c == 0), stop=(c == 2))
        ins.then_inc(self.projected, 1)

    def copy(self, act, s):
        act.wait_ge(self.transposed, s + 1)
        if s >= 1:
            act.wait_ge(self.projected, s)
        act.activation(self.emb_t[:, 0:2, :], self.turned[:, 0:2 * P].rearrange("p (c n) -> p c n", c=2), ACT.Copy)\
           .then_inc(self.copied, 1)
        act.activation(self.emb_t[0:80, 2, :], self.turned[0:80, 2 * P:3 * P], ACT.Copy).then_inc(self.copied, 1)

    def store(self, act, s):
        act.wait_ge(self.projected, s + 1)
        act.activation(self.h[:, s, :], self.product[:, 0:DIM], ACT.Copy, scale=16.0).then_inc(self.stored, 1)


def mamba(nc, h, ident, w, bc_dram, token_ids, tables, projections, next_weights):
    with ExitStack() as ctx:
        mem = Memory(nc, ctx, "mam")
        S = SEQ_PER_GROUP
        UNITS = NQ * DC
        RING = 4
        w_in = mem.sb("w_in", [P, KC, 2 * INNER])
        w_x = mem.sb("w_x", [P, DC, DT_RANK + 2 * STATE])
        w_dt = mem.sb("w_dt", [DT_RANK, INNER])
        w_out = mem.sb("w_out", [P, DC, DIM])
        gamma, beta = mem.sb("gamma", [P, KC]), mem.sb("beta", [P, KC])
        conv_w, conv_b = mem.sb("conv_w", [P, DC, TAPS]), mem.sb("conv_b", [P, DC])
        b_dt, skip = mem.sb("b_dt", [P, DC]), mem.sb("skip", [P, DC])
        skip_diag = mem.sb("skip_diag", [P, DC, P])
        a_log, decay = mem.sb("a_log", [P, DC, STATE]), mem.sb("decay", [P, DC, STATE])

        xa = mem.sb("xa", [P, S, DIM])
        xn_t = mem.sb("xn_t", [P, KC, GT])
        xs = mem.sb("xs", [P, DC, S, TAPS - 1 + P])
        taps = mem.sb("taps", [P, DC, TAPS, P])
        x_proj = mem.sb("x_proj", [DT_RANK + 2 * STATE, GT])
        soft = mem.sb("soft", [P, 2, GT])
        xn = soft[:, :, :].rearrange("p c t -> p (c t)").rearrange("p (s d) -> p s d", d=DIM)
        delta = mem.sb("delta", [P, DC, GT])
        delta_u = mem.sb("delta_u", [P, DC, GT])
        u = mem.sb("u", [P, DC, GT])
        silu_z = mem.sb("silu_z", [P, DC, GT])
        bc = mem.sb("bc", [P, 2, 2, SQ, GT])
        da = mem.sb("da", [P, 2, SQ, GT])
        hs = mem.sb("hs", [P, RING, SQ, GT])
        y = silu_z
        stats, mean_var, rstd, half = norm_scratch(mem, S)

        bank = mem.ps("bank", [P, 2, 512])
        wide = mem.ps("wide", [P, 2, 512])
        y_ps = mem.ps("y_ps", [P, DC, 512])
        embedding = Embedding(nc, ctx, h, ident, token_ids, tables, projections, wide)

        weights_in = mem.sem("weights_in")
        decay_ready = mem.sem("decay_ready")
        pre_chain, fed, out_chain = (
            mem.sem(n) for n in ("pre_chain", "fed", "out_chain"))
        stats_ready, guessed, pool_chain = mem.sem("stats_ready"), mem.sem("guessed"), mem.sem("pool_chain")
        xn_ready, xn_transposed, xn_t_ready = mem.sem("xn_ready"), mem.sem("xn_transposed"), mem.sem("xn_t_ready")
        xz_ready = mem.sem("xz_ready")
        bank_free = [mem.sem(f"bank_free{b}") for b in range(2)]
        wide_free = mem.sem("wide_free")
        xs_ready, conv_ready, u_ready, z_ready = (mem.sem(n) for n in ("xs_ready", "conv_ready", "u_ready", "z_ready"))
        proj_ready, proj_copied = mem.sem("proj_ready"), mem.sem("proj_copied")
        bc_written, bc_in, bc_free = mem.sem("bc_written"), [mem.sem("bc_in0"), mem.sem("bc_in1")], mem.sem("bc_free")
        pre_delta, log_ready = mem.sem("pre_delta"), mem.sem("log_ready")
        act_chain = mem.sem("act_chain")
        delta_ready = mem.sem("delta_ready")
        da_ready, scanned, hc_ready, summed = (mem.sem(n) for n in ("da_ready", "scanned", "hc_ready", "summed"))
        y_free, y_ready, out_ready = mem.sem("y_free"), mem.sem("y_ready"), mem.sem("out_ready")
        diag_ready = mem.sem("diag_ready")

        BANK_USES = (9, 8)
        PRE_LINKS = 3 * S + DC
        VARIANCE_LINKS, POOL_LINKS = 8, 12
        ACT_LINKS = 3 * DC

        def by_seq(v):
            return v.rearrange("p (s t) -> p s t", t=P)

        def h_tiles(g):
            return [h[:, bass.ds(g * S + s, 1), :].rearrange("p a d -> p (a d)") for s in range(S)]

        def through(first, end):
            return [(s if s < end else None, s - 1 if s > first else None) for s in range(first, end + 1)]

        def at(slots, pairs):
            spread = {n: [pair] for n, pair in zip(slots, pairs)}
            spread[slots[-1]] += pairs[len(slots):]
            return spread

        def run_groups(eng, unit, prepare, beside, tail, embed_first=(None, None), embed_before={}, embed_in_first={},
                       start=None):
            enter, leave = embed_first

            def embed(pairs):
                for entering, leaving in pairs:
                    if entering is not None:
                        enter(eng, entering)
                    if leaving is not None:
                        leave(eng, leaving)

            def group(g, first, last):
                for n in range(UNITS):
                    unit(g, n)
                    if not first and n in tail:
                        tail[n](g - 1)
                    for step in beside.get(n, ()):
                        step(g)
                    if not last:
                        for step in prepare.get(n, ()):
                            step(g + 1)
                    if first:
                        embed(embed_in_first.get(n, ()))

            if enter:
                embed(through(0, S))
            for n in range(UNITS):
                for step in prepare.get(n, ()):
                    step(0)
                embed(embed_before.get(n, ()))
            if start:
                start()
            group(0, True, False)
            with eng.Fori(1, GROUPS - 1) as g:
                group(g, False, False)
            group(GROUPS - 1, False, True)
            for n in sorted(tail):
                tail[n](GROUPS - 1)

        with nc.Block() as block:
            @block.sync
            def _(sp):
                embedding.load(sp)
                for dst, src in ((w_in[:, :, :], w["W_in"]), (w_x[:, :, :], w["W_xproj"]), (w_dt[:, :], w["W_dt"]),
                                 (w_out[:, :, :], w["W_out"]), (gamma[:, :], w["ln_gamma"]), (beta[:, :], w["ln_beta"]),
                                 (conv_w[:, :, :], w["conv_w"]), (conv_b[:, :], w["conv_b"]), (b_dt[:, :], w["b_dt"]),
                                 (skip[:, :], w["D_param"]), (a_log[:, :, :], w["A_log"])):
                    sp.dma_start(dst, src).then_inc(weights_in, 16)
                next_weights.start_loads(sp)
                sp.sem_inc(bc_free, 2)
                with sp.Fori(0, GROUPS) as g:
                    sp.wait_ge(bc_written, 16 * g + 16)
                    for q in range(NQ):
                        sp.wait_ge(bc_free, nth(g, NQ, q))
                        for k in range(2):
                            row = k * STATE + q * SQ
                            src = bc_dram[bass.ds(g, 1), row:row + SQ, :].rearrange("g r t -> (g r t)")
                            sp.dma_start(bc[:, q % 2, k, :, :].rearrange("p r t -> p (r t)"),
                                         src.partition_broadcast(P)).then_inc(bc_in[q % 2], 16)

            @block.gpsimd
            def _(pool):
                def write_bc(g):
                    pool.wait_ge(proj_copied, nth(g, 1))
                    pool.dma_start(bc_dram[bass.ds(g, 1), :, :].rearrange("g r t -> (g r) t"),
                                   x_proj[DT_RANK:, :]).then_inc(bc_written, 16)

                def norms(g):
                    for k in range(2):
                        link = Chain(pool, pool_chain, (g * 2 + k) * POOL_LINKS)
                        pool.wait_ge(stats_ready, nth(g, 2, k))
                        mean, var, even_odd = (mean_var[:, n, :] for n in range(3))
                        link(pool.tensor_tensor(mean, stats[:, :, 1], stats[:, :, 4], ALU.add))
                        link(pool.tensor_scalar(mean, mean, 0.5, None, ALU.mult))
                        link(pool.tensor_tensor(even_odd, stats[:, :, 1], stats[:, :, 4], ALU.subtract))
                        link(pool.tensor_tensor(even_odd, even_odd, even_odd, ALU.mult))
                        link(pool.tensor_scalar(even_odd, even_odd, 0.25, None, ALU.mult))
                        link(pool.tensor_tensor(var, stats[:, :, 2], stats[:, :, 5], ALU.add))
                        link(pool.tensor_scalar(var, var, 1.0 / DIM, EPS, ALU.mult, ALU.add))
                        link(pool.tensor_tensor(var, var, even_odd, ALU.add))
                        assert link.n == VARIANCE_LINKS
                        pool.wait_ge(guessed, nth(g, 4, 2 * k + 1))
                        link(pool.tensor_tensor(half[:, :], rstd[:, :], rstd[:, :], ALU.mult))
                        link(pool.tensor_tensor(half[:, :], half[:, :], var, ALU.mult))
                        link(pool.tensor_scalar(half[:, :], half[:, :], -0.5, 1.5, ALU.mult, ALU.add))
                        link(pool.tensor_tensor(rstd[:, :], rstd[:, :], half[:, :], ALU.mult))
                        assert link.n == POOL_LINKS

                embedding.gather(pool, range(2 * S))
                norms(0)
                write_bc(0)
                embedding.gather(pool, range(2 * S, 3 * S))
                norms(1)
                embedding.gather(pool, range(3 * S, TILES))
                write_bc(1)
                for g in range(2, GROUPS):
                    norms(g)
                    write_bc(g)

            @block.tensor
            def _(pe):
                def take(g, b, use):
                    pe.wait_ge(bank_free[b], nth(g, BANK_USES[b], use))

                def transpose_x(g):
                    if isinstance(g, int) and g == 0:
                        pe.wait_ge(weights_in, 16 * 11)
                    pe.wait_ge(xn_ready, nth(g, 1))
                    if isinstance(g, int):
                        pe.wait_ge(embedding.stored, (g + 1) * S)
                    pe.wait_ge(wide_free, 1 if isinstance(g, int) and g == 0 else 2 * g)
                    for k in range(KC):
                        for s in range(S):
                            ins = pe.transpose(wide[:, k, s * P:(s + 1) * P], xn[:, s, k * P:(k + 1) * P], ident[:, :])
                    ins.then_inc(xn_transposed, 1)

                def in_product(c):
                    def step(g):
                        if c == 0:
                            pe.wait_ge(xn_t_ready, nth(g, KC, KC - 1))
                        take(g, c % 2, c // 2 if c < DC else 7 - c % 2 + (c - DC) // 2)
                        for k in range(KC):
                            ins = pe.matmul(bank[:, c % 2, :], w_in[:, k, c * P:(c + 1) * P], xn_t[:, k, :],
                                            start=(k == 0), stop=(k == KC - 1))
                        ins.then_inc(xz_ready, 1)
                    return step

                def convolve(c):
                    def step(g):
                        pe.wait_ge(xs_ready, nth(g, DC, c))
                        take(g, c % 2, 2 + c // 2)
                        for k in range(TAPS):
                            ins = pe.matmul(bank[:, c % 2, :], taps[:, c, k, :], xs[:, c, :, k:k + P],
                                            start=(k == 0), stop=(k == TAPS - 1))
                        ins.then_inc(conv_ready, 1)
                    return step

                def bc_dt_product(g):
                    pe.wait_ge(u_ready, nth(g, DC, DC - 1))
                    take(g, 0, 4)
                    for c in range(DC):
                        ins = pe.matmul(bank[0:DT_RANK + 2 * STATE, 0, :], w_x[:, c, :], u[:, c, :],
                                        start=(c == 0), stop=(c == DC - 1))
                    ins.then_inc(proj_ready, 1)

                def delta_product(c):
                    def step(g):
                        if c == 0:
                            pe.wait_ge(proj_copied, nth(g, 1))
                        take(g, c % 2, 5 - c % 2 + c // 2)
                        pe.matmul(bank[:, c % 2, :], w_dt[:, c * P:(c + 1) * P], x_proj[0:DT_RANK, :],
                                  start=True, stop=True).then_inc(pre_delta, 1)
                    return step

                def unit(g, n):
                    q, c = divmod(n, DC)
                    if q == 0:
                        pe.wait_ge(y_free, nth(g, DC, c))
                    pe.wait_ge(hc_ready, nth(g, UNITS, n))
                    if q == 0:
                        pe.matmul(y_ps[:, c, :], skip_diag[:, c, :], u[:, c, :], start=True, stop=False)
                    for i in range(SQ):
                        ins = pe.matmul(y_ps[:, c, :], ident[:, :], hs[:, n % RING, i, :],
                                        start=False, stop=(q == NQ - 1 and i == SQ - 1))
                    ins.then_inc(summed, 1)

                def out_product(g):
                    pe.wait_ge(y_ready, nth(g, DC, DC - 1))
                    pe.wait_ge(embedding.stored, TILES)
                    pe.wait_ge(wide_free, 2 * g + 2 if isinstance(g, int) and g == GROUPS - 1 else 2 * g + 3)
                    for s in range(S):
                        for c in range(DC):
                            ins = pe.matmul(wide[:, s // 2, (s % 2) * DIM:(s % 2 + 1) * DIM],
                                            y[:, c, s * P:(s + 1) * P], w_out[:, c, :],
                                            start=(c == 0), stop=(c == DC - 1))
                    ins.then_inc(out_ready, 1)

                def embed_turn(pe, s):
                    if s == S or s == 2 * S:
                        pe.wait_ge(wide_free, s // S + 1)
                    embedding.turn(pe, s)

                pe.wait_ge(diag_ready, 2 + DC * (1 + TAPS))
                run_groups(pe, unit,
                           {3: [transpose_x], 4: [in_product(0), in_product(1)], 5: [in_product(2), in_product(3)],
                            6: [convolve(0)], 7: [convolve(1)], 8: [convolve(2)], 9: [convolve(3)],
                            11: [bc_dt_product], 12: [delta_product(0), delta_product(1)],
                            13: [delta_product(2), delta_product(3)]},
                           {0: [in_product(4), in_product(5)], 2: [in_product(6), in_product(7)]},
                           {0: out_product}, (embed_turn, embedding.project),
                           at(range(4, 9), through(S, 2 * S)), at(range(6, 15), through(2 * S, TILES)))

            @block.scalar
            def _(act):
                act.wait_ge(weights_in, 16 * 11)
                act.preload_act_table_set("natural_log_exp_and_others")
                act.activation(decay[:, :, :], a_log[:, :, :], ACT.Exp).then_inc(decay_ready, 1)

                def guess(k):
                    def step(g):
                        act.wait_ge(pool_chain, (g * 2 + k) * POOL_LINKS + VARIANCE_LINKS)
                        act.activation(half[:, :], mean_var[:, 1, :], ACT.Ln).then_inc(guessed, 1)
                        act.wait_ge(guessed, nth(g, 4, 2 * k))
                        act.activation(rstd[:, :], half[:, :], ACT.Exp, scale=-0.5).then_inc(guessed, 1)
                    return step

                def keep_x(g):
                    act.wait_ge(xn_transposed, nth(g, 1))
                    for k in range(KC):
                        act.activation(xn_t[:, k, :], wide[:, k, :], ACT.Identity, bias=beta[:, k:k + 1],
                                       scale=gamma[:, k:k + 1]).then_inc(xn_t_ready, 1)
                    act.wait_ge(xn_t_ready, nth(g, KC, KC - 1))
                    act.sem_inc(wide_free, 1)

                def keep_xs(c):
                    def step(g):
                        act.wait_ge(xz_ready, nth(g, 2 * DC, c))
                        act.activation(xs[:, c, :, TAPS - 1:], by_seq(bank[:, c % 2, :]), ACT.Copy).then_inc(xs_ready, 1)
                        act.wait_ge(xs_ready, nth(g, DC, c))
                        act.sem_inc(bank_free[c % 2], 1)
                    return step

                def silu_of_z(g):
                    for c in range(DC):
                        act.wait_ge(xz_ready, nth(g, 2 * DC, DC + c))
                        act.activation(silu_z[:, c, :], bank[:, c % 2, :], ACT.Silu).then_inc(z_ready, 1)
                        act.wait_ge(z_ready, nth(g, DC, c))
                        act.sem_inc(bank_free[c % 2], 1)
                    act.preload_act_table_set("natural_log_exp_and_others")

                def silu_of_x(chunks):
                    def step(g):
                        for c in chunks:
                            act.wait_ge(conv_ready, nth(g, DC, c))
                            act.activation(u[:, c, :], bank[:, c % 2, :], ACT.Silu, bias=conv_b[:, c:c + 1]).then_inc(u_ready, 1)
                            act.wait_ge(u_ready, nth(g, DC, c))
                            act.sem_inc(bank_free[c % 2], 1)
                        act.preload_act_table_set("natural_log_exp_and_others")
                    return step

                def keep_proj(g):
                    act.wait_ge(proj_ready, nth(g, 1))
                    if not isinstance(g, int) or g:
                        act.wait_ge(bc_written, 16 * g)
                    act.activation(x_proj[:, :], bank[0:DT_RANK + 2 * STATE, 0, :], ACT.Copy)\
                       .then_inc(proj_copied, 1)
                    act.wait_ge(proj_copied, nth(g, 1))
                    act.sem_inc(bank_free[0], 1)

                def softplus_terms(chunks):
                    def step(g):
                        for c in chunks:
                            link = Chain(act, act_chain, g * ACT_LINKS + 3 * c)
                            if not isinstance(g, int) or g:
                                act.wait_ge(da_ready, g * UNITS - (DC - 1) + c)
                            act.wait_ge(pre_delta, nth(g, DC, c))
                            if c >= 2:
                                act.wait_ge(delta_ready, nth(g, DC, c - 2))
                            act.activation(delta[:, c, :], bank[:, c % 2, :], ACT.Relu, bias=b_dt[:, c:c + 1])
                            link(act.activation(soft[:, c % 2, :], bank[:, c % 2, :], ACT.Abs, bias=b_dt[:, c:c + 1]))
                            act.sem_inc(bank_free[c % 2], 1)
                            link(act.activation(soft[:, c % 2, :], soft[:, c % 2, :], ACT.Exp, scale=-1.0))
                            link(act.activation(soft[:, c % 2, :], soft[:, c % 2, :], ACT.Ln, bias=1.0))
                            act.sem_inc(log_ready, 1)
                    return step

                def unit(g, n):
                    q, c = divmod(n, DC)
                    if q == 0:
                        act.wait_ge(delta_ready, nth(g, DC, c))
                    act.wait_ge(scanned, nth(g, UNITS, n))
                    for i in range(SQ):
                        ins = act.activation(by_seq(da[:, n % 2, i, :])[:, :, 1:], by_seq(delta[:, c, :])[:, :, 1:],
                                             ACT.Exp, scale=decay[:, c, q * SQ + i:q * SQ + i + 1])
                    ins.then_inc(da_ready, 1)

                run_groups(act, unit,
                           {2: [guess(0)], 3: [guess(1)], 5: [keep_x], 6: [keep_xs(0), keep_xs(1)], 7: [keep_xs(2), keep_xs(3)],
                            9: [silu_of_x((0, 1))], 11: [silu_of_x((2, 3))], 13: [keep_proj],
                            14: [softplus_terms((0, 1))], 15: [softplus_terms((2, 3))]},
                           {4: [silu_of_z]}, {}, (embedding.copy, embedding.store),
                           at(range(6, 10), through(S, 2 * S)), at(range(7, 16), through(2 * S, TILES)))

            @block.vector
            def _(dve):
                embedding.number_rows(dve)
                dve.memset(da[:, :, :, :], 0.0).then_inc(diag_ready, 1)
                dve.wait_ge(decay_ready, 1)
                dve.tensor_scalar(decay[:, :, :], decay[:, :, :], -1.0, None, ALU.mult).then_inc(decay_ready, 1)
                dve.wait_ge(decay_ready, 2)
                dve.memset(xs[:, :, :, 0:TAPS - 1], 0.0).then_inc(diag_ready, 1)
                dve.wait_ge(diag_ready, 2)
                for c in range(DC):
                    dve.tensor_scalar(skip_diag[:, c, :], ident[:, :], skip[:, c:c + 1], None, ALU.mult).then_inc(diag_ready, 1)
                    for k in range(TAPS):
                        dve.tensor_scalar(taps[:, c, k, :], ident[:, :], conv_w[:, c, k:k + 1], None, ALU.mult)\
                           .then_inc(diag_ready, 1)
                for b in range(2):
                    dve.sem_inc(bank_free[b], 1)
                dve.sem_inc(wide_free, 1)
                dve.sem_inc(y_free, DC)
                dve.sem_inc(scanned, 2)

                def take_stats(tiles):
                    for i, v in enumerate(tiles):
                        ins = dve.bn_stats(stats[:, i, :], v)
                    ins.then_inc(stats_ready, 1)

                def apply_norm(g, k, outs, tiles, link):
                    dve.wait_ge(pool_chain, (g * 2 + k + 1) * POOL_LINKS)
                    for i, v in enumerate(tiles):
                        link(dve.tensor_scalar(outs[i], v, mean_var[:, 0, i:i + 1], rstd[:, i:i + 1], ALU.subtract, ALU.mult),
                             wait=i == S - 1)

                xa_tiles, xn_tiles = [xa[:, s, :] for s in range(S)], [xn[:, s, :] for s in range(S)]

                def stats_of_h(g):
                    dve.wait_ge(embedding.stored, g * S + S)
                    take_stats(h_tiles(g))

                def norm_h(g):
                    apply_norm(g, 0, xa_tiles, h_tiles(g), Chain(dve, pre_chain, g * PRE_LINKS))
                    take_stats(xa_tiles)

                def norm_x(g):
                    link = Chain(dve, pre_chain, g * PRE_LINKS + S)
                    apply_norm(g, 1, xn_tiles, xa_tiles, link)
                    dve.sem_inc(xn_ready, 1)
                    for s, h_s in enumerate(h_tiles(g)):
                        link(dve.tensor_tensor(h_s, h_s, xa[:, s, :], ALU.add), wait=s == S - 1)

                def softplus(chunks):
                    def step(g):
                        for c in chunks:
                            link = Chain(dve, pre_chain, (g + 1) * PRE_LINKS - DC + c)
                            dve.wait_ge(log_ready, nth(g, DC, c))
                            dve.tensor_tensor(delta[:, c, :], delta[:, c, :], soft[:, c % 2, :], ALU.add)\
                               .then_inc(delta_ready, 1)
                            dve.wait_ge(delta_ready, nth(g, DC, c))
                            link(dve.tensor_tensor(delta_u[:, c, :], delta[:, c, :], u[:, c, :], ALU.mult))
                    return step

                def feed(g, n):
                    q, c = divmod(n, DC)
                    if c == 0:
                        dve.wait_ge(bc_in[q % 2], 32 * (g * (NQ // 2) + q // 2 + 1))
                    if n >= RING:
                        dve.wait_ge(summed, nth(g, UNITS, n - RING))
                    elif not isinstance(g, int) or g:
                        dve.wait_ge(summed, g * UNITS + n - RING + 1)
                    dve.tensor_tensor(hs[:, n % RING, :, :], delta_u[:, c, :].unsqueeze(1).to_broadcast([P, SQ, GT]),
                                      bc[:, q % 2, 0, :, :], ALU.mult).then_inc(fed, 1)

                def unit(g, n):
                    q, c = divmod(n, DC)
                    flat = hs[:, n % RING, :, :].rearrange("p i t -> p (i t)")
                    dve.wait_ge(fed, nth(g, UNITS, n))
                    dve.wait_ge(da_ready, nth(g, UNITS, n))
                    dve.tensor_tensor_scan(flat, da[:, n % 2, :, :].rearrange("p i t -> p (i t)"), flat,
                                           0.0, ALU.mult, ALU.add).then_inc(scanned, 1)
                    if n + 1 < UNITS:
                        feed(g, n + 1)
                    elif not isinstance(g, int) or g + 1 < GROUPS:
                        feed(g + 1, 0)
                    dve.wait_ge(scanned, nth(g, UNITS, n) + 2)
                    dve.tensor_tensor(hs[:, n % RING, :, :], hs[:, n % RING, :, :], bc[:, q % 2, 1, :, :], ALU.mult)\
                       .then_inc(hc_ready, 1)
                    if c == DC - 1:
                        dve.wait_ge(hc_ready, nth(g, UNITS, n))
                        dve.sem_inc(bc_free, 1)
                    if n == UNITS - 2:
                        gate(g, 0)
                    if n == UNITS - 1:
                        gate(g, 1)
                        gate(g, 2)

                def gate(g, c):
                    dve.wait_ge(summed, nth(g, UNITS, UNITS - DC + c))
                    if c == 0 or c == DC - 1:
                        dve.wait_ge(z_ready, nth(g, DC, c if c else DC - 2))
                    dve.tensor_tensor(y[:, c, :], y_ps[:, c, :], silu_z[:, c, :], ALU.mult).then_inc(y_ready, 1)
                    dve.wait_ge(y_ready, nth(g, DC, c))
                    dve.sem_inc(y_free, 1)

                def add_out(g):
                    link = Chain(dve, out_chain, g * S)
                    dve.wait_ge(out_ready, nth(g, 1))
                    for s, h_s in enumerate(h_tiles(g)):
                        link(dve.tensor_tensor(h_s, h_s, wide[:, s // 2, (s % 2) * DIM:(s % 2 + 1) * DIM], ALU.add),
                             wait=s == S - 1)
                    dve.sem_inc(wide_free, 1)

                run_groups(dve, unit,
                           {0: [stats_of_h], 1: [norm_h], 2: [norm_x], 14: [softplus((0, 1))], 15: [softplus((2, 3))]},
                           {}, {0: lambda g: gate(g, DC - 1), 1: add_out}, start=lambda: feed(0, 0))


def attention(nc, h, ident, w, next_weights):
    with ExitStack() as ctx:
        mem = Memory(nc, ctx, "att")
        q_cos, q_sin = mem.sb("q_cos", [P, KC, TOKENS]), mem.sb("q_sin", [P, KC, TOKENS])
        keys = mem.sb("keys", [P, TILES, KV_HEADS, P])
        v = mem.sb("v", [P, TILES, KV_HEADS, HEAD_DIM + 1])
        wout = mem.sb("wout", [P, KC, DIM])
        bout = mem.sb("bout", [P, DIM])
        ident_b = mem.sb("ident_b", [P, P], BF16)
        causal = mem.sb("causal", [P, KV_HEADS, P], BF16)
        attention_inputs(nc, h, ident, w, next_weights, q_cos, q_sin, keys, v, wout, bout, ident_b, causal)
        attention_heads(nc, h, ident, q_cos, q_sin, keys, v, wout, bout, ident_b, causal)


def attention_inputs(nc, h, ident, w, next_weights, q_cos, q_sin, keys, v, wout, bout, ident_b, causal):
    q_rank, kv_rank, kv_width = 64, 32, KV_HEADS * HEAD_DIM
    S = SEQ_PER_GROUP
    with ExitStack() as ctx:
        mem = Memory(nc, ctx, "qkv")
        wqa, wkva = mem.sb("wqa", [P, KC, q_rank]), mem.sb("wkva", [P, KC, kv_rank])
        wqb = mem.sb("wqb", [q_rank, 2, DIM])
        wk = mem.sb("wk", [kv_rank, 2, 2 * kv_width])
        wv = mem.sb("wv", [kv_rank, kv_width])
        rope_q, rope_k = mem.sb("rope_q", [P, 2, P]), mem.sb("rope_k", [P, 2, P])
        key_head = mem.sb("key_head", [P, KV_HEADS])

        x = mem.sb("x", [P, S, DIM])
        x_t = mem.sb("x_t", [P, KC, GT])
        qa, kva = mem.sb("qa", [q_rank, GT]), mem.sb("kva", [kv_rank, GT])
        k_cos, k_sin = mem.sb("k_cos", [P, GT]), mem.sb("k_sin", [P, GT])
        scratch = norm_scratch(mem, S)

        xt_ps = mem.ps("xt_ps", [P, KC, 512])
        low_ps = mem.ps("low_ps", [P, 2, 512])
        qk_ps = mem.ps("qk_ps", [P, 2, 512])
        v_ps = mem.ps("v_ps", [P, 512])

        weights_in, constants = mem.sem("weights_in"), mem.sem("constants")
        norm_chain, keys_chain = mem.sem("norm_chain"), mem.sem("keys_chain")
        x_ready, x_turned, x_t_ready = mem.sem("x_ready"), mem.sem("x_turned"), mem.sem("x_t_ready")
        low_done, low_ready = mem.sem("low_done"), mem.sem("low_ready")
        qk_done, qk_used = mem.sem("qk_done"), mem.sem("qk_used")
        v_done, v_ready = mem.sem("v_done"), mem.sem("v_ready")

        USES = 2 * (KC + 1)
        loads = ((wqa[:, :, :], w["Wqa"]), (wkva[:, :, :], w["Wkva"]), (wqb[:, :, :], w["Wqb"]), (wk[:, :, :], w["Wk"]),
                 (wv[:, :], w["Wv"]), (wout[:, :, :], w["Wout"]), (bout[:, :], w["bout"].partition_broadcast(P)),
                 (rope_q[:, :, :], w["rope_q"]),
                 (rope_k[:, :, :], w["rope_k"]), (key_head[:, :], w["key_head"]))

        def by_seq(a):
            return a.rearrange("p (s t) -> p s t", t=P)

        with nc.Block() as block:
            @block.sync
            def _(sp):
                for dst, src in loads:
                    sp.dma_start(dst, src).then_inc(weights_in, 16)
                next_weights.start_loads(sp)

            @block.gpsimd
            def _(pool):
                pool.memset(v[:, :, :, :], 1.0).then_inc(constants, 1)
                pool.tensor_copy(ident_b[:, :], ident[:, :]).then_inc(constants, 1)
                pool.memset(causal[:, :, :], 0.0).then_inc(constants, 1)
                pool.wait_ge(constants, 3)
                pool.affine_select(out=causal[:, :, :], in_=causal[:, :, :], compare_op=ALU.is_ge, fill=-1e30, base=0,
                                   pattern=[[0, KV_HEADS], [-1, P]], channel_multiplier=1).then_inc(constants, 1)
                pool.wait_ge(constants, 4)

            @block.tensor
            def _(pe):
                pe.wait_ge(weights_in, 16 * len(loads))

                def turn(g):
                    pe.wait_ge(x_ready, nth(g, 1))
                    for k in range(KC):
                        for s in range(S):
                            ins = pe.transpose(xt_ps[:, k, s * P:(s + 1) * P], x[:, s, k * P:(k + 1) * P], ident[:, :])
                        ins.then_inc(x_turned, 1)

                def products(g):
                    pe.wait_ge(x_t_ready, nth(g, KC, KC - 1))
                    for b, (wgt, rank) in enumerate(((wqa, q_rank), (wkva, kv_rank))):
                        for k in range(KC):
                            ins = pe.matmul(low_ps[0:rank, b, :], wgt[:, k, :], x_t[:, k, :],
                                            start=(k == 0), stop=(k == KC - 1))
                        ins.then_inc(low_done, 1)
                    for c in range(KC + 1):
                        if c == 0 or c == KC:
                            pe.wait_ge(low_ready, nth(g, 2, min(c, 1)))
                        for b in range(2):
                            pe.wait_ge(qk_used, nth(g, USES, 2 * c + b))
                            if c < KC:
                                ins = pe.matmul(qk_ps[:, b, :], wqb[:, b, c * P:(c + 1) * P], qa[:, :], start=True, stop=True)
                            else:
                                ins = pe.matmul(qk_ps[:, b, :], wk[:, b, :], kva[:, :], start=True, stop=True)
                            ins.then_inc(qk_done, 1)
                    pe.wait_ge(v_ready, nth(g, 1))
                    for s in range(S):
                        ins = pe.matmul(v_ps[:, s * kv_width:(s + 1) * kv_width], kva[:, s * P:(s + 1) * P], wv[:, :],
                                        start=True, stop=True)
                    ins.then_inc(v_done, 1)

                turn(0)
                with pe.Fori(0, GROUPS - 1) as g:
                    products(g)
                    turn(g + 1)
                products(GROUPS - 1)

            @block.scalar
            def _(act):
                act.wait_ge(constants, 4)

                def keep_x(g):
                    for k in range(KC):
                        act.wait_ge(x_turned, nth(g, KC, k))
                        act.activation(x_t[:, k, :], xt_ps[:, k, :], ACT.Copy).then_inc(x_t_ready, 1)

                def keep_low(g):
                    for b, (dst, rank) in enumerate(((qa, q_rank), (kva, kv_rank))):
                        act.wait_ge(low_done, nth(g, 2, b))
                        act.activation(dst[:, :], low_ps[0:rank, b, :], ACT.Copy).then_inc(low_ready, 1)

                keep_x(0)
                with act.Fori(0, GROUPS - 1) as g:
                    keep_low(g)
                    keep_x(g + 1)
                keep_low(GROUPS - 1)

            @block.vector
            def _(dve):
                dve.sem_inc(qk_used, 2)
                dve.sem_inc(v_ready, 1)

                def normalise(g):
                    link = Chain(dve, norm_chain, g * norm_links(S))
                    h_tiles = [h[:, bass.ds(g * S + s, 1), :].rearrange("p a d -> p (a d)") for s in range(S)]
                    if not isinstance(g, int):
                        dve.wait_ge(x_turned, g * KC)
                    layer_norm(dve, link, [x[:, s, :] for s in range(S)], h_tiles, *scratch)
                    dve.sem_inc(x_ready, 1)

                def rotate(g):
                    for c in range(KC + 1):
                        for b, (q_part, k_part) in enumerate(((q_cos, k_cos), (q_sin, k_sin))):
                            to = q_part[:, c, bass.ds(g * GT, GT)] if c < KC else k_part[:, :]
                            dve.wait_ge(qk_done, nth(g, USES, 2 * c + b))
                            rope = rope_q if c < KC else rope_k
                            dve.tensor_tensor(by_seq(to), by_seq(qk_ps[:, b, :]),
                                              rope[:, b, :].unsqueeze(1).to_broadcast([P, S, P]), ALU.mult)\
                               .then_inc(qk_used, 1)

                def lay_keys(g):
                    link = Chain(dve, keys_chain, g * (1 + KV_HEADS))
                    dve.wait_ge(qk_used, nth(g, USES, USES - 1) + 2)
                    link(dve.tensor_tensor(k_cos[:, :], k_cos[:, :], k_sin[:, :], ALU.add))
                    for c in range(KV_HEADS):
                        link(dve.tensor_scalar(keys[:, bass.ds(g * S, S), c, :], by_seq(k_cos[:, :]),
                                               key_head[:, c:c + 1], None, ALU.mult), wait=c == KV_HEADS - 1)
                    dve.wait_ge(v_done, nth(g, 1))
                    dve.tensor_copy(v[:, bass.ds(g * S, S), :, 0:HEAD_DIM].rearrange("p s c d -> p (s c) d"),
                                    v_ps[:, 0:S * kv_width].rearrange("p (n d) -> p n d", d=HEAD_DIM)).then_inc(v_ready, 1)

                normalise(0)
                dve.wait_ge(weights_in, 16 * len(loads))
                dve.wait_ge(constants, 4)
                with dve.Fori(0, GROUPS - 1) as g:
                    normalise(g + 1)
                    rotate(g)
                    lay_keys(g)
                rotate(GROUPS - 1)
                lay_keys(GROUPS - 1)


def attention_heads(nc, h, ident, q_cos, q_sin, keys, v, wout, bout, ident_b, causal):
    reps = HEADS // KV_HEADS
    half = KV_HEADS * HEAD_DIM
    with ExitStack() as ctx:
        mem = Memory(nc, ctx, "heads")
        q = mem.sb("q", [P, 2, reps, P])
        top = mem.sb("top", [P, HEADS])
        prob = mem.sb("prob", [P, 2, HEADS, P])
        prob_t = mem.sb("prob_t", [P, reps, KV_HEADS, P])
        inverse = mem.sb("inverse", [P, HEADS])
        o = mem.sb("o", [P, DIM])
        o_t = mem.sb("o_t", [P, KC, P])

        s_ps = mem.ps("s_ps", [P, reps, KV_HEADS, P])
        pt_ps = mem.ps("pt_ps", [P, 2, 512])
        o_ps = mem.ps("o_ps", [P, 512])
        out_ps = mem.ps("out_ps", [P, 512])

        top_chain, o_chain, h_chain = mem.sem("top_chain"), mem.sem("o_chain"), mem.sem("h_chain")
        q_ready, scores_done, scores_free, shifted, prob_ready = (
            mem.sem(n) for n in ("q_ready", "scores_done", "scores_free", "shifted", "prob_ready"))
        prob_turned, prob_t_ready, prob_used = mem.sem("prob_turned"), mem.sem("prob_t_ready"), mem.sem("prob_used")
        o_ready, o_turned, o_t_ready = (mem.sem(n) for n in ("o_ready", "o_turned", "o_t_ready"))
        out_done, out_added = mem.sem("out_done"), mem.sem("out_added")

        def over_sequences(eng, body):
            body(0, 0, True, False)
            with eng.Fori(0, TILES // 2 - 2) as pair:
                body(pair * 2 + 1, 1, False, False)
                body(pair * 2 + 2, 0, False, False)
            for s in range(TILES - 3, TILES):
                body(s, s % 2, False, s == TILES - 1)

        with nc.Block() as block:
            @block.tensor
            def _(pe):
                def scores(s, b, part):
                    pe.wait_ge(q_ready, s * 2 + 3)
                    pe.wait_ge(scores_free, s * 2 + part + 1)
                    for r in range(part * 2, part * 2 + 2):
                        pe.matmul(s_ps[:, r, :, :].rearrange("p c k -> p (c k)"), ident_b[:, :],
                                  causal[:, :, :].rearrange("p c k -> p (c k)"), start=True, stop=False)
                        ins = pe.matmul(s_ps[:, r, :, :].rearrange("p c k -> p (c k)"), q[:, b, r, :],
                                        keys[:, bass.ds(s, 1), :, :].rearrange("p a c k -> p (a c k)"),
                                        start=False, stop=True)
                    ins.then_inc(scores_done, 1)

                def turn_prob(s, b, r, first):
                    if r >= 2 or not first:
                        pe.wait_ge(prob_t_ready, s * reps + r - 1)
                    for c in range(KV_HEADS):
                        ins = pe.transpose(pt_ps[:, r % 2, c * P:(c + 1) * P], prob[:, b, r * KV_HEADS + c, :], ident[:, :])
                    ins.then_inc(prob_turned, 1)

                def values(s, r):
                    pe.wait_ge(prob_t_ready, s * reps + r + 1)
                    for c in range(KV_HEADS):
                        head = c * reps + r
                        ins = pe.matmul(o_ps[:, head * 17:(head + 1) * 17], prob_t[:, r, c, :],
                                        v[:, bass.ds(s, 1), c, :].rearrange("p a d -> p (a d)"), start=True, stop=True)
                    ins.then_inc(prob_used, 1)

                def turn_o(s):
                    pe.wait_ge(o_ready, s + 1)
                    pe.wait_ge(out_added, s + 1)
                    for k in range(KC):
                        ins = pe.transpose(out_ps[:, k * P:(k + 1) * P], o[:, k * P:(k + 1) * P], ident[:, :])
                    ins.then_inc(o_turned, 1)

                def project(s):
                    pe.wait_ge(o_t_ready, s + 1)
                    for k in range(KC):
                        ins = pe.matmul(out_ps[:, 0:DIM], o_t[:, k, :], wout[:, k, :], start=(k == 0), stop=(k == KC - 1))
                    ins.then_inc(out_done, 1)

                def sequence(s, b, first, last):
                    for part in range(2):
                        pe.wait_ge(prob_ready, s * 2 + part + 1)
                        turn_prob(s, b, part * 2, first)
                        turn_prob(s, b, part * 2 + 1, first)
                        if not last:
                            scores(s + 1, 1 - b, part)
                        if part == 0 and not first:
                            turn_o(s - 1)
                        values(s, part * 2)
                        values(s, part * 2 + 1)
                        if part == 0 and not first:
                            project(s - 1)

                scores(0, 0, 0)
                scores(0, 0, 1)
                over_sequences(pe, sequence)
                turn_o(TILES - 1)
                project(TILES - 1)

            @block.scalar
            def _(act):
                def exponent(s, b, part):
                    act.wait_ge(shifted, s * 2 + part + 1)
                    flat = prob[:, b, part * 8:part * 8 + 8, :].rearrange("p n k -> p (n k)")
                    act.activation(flat, flat, ACT.Exp).then_inc(prob_ready, 1)

                def keep_prob(s, r, first):
                    act.wait_ge(prob_turned, s * reps + r + 1)
                    if not first:
                        act.wait_ge(prob_used, s * reps - reps + r + 1)
                    act.activation(prob_t[:, r, :, :].rearrange("p c q -> p (c q)"), pt_ps[:, r % 2, :], ACT.Copy)\
                       .then_inc(prob_t_ready, 1)

                def keep_o(s):
                    act.wait_ge(o_turned, s + 1)
                    act.activation(o_t[:, :, :].rearrange("p k n -> p (k n)"), out_ps[:, 0:DIM], ACT.Copy)\
                       .then_inc(o_t_ready, 1)

                def sequence(s, b, first, last):
                    keep_prob(s, 0, first)
                    keep_prob(s, 1, first)
                    exponent(s, b, 1)
                    if not first:
                        keep_o(s - 1)
                    keep_prob(s, 2, first)
                    keep_prob(s, 3, first)
                    if not last:
                        exponent(s + 1, 1 - b, 0)

                exponent(0, 0, 0)
                over_sequences(act, sequence)
                keep_o(TILES - 1)

            @block.vector
            def _(dve):
                dve.memset(q[:, :, :, :], 0.0).then_inc(q_ready, 1)
                dve.wait_ge(q_ready, 1)
                dve.sem_inc(scores_free, 2)
                dve.sem_inc(out_added, 1)

                def h_tile(s):
                    return h[:, bass.ds(s, 1), :].rearrange("p a d -> p (a d)")

                def add_q(s, b):
                    if not isinstance(s, int) or s >= 2:
                        dve.wait_ge(scores_done, s * 2 - 2)
                    for n in range(2):
                        rows, cols = slice(n * half, (n + 1) * half), bass.ds(s * P, P)
                        dve.tensor_tensor(q[rows, b, n::2, :], q_cos[rows, :, cols], q_sin[rows, :, cols],
                                          ALU.add).then_inc(q_ready, 1)

                def shift(s, b, part):
                    link = Chain(dve, top_chain, s * 2 + part)
                    heads = slice(part * 8, part * 8 + 8)
                    dve.wait_ge(scores_done, s * 2 + part + 1)
                    scores = s_ps[:, part * 2:part * 2 + 2, :, :].rearrange("p r c k -> p (r c) k")
                    link(dve.tensor_reduce(top[:, heads], scores, AXX, ALU.max))
                    if not isinstance(s, int) or s >= 2:
                        dve.wait_ge(prob_turned, s * reps - reps)
                    dve.tensor_tensor(prob[:, b, heads, :], scores, top[:, heads].unsqueeze(2).to_broadcast([P, 8, P]),
                                      ALU.subtract).then_inc(shifted, 1)
                    dve.wait_ge(shifted, s * 2 + part + 1)
                    dve.sem_inc(scores_free, 1)

                def divide(s, first):
                    link = Chain(dve, o_chain, s)
                    dve.wait_ge(prob_used, s * reps + reps)
                    o_all = o_ps[:, 0:HEADS * 17].rearrange("p (n d) -> p n d", d=17)
                    link(dve.reciprocal(inverse[:, :], o_all[:, :, HEAD_DIM]))
                    if not first:
                        dve.wait_ge(o_turned, s)
                    dve.tensor_tensor(o[:, :].rearrange("p (n d) -> p n d", d=HEAD_DIM), o_all[:, :, 0:HEAD_DIM],
                                      inverse[:, :].unsqueeze(2).to_broadcast([P, HEADS, HEAD_DIM]), ALU.mult)\
                       .then_inc(o_ready, 1)

                def add_out(s):
                    link = Chain(dve, h_chain, s)
                    link(dve.tensor_tensor(h_tile(s), h_tile(s), bout[:, :], ALU.add))
                    dve.wait_ge(out_done, s + 1)
                    dve.tensor_tensor(h_tile(s), h_tile(s), out_ps[:, 0:DIM], ALU.add).then_inc(out_added, 1)

                def sequence(s, b, first, last):
                    if not last:
                        shift(s + 1, 1 - b, 0)
                    if not isinstance(s, int) or s + 2 < TILES:
                        add_q(s + 2, b)
                    if not first:
                        add_out(s - 1)
                    if not last:
                        shift(s + 1, 1 - b, 1)
                    divide(s, first)

                add_q(0, 0)
                add_q(1, 1)
                shift(0, 0, 0)
                shift(0, 0, 1)
                over_sequences(dve, sequence)
                add_out(TILES - 1)


def most_tiles(choices):
    return (TOKENS * choices + EXPERTS * (P - 1)) // P


def over_tiles(eng, n, body):
    body(0, 0, True, False)
    with eng.Fori(0, (n - 3) // 2) as pair:
        body(pair * 2 + 1, 1, False, False)
        body(pair * 2 + 2, 0, False, False)
    body(n - 2, 1, False, False)
    body(n - 1, 0, False, True)


class EarlyWeights:

    def __init__(self, nc, ctx, w, shared, early_w1, stage):
        mem = Memory(nc, ctx, stage)
        self.router_w, self.router_b = mem.sb("router_w", [P, KC, EXPERTS]), mem.sb("router_b", [P, EXPERTS])
        self.b1, self.b2 = mem.sb("b1", [P, FC, EXPERTS]), mem.sb("b2", [P, EXPERTS, DIM])
        loads = [(self.router_w[:, :, :], w["router_w"]), (self.router_b[:, :], w["router_b"].partition_broadcast(P)),
                 (self.b1[:, :, :], w["b1"]),
                 (self.b2[:, :, :].rearrange("p e d -> p (e d)"), w["b2"].partition_broadcast(P))]
        if shared:
            self.gate = mem.sb("gate", [P, FC, EXPERTS])
            self.sw1, self.sw2 = mem.sb("sw1", [P, KC, SHARED_FF]), mem.sb("sw2", [P, SC, DIM])
            self.sb1, self.sgate = mem.sb("sb1", [P, SC]), mem.sb("sgate", [P, SC])
            self.sb2 = mem.sb("sb2", [P, DIM])
            self.ln_g, self.ln_b = mem.sb("ln_g", [P, DIM]), mem.sb("ln_b", [P, DIM])
            self.mix = mem.sb("mix", [P, 1])
            loads += [(self.gate[:, :, :], w["gate"]), (self.sw1[:, :, :], w["sw1"]), (self.sw2[:, :, :], w["sw2"]),
                      (self.sb1[:, :], w["sb1"]), (self.sgate[:, :], w["sgate"]),
                      (self.sb2[:, :], w["sb2"].partition_broadcast(P)),
                      (self.ln_g[:, :], w["ln_g"].partition_broadcast(P)), (self.ln_b[:, :], w["ln_b"].partition_broadcast(P)),
                      (self.mix[:, :], w["shared_weight"].partition_broadcast(P))]
        self.w1 = mem.sb("w1", [P, KC, EXPERTS, FF]) if early_w1 else None
        if early_w1:
            loads += [(self.w1[:, :, e, :], w["w1"][:, :, e, :]) for e in range(EXPERTS)]
        self.loads, self.loaded, self.all = loads, mem.sem("small_loaded"), 16 * len(loads)

    def start_loads(self, queue):
        for dst, src in self.loads:
            queue.dma_start(dst, src).then_inc(self.loaded, 16)


def moe(nc, h, ident, w, early, choices, slots, results, parked, stage, out=None):
    shared = choices == 2
    n_tiles = most_tiles(choices)
    pairs = choices * TILES
    router_w, router_b, b1, b2 = early.router_w, early.router_b, early.b1, early.b2
    if shared:
        gate, sw1, sw2, sb1, sgate, sb2 = early.gate, early.sw1, early.sw2, early.sb1, early.sgate, early.sb2
        ln_g, ln_b, mix = early.ln_g, early.ln_b, early.mix
    with ExitStack() as ctx:
        mem = Memory(nc, ctx, stage)
        x = mem.sb("x", [P, TILES, DIM])
        x_t = h[:, :, :].rearrange("p t d -> p (t d)").rearrange("p (g k n) -> p g k n", g=GROUPS, k=KC)
        w1 = early.w1 if early.w1 is not None else mem.sb("w1", [P, KC, EXPERTS, FF])
        w2 = mem.sb("w2", [P, FC, EXPERTS, DIM])
        ff = mem.sb("ff", [P, 2, FF])
        hidden = ff[:, 0, :]
        active = ff[:, 1, :].rearrange("p (f n) -> p f n", f=FC)
        shared_act = ff[:, :, :].rearrange("p a n -> p (a n)").rearrange("p (f n) -> p f n", f=SC)
        x_in, x_in_t, y_out = (mem.sb(n, [P, 2, DIM]) for n in ("x_in", "x_in_t", "y_out"))
        zeros = mem.sb("zeros", [P, DIM])
        lower, ones = mem.sb("lower", [P, P]), mem.sb("ones", [P, P])
        expert_no = mem.sb("expert_no", [P, EXPERTS])
        tile_no = mem.sb("tile_no", [1, n_tiles, EXPERTS])
        logits, top, top_i = mem.sb("logits", [P, TILES, EXPERTS]), mem.sb("top", [P, TILES, 8]), mem.sb("top_i", [P, TILES, 8], U32)
        top_f = mem.sb("top_f", [P, TILES, choices])
        total, weight = mem.sb("total", [P, TILES]), mem.sb("weight", [P, TILES, choices])
        onehot = mem.sb("onehot", [P, choices, TILES, EXPERTS])
        before = mem.sb("before", [P, choices, TILES, EXPERTS])
        counts = mem.sb("counts", [P, pairs, EXPERTS])
        running = mem.sb("running", [P, pairs, EXPERTS])
        tiles_i = mem.sb("tiles_i", [P, EXPERTS], I32)
        tiles_of, last_tile, base = (mem.sb(n, [P, EXPERTS]) for n in ("tiles_of", "last_tile", "base"))
        slot_f, slot = mem.sb("slot_f", [P, pairs]), mem.sb("slot", [P, pairs], I32)
        passed = mem.sb("passed", [1, n_tiles, EXPERTS])
        expert_f, expert = mem.sb("expert_f", [1, n_tiles]), mem.sb("expert", [1, n_tiles], I32)
        scratch = norm_scratch(mem, SEQ_PER_GROUP)

        h_ps = mem.ps("h_ps", [P, 2, 512])
        ht_ps = mem.ps("ht_ps", [P, 2, 512])
        xt_ps = mem.ps("xt_ps", [P, 512])
        y_ps = mem.ps("y_ps", [P, 2, 512])
        route_ps = mem.ps("route_ps", [P, 512])

        w1_in, w2_in = early.loaded if early.w1 is not None else mem.sem("w1_in"), mem.sem("w2_in")
        constants, chain = mem.sem("constants"), mem.sem("chain")
        x_ready, h_parked, h_back = mem.sem("x_ready"), mem.sem("h_parked"), mem.sem("h_back")
        xt_done, xt_copied = mem.sem("xt_done"), mem.sem("xt_copied")
        logits_done, exp_asked, exp_ready, onehot_ready, counted = (
            mem.sem(n) for n in ("logits_done", "exp_asked", "exp_ready", "onehot_ready", "counted"))
        routed, cleared, scattered = mem.sem("routed"), mem.sem("cleared"), mem.sem("scattered")
        if shared:
            mixed, h_shifted = mem.sem("mixed"), mem.sem("h_shifted")
            diag_ready, combined, sum_used = mem.sem("diag_ready"), mem.sem("combined"), mem.sem("sum_used")
            sh_done, sh_active, sh_out, sh_kept = (mem.sem(n) for n in ("sh_done", "sh_active", "sh_out", "sh_kept"))
        in_loaded = [mem.sem(f"in_loaded{b}") for b in range(2)]
        in_turned, turn_copied = mem.sem("in_turned"), mem.sem("turn_copied")
        hidden_done, hidden_kept = mem.sem("hidden_done"), mem.sem("hidden_kept")
        hidden_turned, active_ready = mem.sem("hidden_turned"), mem.sem("active_ready")
        y_done, y_kept = mem.sem("y_done"), mem.sem("y_kept")
        y_stored, y_out_free = mem.sem("y_stored"), mem.sem("y_out_free")
        if out is not None:
            h_ready, out_stored = mem.sem("h_ready"), mem.sem("out_stored")
        gathered = [mem.sem(f"gathered{g}") for g in range(GROUPS)]

        back = w1[:, :, :, :].rearrange("p k e n -> p (k e n)")[:, 0:TILES * choices * DIM]\
            .rearrange("p (t c d) -> p t c d", t=TILES, c=choices)

        diag = ff[:, :, :].rearrange("p a (n q) -> p a n q", q=P)

        def sum_ps(g, i):
            return (ht_ps if g % 2 else h_ps)[:, i // 2, (i % 2) * DIM:(i % 2 + 1) * DIM]

        def tile_rows(dram, j):
            return dram[bass.ds(j * P, P), :]

        with nc.Block() as block:
            @block.sync
            def _(sp):
                sp.dma_start(parked.rearrange("(t p) d -> p t d", p=P), h[:, :, :]).then_inc(h_parked, 16)
                if early.w1 is None:
                    for e in range(EXPERTS):
                        sp.dma_start(w1[:, :, e, :], w["w1"][:, :, e, :]).then_inc(w1_in, 16)
                for e in range(EXPERTS):
                    sp.dma_start(w2[:, :, e, :], w["w2"][:, :, e, :]).then_inc(w2_in, 16)
                sp.wait_ge(scattered, 16 * pairs)

                def load(j, b, first, last):
                    if not first:
                        sp.wait_ge(in_turned, j - 1 + b)
                    sp.dma_start(x_in[:, b, :], tile_rows(slots, j)).then_inc(in_loaded[b], 16)

                over_tiles(sp, n_tiles, load)
                if out is not None:
                    for g in range(GROUPS):
                        tiles = slice(g * SEQ_PER_GROUP, (g + 1) * SEQ_PER_GROUP)
                        sp.wait_ge(h_ready, g + 1)
                        sp.dma_start(out[tiles, :, :].rearrange("s p d -> p s d"), h[:, tiles, :]).then_inc(out_stored, 16)
                    sp.wait_ge(out_stored, 16 * GROUPS)

            @block.gpsimd
            def _(pool):
                pool.memset(zeros[:, :], 0.0).then_inc(constants, 1)
                pool.memset(lower[:, :], 1.0).then_inc(constants, 1)
                pool.memset(ones[:, :], 1.0).then_inc(constants, 1)
                pool.wait_ge(constants, 3)
                pool.affine_select(out=lower[:, :], in_=lower[:, :], compare_op=ALU.is_gt, fill=0.0, base=0,
                                   pattern=[[1, P]], channel_multiplier=-1).then_inc(constants, 1)
                pool.iota(expert_no[:, :], pattern=[[1, EXPERTS]], base=0, channel_multiplier=0,
                          allow_small_or_imprecise_dtypes=True).then_inc(constants, 1)
                pool.iota(tile_no[:, :, :], pattern=[[1, n_tiles], [0, EXPERTS]], base=0, channel_multiplier=0,
                          allow_small_or_imprecise_dtypes=True).then_inc(constants, 1)
                pool.dma_start(slots.rearrange("(a p) d -> p a d", p=P),
                               zeros[:, :].unsqueeze(1).to_broadcast([P, n_tiles, DIM])).then_inc(cleared, 16)
                pool.wait_ge(cleared, 16)
                pool.wait_ge(routed, 1)
                for t in range(TILES):
                    for k in range(choices):
                        pool.indirect_dma_start(
                            slots, bass.IndirectOffsetOnAxis(slot[:, k * TILES + t:k * TILES + t + 1].bitcast(U32), 0),
                            x[:, t, :], None, bounds_check=n_tiles * P - 1, oob_is_err=False).then_inc(scattered, 16)

                pool.wait_ge(scattered, 16 * pairs)
                pool.dma_start(x[:, :, :], parked.rearrange("(t p) d -> p t d", p=P)).then_inc(h_back, 16)
                pool.wait_ge(h_back, 16)
                if shared:
                    pool.tensor_tensor(x[:, :, :], x[:, :, :], ln_b[:, :].unsqueeze(1).to_broadcast([P, TILES, DIM]),
                                       ALU.add).then_inc(h_shifted, 1)
                pool.sem_inc(y_out_free, 2)

                def store(j, b, first, last):
                    pool.wait_ge(y_kept, j + 2)
                    pool.dma_start(tile_rows(results, j), y_out[:, b, :]).then_inc(y_stored, 16)
                    pool.wait_ge(y_stored, j * 16 + 16)
                    pool.sem_inc(y_out_free, 1)

                over_tiles(pool, n_tiles, store)
                for t in range(TILES):
                    for k in range(choices):
                        n = k * TILES + t
                        pool.indirect_dma_start(
                            back[:, t, k, :], None, results, bass.IndirectOffsetOnAxis(slot[:, n:n + 1].bitcast(U32), 0),
                            bounds_check=n_tiles * P - 1, oob_is_err=False).then_inc(gathered[t // SEQ_PER_GROUP], 16)

            @block.tensor
            def _(pe):
                pe.wait_ge(early.loaded, early.all)

                def turn_x(g):
                    pe.wait_ge(x_ready, g + 1)
                    for t in range(g * SEQ_PER_GROUP, (g + 1) * SEQ_PER_GROUP):
                        if t >= 2:
                            pe.wait_ge(xt_copied, t - 1)
                        for k in range(KC):
                            ins = pe.transpose(ht_ps[:, t % 2, k * P:(k + 1) * P], x[:, t, k * P:(k + 1) * P], ident[:, :])
                        ins.then_inc(xt_done, 1)

                def route(g):
                    pe.wait_ge(xt_copied, (g + 1) * SEQ_PER_GROUP)
                    for s in range(SEQ_PER_GROUP):
                        t = g * SEQ_PER_GROUP + s
                        for k in range(KC):
                            ins = pe.matmul(route_ps[:, t * EXPERTS:(t + 1) * EXPERTS], x_t[:, g, k, s * P:(s + 1) * P],
                                            router_w[:, k, :], start=(k == 0), stop=(k == KC - 1))
                    ins.then_inc(logits_done, 1)

                def count():
                    pe.wait_ge(onehot_ready, choices)
                    pe.wait_ge(constants, 6)
                    picks = onehot[:, :, :, :].rearrange("p c t e -> p (c t e)")
                    pe.matmul(ht_ps[:, 0, 0:pairs * EXPERTS], lower[:, :], picks, start=True, stop=True)
                    pe.matmul(ht_ps[:, 1, 0:pairs * EXPERTS], ones[:, :], picks, start=True, stop=True).then_inc(counted, 1)

                def shared_first(g):
                    for f in range(SC):
                        n = g * SC + f
                        if n >= 2:
                            pe.wait_ge(sh_active, n - 1)
                        for k in range(KC):
                            ins = pe.matmul(h_ps[:, n % 2, :], sw1[:, k, f * P:(f + 1) * P], x_t[:, g, k, :],
                                            start=(k == 0), stop=(k == KC - 1))
                        ins.then_inc(sh_done, 1)

                def shared_second(g):
                    pe.wait_ge(sh_active, (g + 1) * SC)
                    for n in range(g * SEQ_PER_GROUP, (g + 1) * SEQ_PER_GROUP):
                        if n >= 2:
                            pe.wait_ge(sh_kept, n - 1)
                        s = n % SEQ_PER_GROUP
                        for f in range(SC):
                            ins = pe.matmul(y_ps[:, n % 2, 0:DIM], shared_act[:, f, s * P:(s + 1) * P], sw2[:, f, :],
                                            start=(f == 0), stop=(f == SC - 1))
                        ins.then_inc(sh_out, 1)

                if shared:
                    turn_x(0)
                    route(0)
                    shared_first(0)
                    for g in range(1, GROUPS):
                        turn_x(g)
                        route(g)
                    shared_second(0)
                    count()
                    for g in range(1, GROUPS):
                        shared_first(g)
                        shared_second(g)
                    pe.wait_ge(sh_kept, TILES)
                else:
                    for g in range(GROUPS):
                        turn_x(g)
                        route(g)
                    count()
                pe.wait_ge(routed, 1)

                def turn_input(j, b):
                    pe.wait_ge(in_loaded[b], (j // 2 + 1) * 16 if isinstance(j, int) else j * 8 + (8 if b else 16))
                    pe.wait_ge(turn_copied, j) if not isinstance(j, int) or j > 0 else None
                    for k in range(KC):
                        ins = pe.transpose(xt_ps[:, k * P:(k + 1) * P], x_in[:, b, k * P:(k + 1) * P], ident[:, :])
                    ins.then_inc(in_turned, 1)

                def second(j, e):
                    pe.wait_ge(active_ready, j + 1)
                    for f in range(FC):
                        ins = pe.matmul(y_ps[:, 0, 0:DIM], active[:, f, :],
                                        w2[:, f, bass.ds(e, 1), :].rearrange("p a d -> p (a d)"),
                                        start=(f == 0), stop=(f == FC - 1))
                    ins.then_inc(y_done, 1)

                def expert_of(j):
                    return pe.value_load(expert[0:1, bass.ds(j, 1)], min_val=0, max_val=EXPERTS - 1)

                def tile(j, b, first, last):
                    e = expert_of(j)
                    e_before = None if first else expert_of(j - 1)
                    pe.wait_ge(turn_copied, j + 1)
                    if not first:
                        pe.wait_ge(hidden_kept, j)
                    for half in range(2):
                        for k in range(KC):
                            ins = pe.matmul(h_ps[:, half, :], x_in_t[:, b, k * P:(k + 1) * P],
                                            w1[:, k, bass.ds(e, 1), half * 512:(half + 1) * 512].rearrange("p a n -> p (a n)"),
                                            start=(k == 0), stop=(k == KC - 1))
                    ins.then_inc(hidden_done, 1)
                    if not last:
                        turn_input(j + 1, 1 - b)
                    if not first:
                        pe.wait_ge(y_kept, j)
                        second(j - 1, e_before)
                    pe.wait_ge(hidden_kept, j + 1)
                    for f in range(FC):
                        ins = pe.transpose(ht_ps[:, f // 4, (f % 4) * P:(f % 4 + 1) * P], hidden[:, f * P:(f + 1) * P],
                                           ident[:, :])
                    ins.then_inc(hidden_turned, 1)

                if early.w1 is None:
                    pe.wait_ge(w1_in, 16 * EXPERTS)
                pe.wait_ge(w2_in, 16 * EXPERTS)
                turn_input(0, 0)
                over_tiles(pe, n_tiles, tile)
                e = expert_of(n_tiles - 1)
                pe.wait_ge(y_kept, n_tiles)
                second(n_tiles - 1, e)
                if shared:
                    for g in range(GROUPS):
                        pe.wait_ge(diag_ready, g + 1)
                        pe.wait_ge(gathered[g], 16 * SEQ_PER_GROUP * choices)
                        if g >= 2:
                            pe.wait_ge(sum_used, g - 1)
                        for i in range(SEQ_PER_GROUP):
                            t = g * SEQ_PER_GROUP + i
                            pe.matmul(sum_ps(g, i), ident[:, :], h[:, t, :], start=True, stop=False)
                            for k in range(choices):
                                ins = pe.matmul(sum_ps(g, i), diag[:, g % 2, i * choices + k, :], back[:, t, k, :],
                                                start=False, stop=(k == choices - 1))
                        ins.then_inc(combined, 1)

            @block.scalar
            def _(act):
                def keep_x(g):
                    for s in range(SEQ_PER_GROUP):
                        t = g * SEQ_PER_GROUP + s
                        act.wait_ge(xt_done, t + 1)
                        act.activation(x_t[:, g, :, s * P:(s + 1) * P],
                                       ht_ps[:, t % 2, 0:DIM].rearrange("p (k n) -> p k n", k=KC), ACT.Copy).then_inc(xt_copied, 1)

                def exponent():
                    act.wait_ge(exp_asked, 1)
                    act.activation(top[:, :, :], top[:, :, :], ACT.Exp).then_inc(exp_ready, 1)

                def gelu_shared(g):
                    for f in range(SC):
                        n = g * SC + f
                        act.wait_ge(sh_done, n + 1)
                        if f == 0 and n:
                            act.wait_ge(sh_out, n)
                        act.activation(shared_act[:, f, :], h_ps[:, n % 2, :], ACT.Gelu, bias=sb1[:, f:f + 1],
                                       scale=sgate[:, f:f + 1]).then_inc(sh_active, 1)

                def keep_shared(g):
                    for t in range(g * SEQ_PER_GROUP, (g + 1) * SEQ_PER_GROUP):
                        act.wait_ge(sh_out, t + 1)
                        act.activation(h[:, t, :], y_ps[:, t % 2, 0:DIM], ACT.Copy, scale=mix[:, 0:1]).then_inc(sh_kept, 1)

                if shared:
                    act.wait_ge(early.loaded, early.all)
                    act.activation(mix[:, :], mix[:, :], ACT.Exp, scale=-1.0).then_inc(mixed, 1)
                act.wait_ge(h_parked, 16)
                keep_x(0)
                if shared:
                    act.wait_ge(mixed, 5)
                    gelu_shared(0)
                for g in range(1, GROUPS):
                    keep_x(g)
                if shared:
                    keep_shared(0)
                exponent()
                if shared:
                    for g in range(1, GROUPS):
                        gelu_shared(g)
                        keep_shared(g)

                def turn_copy(j, b):
                    act.wait_ge(in_turned, j + 1)
                    act.activation(x_in_t[:, b, :], xt_ps[:, 0:DIM], ACT.Copy).then_inc(turn_copied, 1)

                def tile(j, b, first, last):
                    if not last:
                        turn_copy(j + 1, 1 - b)
                    e = act.value_load(expert[0:1, bass.ds(j, 1)], min_val=0, max_val=EXPERTS - 1)
                    act.wait_ge(hidden_turned, j + 1)
                    for f in range(FC):
                        act_args = dict(bias=b1[:, f, bass.ds(e, 1)])
                        if shared:
                            act_args["scale"] = gate[:, f, bass.ds(e, 1)]
                        ins = act.activation(active[:, f, :], ht_ps[:, f // 4, (f % 4) * P:(f % 4 + 1) * P],
                                             ACT.Gelu if shared else ACT.Relu, **act_args)
                    ins.then_inc(active_ready, 1)

                act.wait_ge(routed, 1)
                turn_copy(0, 0)
                over_tiles(act, n_tiles, tile)
                if shared:
                    act.wait_ge(y_done, n_tiles)
                    for g in range(GROUPS):
                        if g >= 2:
                            act.wait_ge(combined, g - 1)
                        for n in range(SEQ_PER_GROUP * choices):
                            t, k = g * SEQ_PER_GROUP + n // choices, n % choices
                            ins = act.activation(diag[:, g % 2, n, :], ident[:, :], ACT.Copy, scale=weight[:, t, k:k + 1])
                        ins.then_inc(diag_ready, 1)

            @block.vector
            def _(dve):
                link = Chain(dve, chain)
                for g in range(GROUPS):
                    tiles = range(g * SEQ_PER_GROUP, (g + 1) * SEQ_PER_GROUP)
                    layer_norm(dve, link, [x[:, t, :] for t in tiles], [h[:, t, :] for t in tiles], *scratch)
                    dve.sem_inc(x_ready, 1)
                    if shared and g == 0:
                        dve.wait_ge(mixed, 1)
                        dve.tensor_scalar(mix[:, :], mix[:, :], 1.0, None, ALU.add).then_inc(mixed, 1)
                        dve.wait_ge(mixed, 2)
                        dve.reciprocal(mix[:, :], mix[:, :]).then_inc(mixed, 1)
                        dve.tensor_tensor(b1[:, :, :], b1[:, :, :], gate[:, :, :], ALU.mult).then_inc(mixed, 1)
                        dve.tensor_tensor(sb1[:, :], sb1[:, :], sgate[:, :], ALU.mult).then_inc(mixed, 1)
                dve.wait_ge(early.loaded, early.all)
                dve.wait_ge(logits_done, GROUPS)
                link(dve.tensor_tensor(logits[:, :, :], route_ps[:, 0:TILES * EXPERTS].rearrange("p (t e) -> p t e", e=EXPERTS),
                                       router_b[:, :].unsqueeze(1).to_broadcast([P, TILES, EXPERTS]), ALU.add))
                for t in range(TILES):
                    link(dve.max(top[:, t, :], logits[:, t, :]), wait=t == TILES - 1)
                for t in range(TILES):
                    link(dve.max_index(top_i[:, t, :], top[:, t, :], logits[:, t, :]), wait=t == TILES - 1)
                link(dve.tensor_copy(top_f[:, :, :], top_i[:, :, 0:choices]))
                link(dve.tensor_copy(total[:, :], top[:, :, 0]))
                dve.tensor_tensor(top[:, :, :], top[:, :, :], total[:, :].unsqueeze(2).to_broadcast([P, TILES, 8]),
                                  ALU.subtract).then_inc(exp_asked, 1)
                dve.wait_ge(constants, 6)
                for k in range(choices):
                    dve.tensor_tensor(onehot[:, k, :, :], top_f[:, :, k:k + 1].to_broadcast([P, TILES, EXPERTS]),
                                      expert_no[:, :].unsqueeze(1).to_broadcast([P, TILES, EXPERTS]),
                                      ALU.is_equal).then_inc(onehot_ready, 1)
                width = pairs * EXPERTS
                dve.wait_ge(counted, 1)
                link(dve.tensor_copy(before[:, :, :, :].rearrange("p c t e -> p (c t e)"), ht_ps[:, 0, 0:width]))
                link(dve.tensor_copy(counts[:, :, :].rearrange("p n e -> p (n e)"), ht_ps[:, 1, 0:width]))
                for e in range(EXPERTS):
                    link(dve.tensor_tensor_scan(running[:, :, e], ones[:, 0:pairs], counts[:, :, e], 0.0, ALU.mult, ALU.add),
                         wait=e == EXPERTS - 1)
                link(dve.tensor_scalar(tiles_i[:, :], running[:, pairs - 1, :], float(P - 1), None, ALU.add))
                link(dve.tensor_scalar(tiles_i[:, :], tiles_i[:, :], 7, None, ALU.logical_shift_right))
                link(dve.tensor_copy(tiles_of[:, :], tiles_i[:, :]))
                link(dve.tensor_tensor_scan(last_tile[:, :], ones[:, 0:EXPERTS], tiles_of[:, :], 0.0, ALU.mult, ALU.add))
                link(dve.tensor_tensor(base[:, :], last_tile[:, :], tiles_of[:, :], ALU.subtract))
                link(dve.tensor_scalar(base[:, :], base[:, :], float(P), None, ALU.mult))
                at = before[:, :, :, :].rearrange("p c t e -> p (c t) e")
                link(dve.tensor_tensor(at, at, running[:, :, :], ALU.add))
                link(dve.tensor_tensor(at, at, counts[:, :, :], ALU.subtract))
                link(dve.tensor_tensor(at, at, base[:, :].unsqueeze(1).to_broadcast([P, pairs, EXPERTS]), ALU.add))
                link(dve.tensor_tensor(at, at, onehot[:, :, :, :].rearrange("p c t e -> p (c t) e"), ALU.mult))
                link(dve.tensor_reduce(slot_f[:, :], at, AXX, ALU.add))
                link(dve.tensor_copy(slot[:, :], slot_f[:, :]))
                link(dve.tensor_tensor(passed[:, :, :], last_tile[0:1, :].unsqueeze(1).to_broadcast([1, n_tiles, EXPERTS]),
                                       tile_no[:, :, :], ALU.is_le))
                link(dve.tensor_reduce(expert_f[:, :], passed[:, :, :], AXX, ALU.add))
                link(dve.tensor_scalar(expert[:, :], expert_f[:, :], float(EXPERTS - 1), None, ALU.min))
                dve.sem_inc(routed, 1)
                dve.wait_ge(exp_ready, 1)
                link(dve.tensor_reduce(total[:, :], top[:, :, 0:2] if shared else top[:, :, :], AXX, ALU.add))
                link(dve.reciprocal(total[:, :], total[:, :]))
                link(dve.tensor_tensor(weight[:, :, :], top[:, :, 0:choices],
                                       total[:, :].unsqueeze(2).to_broadcast([P, TILES, choices]), ALU.mult))
                if shared:
                    link(dve.tensor_scalar(sb2[:, :], sb2[:, :], mix[:, 0:1], None, ALU.mult))
                    for t in range(TILES):
                        dve.wait_ge(sh_kept, t + 1)
                        link(dve.tensor_tensor(h[:, t, :], h[:, t, :], sb2[:, :], ALU.add), wait=t == TILES - 1)
                dve.sem_inc(y_kept, 1)

                def keep_y(j, b):
                    e = dve.value_load(expert[0:1, bass.ds(j, 1)], min_val=0, max_val=EXPERTS - 1)
                    dve.wait_ge(y_done, j + 1)
                    dve.wait_ge(y_out_free, j + 1)
                    dve.tensor_tensor(y_out[:, b, :], y_ps[:, 0, 0:DIM],
                                      b2[:, bass.ds(e, 1), :].rearrange("p a d -> p (a d)"), ALU.add).then_inc(y_kept, 1)

                def tile(j, b, first, last):
                    dve.wait_ge(hidden_done, j + 1)
                    if not first:
                        dve.wait_ge(hidden_turned, j)
                    dve.tensor_copy(hidden, h_ps[:, :, :].rearrange("p a n -> p (a n)")).then_inc(hidden_kept, 1)
                    if not first:
                        keep_y(j - 1, 1 - b)

                over_tiles(dve, n_tiles, tile)
                keep_y(n_tiles - 1, (n_tiles - 1) % 2)

                dve.wait_ge(h_back, 16)
                if shared:
                    dve.wait_ge(h_shifted, 1)
                for g in range(GROUPS):
                    tiles = range(g * SEQ_PER_GROUP, (g + 1) * SEQ_PER_GROUP)

                    def each(instruction):
                        for i, t in enumerate(tiles):
                            link(instruction(i, t), wait=t == tiles[-1])

                    if shared:
                        dve.wait_ge(combined, g + 1)
                        mean, rstd = norm_statistics(dve, link, [sum_ps(g, i) for i in range(SEQ_PER_GROUP)], *scratch)
                        each(lambda i, t: dve.scalar_tensor_tensor(h[:, t, :], sum_ps(g, i), mean[:, i:i + 1], ln_g[:, :],
                                                                   ALU.subtract, ALU.mult))
                        dve.sem_inc(sum_used, 1)
                        each(lambda i, t: dve.scalar_tensor_tensor(h[:, t, :], h[:, t, :], rstd[:, i:i + 1], x[:, t, :],
                                                                   ALU.mult, ALU.add))
                    else:
                        dve.wait_ge(gathered[g], 16 * SEQ_PER_GROUP * choices)
                        each(lambda i, t: dve.scalar_tensor_tensor(h[:, t, :], back[:, t, 0, :], weight[:, t, 0:1], x[:, t, :],
                                                                   ALU.mult, ALU.add))
                    if out is not None:
                        dve.sem_inc(h_ready, 1)


def build(nc, x, out, stages=9):
    with ExitStack() as ctx:
        h = ctx.enter_context(nc.sbuf_tensor("h", [P, TILES, DIM], F32))
        ident = make_constants(nc, ctx)
        bc_dram = nc.dram_tensor("bc_rows", (GROUPS, 2 * STATE, GT), F32, kind="Internal").ap()
        parked = nc.dram_tensor("h_parked", (TOKENS, DIM), F32, kind="Internal").ap()

        def expert_rows(name, choices):
            return nc.dram_tensor(name, (most_tiles(choices) * P, DIM), F32, kind="Internal").ap()

        def part(prefix):
            return {k[len(prefix):]: v for k, v in x.items() if k.startswith(prefix)}

        with ExitStack() as layer:
            early = EarlyWeights(nc, layer, part("moe0_"), True, False, "moe0")
            mamba(nc, h, ident, part("mamba_"), bc_dram, x["x"], [x["emb_head"], x["emb_tail_0"], x["emb_tail_1"]],
                  x["emb_proj"], early)
            if stages >= 3:
                moe(nc, h, ident, part("moe0_"), early, 2, expert_rows("slots0", 2), expert_rows("results0", 2), parked, "moe0")
        with ExitStack() as layer:
            if stages >= 4:
                early = EarlyWeights(nc, layer, part("moe1_"), False, True, "moe1")
                attention(nc, h, ident, part("att_"), early)
            if stages >= 5:
                moe(nc, h, ident, part("moe1_"), early, 1, expert_rows("slots1", 1), expert_rows("results1", 1), parked, "moe1",
                    out)
        if stages < 5:
            stored = ctx.enter_context(nc.semaphore("h_stored"))
            with nc.Block() as block:
                @block.sync
                def _(sp):
                    sp.dma_start(out.rearrange("s p d -> p s d"), h[:, :, :]).then_inc(stored, 16)
                    sp.wait_ge(stored, 16)


def rope_tables(rows, scale):
    d = np.arange(rows) % HEAD_DIM
    inv_freq = (np.float32(1) / np.float32(10000) ** ((d // 2 * 2).astype(np.float32) / np.float32(HEAD_DIM))).astype(np.float32)
    angle = inv_freq[:, None] * np.arange(P, dtype=np.float32)
    sign = np.where(d % 2 == 0, np.float32(-1), np.float32(1))[:, None]
    return (np.stack([np.cos(angle), sign * np.sin(angle)], 1) * np.float32(scale)).astype(np.float32)


def host_layout(inputs):
    a = {k: np.asarray(v) for k, v in inputs.items()}

    def rows(m):
        return m.reshape(m.shape[0] // P, P, *m.shape[1:]).swapaxes(0, 1)

    t0, m0, f0, t1, f1 = "L0_tok_", "L0_attn_", "L0_ffn_", "L1_attn_", "L1_ffn_"
    swapped = np.arange(DIM) ^ 1
    kv = a[t1 + "Wkvb"].reshape(-1, KV_HEADS * HEAD_DIM, 2)
    by_r = np.arange(DIM).reshape(KV_HEADS, HEADS // KV_HEADS, HEAD_DIM).swapaxes(0, 1).reshape(-1)
    kv_width = KV_HEADS * HEAD_DIM
    wk = np.stack([kv[:, :, 0], kv[:, swapped[:kv_width], 0]], 1)
    return {
        "x": a["x"].T,
        "emb_head": a[t0 + "head_weight"].T,
        "emb_tail_0": a[t0 + "tail_weight_0"].T,
        "emb_tail_1": a[t0 + "tail_weight_1"].T,
        "emb_proj": np.concatenate([a[t0 + "head_weight_proj"].T, a[t0 + "tail_weight_proj_0"].T,
                                    a[t0 + "tail_weight_proj_1"].T]),
        "mamba_ln_gamma": rows(a[m0 + "ln_gamma"]),
        "mamba_ln_beta": rows(a[m0 + "ln_beta"]),
        "mamba_W_in": rows(a[m0 + "W_in"].T),
        "mamba_conv_w": rows(a[m0 + "conv_w"][:, 0, :]),
        "mamba_conv_b": rows(a[m0 + "conv_b"]),
        "mamba_W_xproj": rows(a[m0 + "W_xproj"].T),
        "mamba_W_dt": a[m0 + "W_dt"].T,
        "mamba_b_dt": rows(a[m0 + "b_dt"]),
        "mamba_A_log": rows(a[m0 + "A_log"]),
        "mamba_D_param": rows(a[m0 + "D_param"]),
        "mamba_W_out": rows(a[m0 + "W_out"].T),
        "moe0_router_w": rows(a[f0 + "router_w"]),
        "moe0_router_b": a[f0 + "router_b"],
        "moe0_w1": rows(a[f0 + "w1"].swapaxes(0, 1)),
        "moe0_b1": rows(a[f0 + "b1"].T),
        "moe0_gate": rows(a[f0 + "gate"].T),
        "moe0_w2": rows(a[f0 + "w2"].swapaxes(0, 1)),
        "moe0_b2": a[f0 + "b2"].reshape(-1),
        "moe0_sw1": rows(a[f0 + "sw1"]),
        "moe0_sb1": rows(a[f0 + "sb1"]),
        "moe0_sgate": rows(a[f0 + "sgate"]),
        "moe0_sw2": rows(a[f0 + "sw2"]),
        "moe0_sb2": a[f0 + "sb2"],
        "moe0_shared_weight": a[f0 + "shared_weight"].reshape(1),
        "moe0_ln_g": a[f0 + "ln_g"],
        "moe0_ln_b": a[f0 + "ln_b"],
        "att_Wqa": rows(a[t1 + "Wqa"]),
        "att_Wkva": rows(a[t1 + "Wkva"]),
        "att_Wqb": np.stack([a[t1 + "Wqb"][:, by_r], a[t1 + "Wqb"][:, swapped[by_r]]], 1),
        "att_Wk": np.concatenate([wk, wk], 2),
        "att_Wv": kv[:, :, 1],
        "att_Wout": rows(a[t1 + "Wout"]),
        "att_bout": a[t1 + "bout"],
        "att_rope_q": rope_tables(P, float(HEAD_DIM) ** -0.5),
        "att_rope_k": rope_tables(P, 1.0),
        "att_key_head": (np.arange(P)[:, None] % kv_width // HEAD_DIM == np.arange(KV_HEADS)).astype(np.float32),
        "moe1_router_w": rows(a[f1 + "w_gate"]),
        "moe1_router_b": a[f1 + "b_gate"],
        "moe1_w1": rows(a[f1 + "W1"].swapaxes(0, 1)),
        "moe1_b1": rows(a[f1 + "b1"].T),
        "moe1_w2": rows(a[f1 + "W2"].swapaxes(0, 1)),
        "moe1_b2": a[f1 + "b2"].reshape(-1),
    }


def program(nc, arrays, stages=9):
    args = {}
    for name, a in arrays.items():
        args[name[3:]] = nc.dram_tensor(name, a.shape, mybir.dt.from_np(a.dtype), kind="ExternalInput").ap()
    out = nc.dram_tensor("out", (TILES, P, DIM), F32, kind="ExternalOutput").ap()
    build(nc, args, out, stages)


def kernel(**inputs):
    import concourse.bacc as bacc
    from concourse.bass_utils import run_bass_kernel_spmd

    arrays = {"in_" + k: np.ascontiguousarray(v) for k, v in host_layout(inputs).items()}
    nc = bacc.Bacc("TRN2", target_bir_lowering=False, num_devices=1)
    program(nc, arrays)
    result = run_bass_kernel_spmd(nc, [arrays], core_ids=[0])
    return result.results[0]["out"]
```
